# Optimizing a Trainium2 kernel written in Bass

```python
import numpy as np
import jax
import jax.numpy as jnp

def _softmax(x, axis=-1):
    return jax.nn.softmax(x, axis=axis)

def _gelu(x):
    return jax.nn.gelu(x, approximate=True)

def _silu(x):
    return jax.nn.silu(x)

def _sigmoid(x):
    return jax.nn.sigmoid(x)

def _layernorm(x, axis=-1, eps=1e-05):
    m = jnp.mean(x, axis=axis, keepdims=True)
    v = jnp.var(x, axis=axis, keepdims=True)
    return (x - m) / jnp.sqrt(v + eps)

def _scatter_add(tgt, idx, src, axis=0):
    return tgt.at[idx].add(src)

def _segment_sum(src, seg, n):
    return jax.ops.segment_sum(src, seg, n)
kernel_name = 'mk_early_fusion_d1_tok_img768_r4_f5ef48'

def setup_inputs(seed: int=0):
    np.random.seed(seed)
    _w = jnp.asarray

    def _rec_inputs():
        import jax
        import jax.numpy as jnp
        _rk = jax.random.key(seed)
        x = -0.000356955 + 1 * jax.random.normal(jax.random.fold_in(_rk, 1), (16, 3, 224, 224), jnp.float32)
        txt = 0.323433 + 0.839583 * jax.random.normal(jax.random.fold_in(_rk, 2), (16, 128, 192), jnp.float32)
        return (x, txt)
    x, txt = _rec_inputs()

    def _L0_tok_setup():
        import jax, jax.numpy as jnp
        import numpy as np
        C, H, W_IMG = (3, 224, 224)
        NP = 14
        PS = H // NP
        D_IN = C * PS * PS
        D = 192
        SEQ = NP * NP + 1
        B = 128

        def _sinusoidal_pos_embed(seq_len, d):
            i = np.arange(seq_len, dtype=np.float64)[:, None]
            j = np.arange(d, dtype=np.float64)[None, :]
            angle = i / np.power(10000.0, (j - j % 2) / d)
            pe = np.where(j % 2 == 0, np.sin(angle), np.cos(angle))
            return jnp.asarray(pe, dtype=jnp.float32)
        key = jax.random.key(seed)
        kx, kw, kc = jax.random.split(key, 3)
        x = jax.random.normal(kx, (B, C, H, W_IMG), dtype=jnp.float32)
        W = jax.random.normal(kw, (D, D_IN), dtype=jnp.float32) * 0.02
        b = jnp.zeros((D,), dtype=jnp.float32)
        class_token = jax.random.uniform(kc, (1, D), dtype=jnp.float32)
        pos_embed = _sinusoidal_pos_embed(SEQ, D)
        return {'x': x, 'W': W, 'b': b, 'class_token': class_token, 'pos_embed': pos_embed}
    _L0_tok_all = _L0_tok_setup()
    _L0_tok_in = {k: v for k, v in _L0_tok_all.items() if k in ('W', 'b', 'class_token', 'pos_embed')}
    del _L0_tok_all

    def _L0_attn_setup():
        import jax, jax.numpy as jnp
        import numpy as np
        EMBED_DIM = 192
        SEQ_LEN = 256
        BATCH = 32
        ALPHA = 0.99

        def _decay_mask(sl: int, alpha: float) -> jnp.ndarray:
            i = jnp.arange(sl, dtype=jnp.float32)
            diff = i[:, None] - i[None, :]
            return jnp.where(diff >= 0, jnp.float32(alpha) ** diff, 0.0)
        key = jax.random.key(seed)
        k1, k2 = jax.random.split(key)
        x = jax.random.normal(k1, (BATCH, SEQ_LEN, EMBED_DIM), dtype=jnp.float32)
        W_qkv = jax.random.normal(k2, (EMBED_DIM, 3 * EMBED_DIM), dtype=jnp.float32) * EMBED_DIM ** (-0.5)
        b_qkv = jnp.zeros((3 * EMBED_DIM,), dtype=jnp.float32)
        return {'x': x, 'W_qkv': W_qkv, 'b_qkv': b_qkv}
    _L0_attn_all = _L0_attn_setup()
    _L0_attn_in = {k: v for k, v in _L0_attn_all.items() if k in ('W_qkv', 'b_qkv')}
    del _L0_attn_all

    def _L0_ffn_setup():
        import jax, jax.numpy as jnp
        import numpy as np
        E = 128
        I = 464
        IS = 928
        K = 6
        G = 1
        TG = 1
        SCALE = 2.5
        CAP = 192

        def moe_forward(hidden_states, Wg, e_bias, W_gate_up, W_down, Wsg, Wsu, Wsd):
            B, S, H = hidden_states.shape
            x = hidden_states.reshape(-1, H)
            T = x.shape[0]
            logits = x.astype(jnp.float32) @ Wg.T
            sig = jax.nn.sigmoid(logits)
            choice = sig + e_bias[None, :]
            grp = choice.reshape(T, G, E // G)
            group_scores = jax.lax.top_k(grp, 2)[0].sum(-1)
            gidx = jax.lax.top_k(group_scores, TG)[1]
            gmask = jnp.zeros((T, G), jnp.float32).at[jnp.arange(T)[:, None], gidx].set(1.0)
            smask = jnp.repeat(gmask, E // G, axis=1)
            scores_for_choice = jnp.where(smask > 0, choice, 0.0)
            topk_idx = jax.lax.top_k(scores_for_choice, K)[1]
            topk_w = jnp.take_along_axis(sig, topk_idx, axis=1)
            topk_w = topk_w / (topk_w.sum(-1, keepdims=True) + 1e-20)
            topk_w = topk_w * SCALE
            P = T * K
            flat_e = topk_idx.reshape(-1)
            order = jnp.argsort(flat_e)
            se = flat_e[order]
            counts = jax.ops.segment_sum(jnp.ones(P, jnp.int32), flat_e, num_segments=E)
            starts = jnp.cumsum(counts) - counts
            pos = jnp.arange(P) - starts[se]
            buf_idx = jnp.where(pos < CAP, se * CAP + pos, E * CAP)
            tok_of_pair = (order // K).astype(jnp.int32)
            w_of_pair = topk_w.reshape(-1)[order]
            token_buf = jnp.zeros((E * CAP,), jnp.int32).at[buf_idx].set(tok_of_pair, mode='drop')
            w_buf = jnp.zeros((E * CAP,), x.dtype).at[buf_idx].set(w_of_pair.astype(x.dtype), mode='drop')
            xb = x[token_buf].reshape(E, CAP, H)
            gu = jnp.einsum('ech,ehf->ecf', xb, W_gate_up)
            g, u = jnp.split(gu, 2, axis=-1)
            inter = jax.nn.silu(g) * u
            yb = jnp.einsum('eci,eih->ech', inter, W_down)
            yb = yb * w_buf.reshape(E, CAP, 1)
            routed = jnp.zeros((T, H), x.dtype).at[token_buf].add(yb.reshape(E * CAP, H))
            shared = jax.nn.silu(x @ Wsg) * (x @ Wsu) @ Wsd
            return (routed + shared).reshape(B, S, H)
        key = jax.random.key(seed)
        ks = jax.random.split(key, 8)
        B, S, H = (1, 512, 192)
        sc = 0.02
        return {'hidden_states': jax.random.normal(ks[0], (B, S, H), jnp.float32), 'Wg': jax.random.normal(ks[1], (E, H), jnp.float32) * sc, 'e_bias': jnp.zeros((E,), jnp.float32), 'W_gate_up': jax.random.normal(ks[2], (E, H, 2 * I), jnp.float32) * sc, 'W_down': jax.random.normal(ks[3], (E, I, H), jnp.float32) * sc, 'Wsg': jax.random.normal(ks[4], (H, IS), jnp.float32) * sc, 'Wsu': jax.random.normal(ks[5], (H, IS), jnp.float32) * sc, 'Wsd': jax.random.normal(ks[6], (IS, H), jnp.float32) * sc}
    _L0_ffn_all = _L0_ffn_setup()
    _L0_ffn_in = {k: v for k, v in _L0_ffn_all.items() if k in ('Wg', 'e_bias', 'W_gate_up', 'W_down', 'Wsg', 'Wsu', 'Wsd')}
    del _L0_ffn_all
    return {'x': x, 'txt': txt, 'L0_tok_W': _L0_tok_in['W'], 'L0_tok_b': _L0_tok_in['b'], 'L0_tok_class_token': _L0_tok_in['class_token'], 'L0_tok_pos_embed': _L0_tok_in['pos_embed'], 'L0_attn_W_qkv': _L0_attn_in['W_qkv'], 'L0_attn_b_qkv': _L0_attn_in['b_qkv'], 'L0_ffn_Wg': _L0_ffn_in['Wg'], 'L0_ffn_e_bias': _L0_ffn_in['e_bias'], 'L0_ffn_W_gate_up': _L0_ffn_in['W_gate_up'], 'L0_ffn_W_down': _L0_ffn_in['W_down'], 'L0_ffn_Wsg': _L0_ffn_in['Wsg'], 'L0_ffn_Wsu': _L0_ffn_in['Wsu'], 'L0_ffn_Wsd': _L0_ffn_in['Wsd']}

def reference(x, txt, L0_tok_W, L0_tok_b, L0_tok_class_token, L0_tok_pos_embed, L0_attn_W_qkv, L0_attn_b_qkv, L0_ffn_Wg, L0_ffn_e_bias, L0_ffn_W_gate_up, L0_ffn_W_down, L0_ffn_Wsg, L0_ffn_Wsu, L0_ffn_Wsd):
    import jax
    import jax.numpy as jnp

    def _L0_tok_ref(x, W, b, class_token, pos_embed):
        import jax, jax.numpy as jnp
        import numpy as np
        C, H, W_IMG = (3, 224, 224)
        NP = 14
        PS = H // NP
        D_IN = C * PS * PS
        D = 192
        SEQ = NP * NP + 1
        B = 128

        def _sinusoidal_pos_embed(seq_len, d):
            i = np.arange(seq_len, dtype=np.float64)[:, None]
            j = np.arange(d, dtype=np.float64)[None, :]
            angle = i / np.power(10000.0, (j - j % 2) / d)
            pe = np.where(j % 2 == 0, np.sin(angle), np.cos(angle))
            return jnp.asarray(pe, dtype=jnp.float32)
        n = x.shape[0]
        p = x.reshape(n, C, NP, PS, NP, PS)
        p = p.transpose(0, 2, 4, 1, 3, 5).reshape(n, NP * NP, D_IN)
        tokens = jnp.einsum('npd,hd->nph', p, W) + b
        cls = jnp.broadcast_to(class_token[None], (n, 1, D))
        tokens = jnp.concatenate([cls, tokens], axis=1)
        return tokens + pos_embed[None]

    def _L0_attn_ref(x, W_qkv, b_qkv):
        import jax, jax.numpy as jnp
        import numpy as np
        EMBED_DIM = 192
        SEQ_LEN = 256
        BATCH = 32
        ALPHA = 0.99

        def _decay_mask(sl: int, alpha: float) -> jnp.ndarray:
            i = jnp.arange(sl, dtype=jnp.float32)
            diff = i[:, None] - i[None, :]
            return jnp.where(diff >= 0, jnp.float32(alpha) ** diff, 0.0)
        bs, sl, d = x.shape
        qkv = x @ W_qkv + b_qkv
        q, k, v = jnp.split(qkv, 3, axis=-1)
        M = _decay_mask(sl, ALPHA)
        dim_sqrt = jnp.sqrt(jnp.float32(d))
        scores = jnp.einsum('bsd,btd->bst', q, k) / dim_sqrt * M
        return jnp.einsum('bst,btd->bsd', scores, v)

    def _L0_ffn_ref(hidden_states, Wg, e_bias, W_gate_up, W_down, Wsg, Wsu, Wsd):
        import jax, jax.numpy as jnp
        import numpy as np
        E = 128
        I = 464
        IS = 928
        K = 6
        G = 1
        TG = 1
        SCALE = 2.5
        CAP = 192

        def moe_forward(hidden_states, Wg, e_bias, W_gate_up, W_down, Wsg, Wsu, Wsd):
            B, S, H = hidden_states.shape
            x = hidden_states.reshape(-1, H)
            T = x.shape[0]
            logits = x.astype(jnp.float32) @ Wg.T
            sig = jax.nn.sigmoid(logits)
            choice = sig + e_bias[None, :]
            grp = choice.reshape(T, G, E // G)
            group_scores = jax.lax.top_k(grp, 2)[0].sum(-1)
            gidx = jax.lax.top_k(group_scores, TG)[1]
            gmask = jnp.zeros((T, G), jnp.float32).at[jnp.arange(T)[:, None], gidx].set(1.0)
            smask = jnp.repeat(gmask, E // G, axis=1)
            scores_for_choice = jnp.where(smask > 0, choice, 0.0)
            topk_idx = jax.lax.top_k(scores_for_choice, K)[1]
            topk_w = jnp.take_along_axis(sig, topk_idx, axis=1)
            topk_w = topk_w / (topk_w.sum(-1, keepdims=True) + 1e-20)
            topk_w = topk_w * SCALE
            P = T * K
            flat_e = topk_idx.reshape(-1)
            order = jnp.argsort(flat_e)
            se = flat_e[order]
            counts = jax.ops.segment_sum(jnp.ones(P, jnp.int32), flat_e, num_segments=E)
            starts = jnp.cumsum(counts) - counts
            pos = jnp.arange(P) - starts[se]
            buf_idx = jnp.where(pos < CAP, se * CAP + pos, E * CAP)
            tok_of_pair = (order // K).astype(jnp.int32)
            w_of_pair = topk_w.reshape(-1)[order]
            token_buf = jnp.zeros((E * CAP,), jnp.int32).at[buf_idx].set(tok_of_pair, mode='drop')
            w_buf = jnp.zeros((E * CAP,), x.dtype).at[buf_idx].set(w_of_pair.astype(x.dtype), mode='drop')
            xb = x[token_buf].reshape(E, CAP, H)
            gu = jnp.einsum('ech,ehf->ecf', xb, W_gate_up)
            g, u = jnp.split(gu, 2, axis=-1)
            inter = jax.nn.silu(g) * u
            yb = jnp.einsum('eci,eih->ech', inter, W_down)
            yb = yb * w_buf.reshape(E, CAP, 1)
            routed = jnp.zeros((T, H), x.dtype).at[token_buf].add(yb.reshape(E * CAP, H))
            shared = jax.nn.silu(x @ Wsg) * (x @ Wsu) @ Wsd
            return (routed + shared).reshape(B, S, H)
        return moe_forward(hidden_states, Wg, e_bias, W_gate_up, W_down, Wsg, Wsu, Wsd)
    h = _L0_tok_ref(x, L0_tok_W, L0_tok_b, L0_tok_class_token, L0_tok_pos_embed)
    h = jnp.concatenate([h, txt], axis=1)
    h = h + _L0_attn_ref(_layernorm(h, axis=-1), L0_attn_W_qkv, L0_attn_b_qkv)
    h = h + _L0_ffn_ref(_layernorm(h, axis=-1), L0_ffn_Wg, L0_ffn_e_bias, L0_ffn_W_gate_up, L0_ffn_W_down, L0_ffn_Wsg, L0_ffn_Wsu, L0_ffn_Wsd)
    return h

_drawn_inputs = setup_inputs


def setup_inputs(seed=0):
    import zlib

    import numpy as np

    out = dict(_drawn_inputs(seed))
    spreads = {'L0_tok_b': (0.0, 0.1), 'L0_attn_b_qkv': (0.0, 0.1), 'L0_ffn_e_bias': (0.0, 0.8)}
    factors = {'L0_tok_class_token': 3.029,
     'L0_ffn_Wg': 8.0,
     'L0_ffn_W_gate_up': 8.0,
     'L0_ffn_W_down': 8.0,
     'L0_ffn_Wsg': 8.0,
     'L0_ffn_Wsu': 8.0,
     'L0_ffn_Wsd': 8.0}
    for name, (base, spread) in spreads.items():
        noise = np.random.default_rng([zlib.crc32(name.encode()), seed]).standard_normal(out[name].shape)
        drawn = base * np.exp(spread * noise) if base else spread * noise
        out[name] = jnp.asarray(drawn.astype(out[name].dtype))
    for name, factor in factors.items():
        out[name] = (out[name] * factor).astype(out[name].dtype)
    return out
```

```python
from contextlib import ExitStack

import concourse.bass as bass
from concourse import mybir

F32 = mybir.dt.float32
F32R = mybir.dt.float32r
BF16 = mybir.dt.bfloat16
I32 = mybir.dt.int32
ALU = mybir.AluOpType
ACT = mybir.ActivationFunctionType

B = 16
NPATCH = 196
DIN = 768
KC = DIN // 128
D = 192
DA = 128
DB = D - DA
TXT = 128
IMG = NPATCH + 1
S = IMG + TXT
SP = S + 1
T = B * S
TL = [128, 128, S - 256]
E = 128
K = 6
I = 464
IS = 928
CAP = 192
CH = CAP // 2
F = 116
EM = I // F
SM = IS // F
YW = D + E
LIST = E + 8
CHUNK = 512
NCHUNK = T // CHUNK
TAIL = T - NCHUNK * CHUNK
SOFF = [0, S, S + (S - 128)]
SCOLS = S + (S - 128) + (S - 256)
EPS = 1e-5
SCALE = 2.5
LOW = -3.0e38
ROUTED = -3.3e38


def wait(eng, sem, value):
    if isinstance(value, int) and value <= 0:
        return
    eng.wait_ge(sem, value)


def wait_apart(eng, passed, *waits):
    for sem, v in waits:
        if not isinstance(v, int) or v > 0:
            eng.wait_ge(sem, v)
            eng.sem_inc(passed, 1)


def build(nc, xp, txt, wtok, btok, cls, pos, wqkv, bqk, bv, wg, ebias, wgu, wdn, wsg, wsu, wsd,
          c_mask, c_cum, c_up, c_ident, c_slot, c_iota, c_ecol, out):
    yw = nc.dram_tensor("yw_rows", (T + CAP, YW), F32, kind="Internal").ap()
    acc = nc.dram_tensor("acc_rows", (T + CAP, D), F32, kind="Internal").ap()
    crow = nc.dram_tensor("count_rows", (B * E, S), F32, kind="Internal").ap()

    with ExitStack() as top:
        def keep(name, shape, dt=F32):
            return top.enter_context(nc.sbuf_tensor(name, shape, dt))

        psum = [top.enter_context(nc.psum_tensor(f"bank{i}", [128, 512], F32)) for i in range(8)]

        all_hiA = keep("all_hiA", [128, T], F32R)
        all_loA = keep("all_loA", [128, T], F32R)
        all_B = keep("all_B", [128, T], F32R)
        ident = keep("ident", [128, 128])
        ones = keep("ones", [128, 128])
        slot = keep("slot", [CH, 2])
        iota = keep("iota", [128, E])
        ecol = keep("ecol", [128, 1])
        up_strict = keep("up_strict", [128, 128])
        images_full = keep("images_full", [CH, 2, E])
        countT = keep("countT", [E, S])

        block_a(nc, psum, all_hiA, all_loA, all_B, ident, ones, slot, iota, ecol, up_strict, images_full, countT,
                yw, acc, crow, xp, txt, wtok, btok, cls, pos, wqkv, bqk, bv, wg, ebias,
                c_mask, c_cum, c_up, c_ident, c_slot, c_iota, c_ecol)
        block_b(nc, psum, ident, ones, slot, iota, ecol, up_strict, images_full, countT, yw, acc, crow, wgu, wdn)
        block_c(nc, psum, all_hiA, all_loA, all_B, acc, wsg, wsu, wsd, out)


def block_a(nc, psum, all_hiA, all_loA, all_B, ident, ones, slot, iota, ecol, up_strict, images_full, countT,
            yw, acc, crow, xp, txt, wtok, btok, cls, pos, wqkv, bqk, bv, wg, ebias,
            c_mask, c_cum, c_up, c_ident, c_slot, c_iota, c_ecol):
    with ExitStack() as ctx:
        def sb(name, shape, dt=F32):
            return ctx.enter_context(nc.sbuf_tensor(name, shape, dt))

        def sem(name):
            return ctx.enter_context(nc.semaphore(name))

        patches = sb("patches", [128, KC, 256])
        w_tok = sb("w_tok", [128, KC, D])
        addend = sb("addend", [128, 2, D])
        pos_sb = sb("pos_sb", [128, 2, D])
        txt2 = sb("txt2", [128, D])
        raw_qkv = sb("raw_qkv", [128, 2, 3 * D])
        qkv_hi = sb("qkv_hi", [128, 2, 3 * D], F32R)
        qkv_lo = sb("qkv_lo", [128, 2, 3 * D], F32R)
        raw_g = sb("raw_g", [128, 2, E])
        g_hi = sb("g_hi", [128, 2, E], F32R)
        g_lo = sb("g_lo", [128, 2, E], F32R)
        b_qk = sb("b_qk", [96, 4])
        b_v = sb("b_v", [128, D])
        e_bias = sb("e_bias", [128, E])
        mask = sb("mask", [128, SCOLS])
        cum32 = sb("cum32", [128, 3, S])
        cum = sb("cum", [128, 3, S], BF16)
        ones_b = sb("ones_b", [128, S], BF16)
        zero = sb("zero", [CH, 2, YW])
        half_neg = sb("half_neg", [128, 3])
        h0 = sb("h0", [128, 3, D])
        h1 = sb("h1", [128, 3, D])
        q_k = sb("q_k", [96, 4, S])
        v_sb = sb("v_sb", [128, 3, D])
        scores = sb("scores", [128, SCOLS])
        sig = sb("sig", [128, 3, E])
        choice = sb("choice", [128, 3, E + 2])
        best = sb("best", [128, 3, 8])
        left = sb("left", [128, 3, E + 2])
        chosen = sb("chosen", [128, 3, E], BF16)
        w_raw = sb("w_raw", [128, 3, E])
        w_sum = sb("w_sum", [128, 3])
        w_sum2 = sb("w_sum2", [128, 3])
        w_inv = sb("w_inv", [128, 3])
        chosen_all = sb("chosen_all", [128, E], BF16)
        y1 = sb("y1", [128, 3, D])
        y2 = sb("y2", [128, 3, YW])
        norm = []
        for i, y in ((1, y1), (2, y2)):
            norm.append(dict(
                y=y, stats=sb(f"stats{i}", [128, 3, 6]), mv=sb(f"mv{i}", [128, 3, 2]), ve=sb(f"ve{i}", [128, 3]),
                rstd=sb(f"rstd{i}", [128, 3]), hiA=sb(f"y{i}_hiA", [128, SP], F32R),
                loA=sb(f"y{i}_loA", [128, SP], F32R), st=sb(f"y{i}_B", [128, SP], F32R),
                s_stats=sem(f"stats{i}_done"), s_mv=sem(f"mv{i}_ready"), s_ve=sem(f"ve{i}_ready"),
                s_rstd=sem(f"rstd{i}_ready"), s_y=sem(f"y{i}_ready"), s_T=sem(f"y{i}T_in_psum"),
                s_hi=sem(f"y{i}T_hi_ready"), s_lo=sem(f"y{i}T_split"), bankA=psum[5 if i == 1 else 3],
                bankB=psum[6 if i == 1 else 4]))
        n1, n2 = norm
        tok_ps, pv_ps, pv2_ps, lg_ps, ct_ps = psum[0], psum[1], psum[2], psum[3], psum[4]
        qk_ps = [psum[7], psum[5], psum[6], psum[0]]
        sc_ps = [psum[7], psum[5], psum[6]]

        passed = sem("passed_a")
        const_in = sem("const_in")
        base_in = sem("base_in")
        base_set = sem("base_set")
        set_up = sem("set_up")
        set_up_act = sem("set_up_act")
        pool_set = sem("pool_set")
        lo_set = sem("lo_set")
        x_in = sem("x_in")
        t1_in = sem("t1_in")
        t2_in = sem("t2_in")
        tok_mm = sem("tok_mm")
        h0_ready = sem("h0_ready")
        h0_txt = sem("h0_txt")
        qk_mm = sem("qk_mm")
        v_mm = sem("v_mm")
        qk_ready = sem("qk_ready")
        v_ready = sem("v_ready")
        sc_mm = sem("sc_mm")
        sc_ready = sem("sc_ready")
        pv_mm = sem("pv_mm")
        h1_ready = sem("h1_ready")
        lg_mm = sem("lg_mm")
        sig_ready = sem("sig_ready")
        choice_ready = sem("choice_ready")
        best_ready = sem("best_ready")
        best6_ready = sem("best6_ready")
        left_ready = sem("left_ready")
        chosen_ready = sem("chosen_ready")
        wraw_ready = sem("wraw_ready")
        wsum_ready = sem("wsum_ready")
        winv_ready = sem("winv_ready")
        w_ready = sem("w_ready")
        all_added = sem("all_added")
        ct_mm = sem("ct_mm")
        ce_mm = sem("ce_mm")
        ct_ready = sem("ct_ready")
        full_ready = sem("full_ready")
        h1_out = sem("h1_out")
        big_out = sem("big_out")
        yw_out = sem("yw_out")
        ct_out = sem("ct_out")
        pad_out = sem("pad_out")
        N_CONST = 17

        with nc.Block() as block:
            @block.sync
            def _(sp):
                sp.dma_start(w_tok[:, :, :], wtok).then_inc(const_in, 16)
                sp.dma_start(pos_sb[:, 0, :], pos[0:128, :]).then_inc(base_in, 16)
                sp.dma_start(pos_sb[0:IMG - 128, 1, :], pos[128:IMG, :]).then_inc(base_in, 16)
                sp.dma_start(addend[0:1, 0, :], cls).then_inc(base_in, 16)
                sp.dma_start(addend[1:128, 0, :], btok.to_broadcast([127, D])).then_inc(base_in, 16)
                sp.dma_start(addend[0:IMG - 128, 1, :], btok.to_broadcast([IMG - 128, D])).then_inc(base_in, 16)

                def load(n):
                    wait_apart(sp, passed, (tok_mm, n))
                    if isinstance(n, int) and n == 0:
                        sp.wait_ge(pool_set, 1)
                    sp.dma_start(patches[:, :, 1:IMG], xp[n, :, :, :]).then_inc(x_in, 16)
                    wait_apart(sp, passed, (h0_ready, n))
                    sp.dma_start(addend[IMG - 128:128, 1, :], txt[n, 0:256 - IMG, :]).then_inc(t1_in, 16)
                    wait_apart(sp, passed, (h0_txt, n))
                    sp.dma_start(txt2[0:TL[2], :], txt[n, 256 - IMG:TXT, :]).then_inc(t2_in, 16)

                def store(n):
                    wait_apart(sp, passed, (h1_ready, n + 1))
                    rows = acc[bass.ds(n * S, S), :]
                    sp.dma_start(rows[0:256, :].rearrange("(t p) c -> p t c", p=128), h1[:, 0:2, :]).then_inc(h1_out, 16)
                    sp.dma_start(rows[256:S, :], h1[0:TL[2], 2, :]).then_inc(h1_out, 16)
                    wait_apart(sp, passed, (n2["s_lo"], n + 1))
                    for big, own in ((all_hiA, n2["hiA"]), (all_loA, n2["loA"]), (all_B, n2["st"])):
                        sp.dma_start(big[:, bass.ds(n * S, S)].bitcast(F32), own[:, 0:S].bitcast(F32)).then_inc(big_out, 16)
                    wait_apart(sp, passed, (w_ready, n + 1))
                    rows = yw[bass.ds(n * S, S), :]
                    sp.dma_start(rows[0:256, :].rearrange("(t p) c -> p t c", p=128), y2[:, 0:2, :]).then_inc(yw_out, 16)
                    sp.dma_start(rows[256:S, :], y2[0:TL[2], 2, :]).then_inc(yw_out, 16)
                    wait_apart(sp, passed, (ct_ready, n + 1))
                    sp.dma_start(crow[bass.ds(n * E, E), :], countT[:, :]).then_inc(ct_out, 16)

                load(0)
                for half, src in ((0, wqkv[0:DA, :]), (1, wqkv[DA:D, :])):
                    sp.dma_start(raw_qkv[0:DA if half == 0 else DB, half, :], src).then_inc(const_in, 16)
                sp.dma_start(raw_qkv[DB:128, 1, :], wqkv[DA:D, :]).then_inc(const_in, 16)
                for half, src in ((0, wg[0:DA, :]), (1, wg[DA:D, :])):
                    sp.dma_start(raw_g[0:DA if half == 0 else DB, half, :], src).then_inc(const_in, 16)
                sp.dma_start(raw_g[DB:128, 1, :], wg[DA:D, :]).then_inc(const_in, 16)
                sp.dma_start(ident[:, :], c_ident).then_inc(const_in, 16)
                sp.dma_start(b_qk[:, :], bqk).then_inc(const_in, 16)
                sp.dma_start(b_v[:, :], bv.to_broadcast([128, D])).then_inc(const_in, 16)
                sp.dma_start(mask[:, :], c_mask).then_inc(const_in, 16)
                sp.dma_start(e_bias[:, :], ebias.to_broadcast([128, E])).then_inc(const_in, 16)
                sp.dma_start(cum32[:, :, :], c_cum).then_inc(const_in, 16)
                sp.dma_start(up_strict[:, :], c_up).then_inc(const_in, 16)
                sp.dma_start(slot[:, :], c_slot).then_inc(const_in, 16)
                sp.dma_start(iota[:, :], c_iota).then_inc(const_in, 16)
                sp.dma_start(ecol[:, :], c_ecol).then_inc(const_in, 16)
                load(1)
                sp.wait_ge(pool_set, 1)
                sp.dma_start(yw[T:T + CAP, :].rearrange("(h p) c -> p h c", p=CH), zero[:, :, :]).then_inc(pad_out, 16)
                with sp.Fori(0, B - 2) as i:
                    store(i)
                    load(i + 2)
                store(B - 2)
                store(B - 1)
                sp.wait_ge(h1_out, 32 * B)
                sp.wait_ge(big_out, 48 * B)
                sp.wait_ge(yw_out, 32 * B)
                sp.wait_ge(ct_out, 16 * B)
                sp.wait_ge(pad_out, 16)

            def rstd_pool(pool, c, n):
                wait_apart(pool, passed, (c["s_mv"], n + 1))
                pool.tensor_scalar(c["ve"][:, :], c["mv"][:, :, 1], EPS, None, ALU.add).then_inc(c["s_ve"], 1)
                pool.wait_ge(c["s_ve"], n + 1)
                wait(pool, c["s_y"], n)
                pool.tensor_tensor(c["rstd"][:, :], c["ve"][:, :], half_neg[:, :], ALU.pow).then_inc(c["s_rstd"], 1)

            @block.gpsimd
            def _(pool):
                pool.memset(patches[:, :, :], 0.0)
                pool.memset(zero[:, :, :], 0.0).then_inc(pool_set, 1)
                pool.memset(half_neg[:, :], -0.5)
                pool.memset(images_full[:, :, :], 0.0)
                pool.memset(ones_b[:, :], 1.0)
                pool.memset(ones[:, :], 1.0)
                pool.memset(chosen_all[:, :], 0.0)
                pool.memset(choice[:, :, :], LOW)
                pool.memset(w_sum[:, :], 1.0)
                for c in norm:
                    pool.memset(c["mv"][:, :, :], 1.0)
                    for name in ("hiA", "loA", "st"):
                        pool.memset(c[name][:, :].bitcast(F32), 0.0)
                pool.memset(w_inv[:, :], 0.0).then_inc(pool_set, 1)
                pool.wait_ge(pool_set, 2)

                def text_rows(n):
                    wait_apart(pool, passed, (h1_ready, n), (t2_in, 16 * n + 16))
                    pool.tensor_copy(h0[0:TL[2], 2, :], txt2[0:TL[2], :]).then_inc(h0_txt, 1)

                def count_chosen(n):
                    pool.wait_ge(chosen_ready, n + 1)
                    pool.wait_ge(ce_mm, n + 1)
                    for t in range(3):
                        wait(pool, all_added, 3 * n + t)
                        pool.tensor_tensor(chosen_all[0:TL[t], :], chosen_all[0:TL[t], :], chosen[0:TL[t], t, :],
                                           ALU.add).then_inc(all_added, 1)

                text_rows(0)
                rstd_pool(pool, n1, 0)
                def step(i):
                    rstd_pool(pool, n2, i)
                    text_rows(i + 1)
                    rstd_pool(pool, n1, i + 1)
                    count_chosen(i)

                step(0)
                with pool.Fori(1, B - 1) as i:
                    step(i)
                rstd_pool(pool, n2, B - 1)
                count_chosen(B - 1)

            @block.scalar
            def _(act):
                act.wait_ge(const_in, 16 * N_CONST)
                act.activation(qkv_hi[:, :, :], raw_qkv[:, :, :], ACT.Copy).then_inc(set_up_act, 1)
                act.activation(g_hi[:, :, :], raw_g[:, :, :], ACT.Copy).then_inc(set_up_act, 1)
                act.wait_ge(pool_set, 2)

                def split_hi(c, n, used, per):
                    act.wait_ge(c["s_T"], n + 1)
                    wait(act, used, n * per)
                    if c is n2:
                        wait(act, big_out, 48 * n)
                    act.activation(c["hiA"][:, 0:S], c["bankA"][:, 0:S], ACT.Copy)
                    act.activation(c["st"][0:DB, 0:S], c["bankB"][0:DB, 0:S], ACT.Copy).then_inc(c["s_hi"], 1)

                def qk_evac(n):
                    wait(act, sc_mm, 3 * n)
                    for m in range(4):
                        act.wait_ge(qk_mm, 4 * n + m + 1)
                        act.activation(q_k[:, m, :], qk_ps[m][0:96, 0:S], ACT.Identity,
                                       bias=b_qk[:, m:m + 1]).then_inc(qk_ready, 1)

                def sigmoid(n):
                    act.wait_ge(lg_mm, n + 1)
                    wait(act, wraw_ready, 3 * n)
                    act.activation(sig[:, 0:2, :], lg_ps[:, 0:2 * E].rearrange("p (t e) -> p t e", t=2), ACT.Sigmoid)
                    act.activation(sig[0:TL[2], 2, :], lg_ps[0:TL[2], 2 * E:3 * E], ACT.Sigmoid).then_inc(sig_ready, 1)

                def counts(n):
                    act.wait_ge(ct_mm, n + 1)
                    wait(act, ct_out, 16 * n)
                    act.activation(countT[:, :], ct_ps[:, 0:S], ACT.Copy).then_inc(ct_ready, 1)

                split_hi(n1, 0, v_mm, 1)
                qk_evac(0)
                def step(i):
                    split_hi(n2, i, lg_mm, 1)
                    split_hi(n1, i + 1, v_mm, 1)
                    sigmoid(i)
                    qk_evac(i + 1)
                    counts(i)

                step(0)
                with act.Fori(1, B - 1) as i:
                    step(i)
                split_hi(n2, B - 1, lg_mm, 1)
                sigmoid(B - 1)
                counts(B - 1)

            @block.tensor
            def _(pe):
                def split_product(ps, a, w_hi, w_lo, stationary):
                    hiA, loA, st = a
                    passes = ((hiA, w_hi[0]), (hiA, w_lo[0]), (loA, w_hi[0]), (st, w_hi[1]), (st, w_lo[1]))
                    for i, (x, w) in enumerate(passes):
                        mm = pe.matmul(ps, x if stationary else w, w if stationary else x, start=i == 0, stop=i == 4)
                    return mm

                def tokens(n):
                    pe.wait_ge(x_in, 16 * n + 16)
                    wait(pe, qk_ready, 4 * n)
                    for t in range(2):
                        for c in range(KC):
                            mm = pe.matmul(tok_ps[:, t * D:(t + 1) * D], patches[:, c, t * 128:(t + 1) * 128],
                                           w_tok[:, c, :], start=c == 0, stop=c == KC - 1)
                    mm.then_inc(tok_mm, 1)

                def turn(c, n):
                    pe.wait_ge(c["s_y"], n + 1)
                    if c is n1:
                        wait(pe, sc_ready, 3 * n)
                    else:
                        wait(pe, full_ready, n)
                        wait(pe, ct_ready, n)
                    for t in range(3):
                        r, o = TL[t], t * 128
                        pe.transpose(c["bankA"][:, o:o + r], c["y"][0:r, t, 0:DA], ident[0:r, 0:r])
                    for t in range(3):
                        r, o = TL[t], t * 128
                        mm = pe.transpose(c["bankB"][0:DB, o:o + r], c["y"][0:r, t, DA:D], ident[0:r, 0:r])
                    mm.then_inc(c["s_T"], 1)

                def qkv(n):
                    pe.wait_ge(n1["s_lo"], n + 1)
                    wait(pe, sc_ready, 3 * n)
                    data = (n1["hiA"][:, :], n1["loA"][:, :], n1["st"][:, :])
                    for m in range(4):
                        cols = slice(m * 96, (m + 1) * 96)
                        split_product(qk_ps[m][0:96, 0:SP], data, [qkv_hi[:, h, cols] for h in range(2)],
                                      [qkv_lo[:, h, cols] for h in range(2)], False).then_inc(qk_mm, 1)
                    wait(pe, h1_ready, n)
                    for t in range(3):
                        r, o = TL[t], t * 128
                        data = (n1["hiA"][:, o:o + r], n1["loA"][:, o:o + r], n1["st"][:, o:o + r])
                        ps = pv_ps[0:r, t * D:(t + 1) * D] if t < 2 else pv2_ps[0:r, 0:D]
                        mm = split_product(ps, data, [qkv_hi[:, h, 2 * D:] for h in range(2)],
                                           [qkv_lo[:, h, 2 * D:] for h in range(2)], True)
                    mm.then_inc(v_mm, 1)

                def score(n):
                    pe.wait_ge(qk_ready, 4 * n + 4)
                    for t in range(3):
                        r, o = TL[t], t * 128
                        for h in range(2):
                            mm = pe.matmul(sc_ps[t][0:r, 0:S - o], q_k[:, 2 + h, o:o + r], q_k[:, h, o:S],
                                           start=h == 0, stop=h == 1)
                        mm.then_inc(sc_mm, 1)

                def attend(n):
                    pe.wait_ge(sc_ready, 3 * n + 3)
                    pe.wait_ge(v_ready, n + 1)
                    for q in range(3):
                        r = TL[q]
                        ps = pv_ps[0:r, q * D:(q + 1) * D] if q < 2 else pv2_ps[0:r, 0:D]
                        for t in range(q + 1):
                            c = SOFF[t] + (q - t) * 128
                            mm = pe.matmul(ps, scores[0:TL[t], c:c + r], v_sb[0:TL[t], t, :], start=t == 0, stop=t == q)
                    mm.then_inc(pv_mm, 1)

                def logits(n):
                    pe.wait_ge(n2["s_lo"], n + 1)
                    for t in range(3):
                        r, o = TL[t], t * 128
                        data = (n2["hiA"][:, o:o + r], n2["loA"][:, o:o + r], n2["st"][:, o:o + r])
                        mm = split_product(lg_ps[0:r, t * E:(t + 1) * E], data, [g_hi[:, h, :] for h in range(2)],
                                           [g_lo[:, h, :] for h in range(2)], True)
                    mm.then_inc(lg_mm, 1)

                def running_counts(n):
                    pe.wait_ge(chosen_ready, n + 1)
                    wait(pe, all_added, 3 * n)
                    for t in range(3):
                        pe.matmul(ct_ps[:, 0:S], chosen[0:TL[t], t, :], cum[0:TL[t], t, :], start=t == 0, stop=False)
                    pe.matmul(ct_ps[:, 0:S], chosen_all[:, :], ones_b[:, :], start=False, stop=True).then_inc(ct_mm, 1)
                    for t in range(3):
                        pe.matmul(lg_ps[:, 0:E], ones_b[0:TL[t], 0:128], chosen[0:TL[t], t, :], start=t == 0, stop=False)
                    pe.matmul(lg_ps[:, 0:E], ones_b[:, 0:128], chosen_all[:, :], start=False, stop=True).then_inc(ce_mm, 1)

                pe.wait_ge(const_in, 16 * N_CONST)
                tokens(0)
                turn(n1, 0)
                pe.wait_ge(lo_set, 3)
                qkv(0)
                score(0)
                def step(i):
                    attend(i)
                    tokens(i + 1)
                    turn(n2, i)
                    turn(n1, i + 1)
                    logits(i)
                    qkv(i + 1)
                    running_counts(i)
                    score(i + 1)

                step(0)
                with pe.Fori(1, B - 1) as i:
                    step(i)
                attend(B - 1)
                turn(n2, B - 1)
                logits(B - 1)
                running_counts(B - 1)

            @block.vector
            def _(dve):
                dve.wait_ge(base_in, 16 * 5)
                dve.tensor_tensor(addend[:, 0, :], addend[:, 0, :], pos_sb[:, 0, :], ALU.add)
                dve.tensor_tensor(addend[0:IMG - 128, 1, :], addend[0:IMG - 128, 1, :], pos_sb[0:IMG - 128, 1, :],
                                  ALU.add).then_inc(base_set, 1)
                dve.wait_ge(base_set, 1)
                dve.wait_ge(pool_set, 2)

                def stats(c, h, n):
                    for t in range(3):
                        ins = dve.bn_stats(c["stats"][0:TL[t], t, :], h[0:TL[t], t, :])
                    ins.then_inc(c["s_stats"], 1)
                    wait_apart(dve, passed, (c["s_stats"], n + 1))
                    for t in range(3):
                        ins = dve.bn_aggr(c["mv"][0:TL[t], t, :], c["stats"][0:TL[t], t, :])
                    ins.then_inc(c["s_mv"], 1)

                def normed(c, h, n):
                    dve.wait_ge(c["s_rstd"], n + 1)
                    wait(dve, c["s_T"], n)
                    if c is n2:
                        wait(dve, yw_out, 32 * n)
                    for t in range(3):
                        r = TL[t]
                        ins = dve.tensor_scalar(c["y"][0:r, t, 0:D], h[0:r, t, :], c["mv"][0:r, t, 0:1],
                                                c["rstd"][0:r, t:t + 1], ALU.subtract, ALU.mult)
                    ins.then_inc(c["s_y"], 1)

                def split_lo(c, n):
                    dve.wait_ge(c["s_hi"], n + 1)
                    dve.tensor_tensor(c["loA"][:, 0:S], c["bankA"][:, 0:S], c["hiA"][:, 0:S].bitcast(F32), ALU.subtract)
                    dve.tensor_tensor(c["st"][DB:128, 0:S], c["bankB"][0:DB, 0:S], c["st"][0:DB, 0:S].bitcast(F32),
                                      ALU.subtract).then_inc(c["s_lo"], 1)

                def token_rows(n):
                    dve.wait_ge(tok_mm, n + 1)
                    dve.wait_ge(t1_in, 16 * n + 16)
                    dve.tensor_tensor(h0[:, 0:2, :], tok_ps[:, 0:2 * D].rearrange("p (t c) -> p t c", t=2),
                                      addend[:, :, :], ALU.add).then_inc(h0_ready, 1)
                    dve.wait_ge(h0_ready, n + 1)
                    dve.wait_ge(h0_txt, n + 1)
                    stats(n1, h0, n)

                def residual(n):
                    dve.wait_ge(pv_mm, n + 1)
                    wait(dve, h1_out, 32 * n)
                    dve.tensor_tensor(h1[:, 0:2, :], pv_ps[:, 0:2 * D].rearrange("p (t c) -> p t c", t=2),
                                      h0[:, 0:2, :], ALU.add)
                    dve.tensor_tensor(h1[0:TL[2], 2, :], pv2_ps[0:TL[2], 0:D], h0[0:TL[2], 2, :],
                                      ALU.add).then_inc(h1_ready, 1)
                    dve.wait_ge(h1_ready, n + 1)
                    stats(n2, h1, n)

                def values(n):
                    dve.wait_ge(v_mm, n + 1)
                    for t in range(3):
                        r = TL[t]
                        ps = pv_ps[0:r, t * D:(t + 1) * D] if t < 2 else pv2_ps[0:r, 0:D]
                        ins = dve.tensor_tensor(v_sb[0:r, t, :], ps, b_v[0:r, :], ALU.add)
                    ins.then_inc(v_ready, 1)

                def decay(n):
                    for t in range(3):
                        r, w = TL[t], S - t * 128
                        dve.wait_ge(sc_mm, 3 * n + t + 1)
                        dve.tensor_tensor(scores[0:r, SOFF[t]:SOFF[t] + w], sc_ps[t][0:r, 0:w],
                                          mask[0:r, SOFF[t]:SOFF[t] + w], ALU.mult).then_inc(sc_ready, 1)

                def route(n):
                    dve.wait_ge(sig_ready, n + 1)
                    for t in range(3):
                        r = TL[t]
                        ins = dve.tensor_tensor(choice[0:r, t, 0:E], sig[0:r, t, :], e_bias[0:r, :], ALU.add)
                    ins.then_inc(choice_ready, 1)
                    wait_apart(dve, passed, (choice_ready, n + 1))
                    for t in range(3):
                        r = TL[t]
                        ins = dve.max(best[0:r, t, :], choice[0:r, t, :])
                    ins.then_inc(best_ready, 1)
                    dve.wait_ge(best_ready, n + 1)
                    dve.memset(best[:, :, K:8], LOW).then_inc(best6_ready, 1)
                    wait_apart(dve, passed, (best6_ready, n + 1))
                    for t in range(3):
                        r = TL[t]
                        ins = dve.match_replace(left[0:r, t, :], best[0:r, t, :], choice[0:r, t, :], ROUTED)
                    ins.then_inc(left_ready, 1)
                    dve.wait_ge(left_ready, n + 1)
                    wait(dve, all_added, 3 * n)
                    for t in range(3):
                        r = TL[t]
                        ins = dve.tensor_tensor(chosen[0:r, t, :], left[0:r, t, 0:E], choice[0:r, t, 0:E], ALU.not_equal)
                    ins.then_inc(chosen_ready, 1)
                    dve.wait_ge(chosen_ready, n + 1)
                    for t in range(3):
                        r = TL[t]
                        ins = dve.scalar_tensor_tensor(w_raw[0:r, t, :], sig[0:r, t, :], 1.0, chosen[0:r, t, :],
                                                       ALU.mult, ALU.mult, accum_out=w_sum[0:r, t:t + 1])
                        ins.then_inc(wraw_ready, 1)
                    dve.wait_ge(wraw_ready, 3 * n + 3)
                    dve.tensor_scalar(w_sum2[:, :], w_sum[:, :], 1e-20, None, ALU.add).then_inc(wsum_ready, 1)
                    dve.wait_ge(wsum_ready, n + 1)
                    dve.reciprocal(w_inv[:, :], w_sum2[:, :]).then_inc(winv_ready, 1)
                    dve.wait_ge(winv_ready, n + 1)
                    for t in range(3):
                        r = TL[t]
                        ins = dve.tensor_scalar(y2[0:r, t, D:YW], w_raw[0:r, t, :], w_inv[0:r, t:t + 1], SCALE,
                                                ALU.mult, ALU.mult)
                    ins.then_inc(w_ready, 1)

                def count_full(n):
                    dve.wait_ge(ce_mm, n + 1)
                    for h in range(2):
                        ins = dve.scalar_tensor_tensor(images_full[:, h, :], lg_ps[0:CH, 0:E], slot[:, h:h + 1],
                                                       images_full[:, h, :], ALU.is_le, ALU.add)
                    ins.then_inc(full_ready, 1)

                token_rows(0)
                normed(n1, h0, 0)
                dve.wait_ge(const_in, 16 * N_CONST)
                dve.wait_ge(set_up_act, 2)
                dve.tensor_tensor(qkv_lo[:, :, :], raw_qkv[:, :, :], qkv_hi[:, :, :].bitcast(F32),
                                  ALU.subtract).then_inc(lo_set, 1)
                dve.tensor_tensor(g_lo[:, :, :], raw_g[:, :, :], g_hi[:, :, :].bitcast(F32),
                                  ALU.subtract).then_inc(lo_set, 1)
                dve.tensor_copy(cum[:, :, :], cum32[:, :, :]).then_inc(lo_set, 1)
                split_lo(n1, 0)
                values(0)
                decay(0)
                def step(i):
                    residual(i)
                    token_rows(i + 1)
                    normed(n2, h1, i)
                    normed(n1, h0, i + 1)
                    split_lo(n2, i)
                    split_lo(n1, i + 1)
                    route(i)
                    values(i + 1)
                    count_full(i)
                    decay(i + 1)

                step(0)
                with dve.Fori(1, B - 1) as i:
                    step(i)
                residual(B - 1)
                normed(n2, h1, B - 1)
                split_lo(n2, B - 1)
                route(B - 1)
                count_full(B - 1)


def block_b(nc, psum, ident, ones, slot, iota, ecol, up_strict, images_full, countT, yw, acc, crow, wgu, wdn):
    with ExitStack() as ctx:
        def sb(name, shape, dt=F32):
            return ctx.enter_context(nc.sbuf_tensor(name, shape, dt))

        def sem(name):
            return ctx.enter_context(nc.semaphore(name))

        active = sb("active", [128, 1])
        rank = sb("rank", [128, 2])
        idle_a = sb("idle_a", [128, 1])
        idle = sb("idle", [128, 1])
        diff = sb("diff", [128, 1])
        place = sb("place", [128, 1])
        pick = sb("pick", [128, E])
        order = sb("order", [1, LIST], I32)
        n_active = sb("n_active", [1, 1], I32)
        full_clip = sb("full_clip", [CH, 2, E])
        row_of = sb("row_of", [CH, 2, E], I32)
        tok_base = sb("tok_base", [CH, 2, E])
        row_idx = sb("row_idx", [CH, 2], I32)
        count_rows = sb("slot_counts", [CH, 2, S])
        le = sb("le", [CH, 2, S])
        before = sb("before", [CH, 2])
        tok = sb("tok", [CH, 2])
        past = sb("past", [CH, 2])
        slot_tok = sb("slot_tok", [CH, LIST, 2], I32)
        get_idx = sb("get_idx", [CH, 2], I32)
        put_idx = sb("put_idx", [CH, 2], I32)
        x_rows = [sb(f"x_rows{p}", [CH, 2, YW]) for p in range(2)]
        w_slot = [sb(f"w_slot{p}", [CH, 2]) for p in range(2)]
        x_hiA = sb("x_hiA", [128, CAP], F32R)
        x_loA = sb("x_loA", [128, CAP], F32R)
        x_st = sb("x_st", [128, CAP], F32R)
        raw_gu = [sb(f"raw_gu{p}", [128, 2, 2 * I]) for p in range(2)]
        raw_dn = [sb(f"raw_dn{p}", [F, EM, D]) for p in range(2)]
        gu_hi = [sb(f"gu_hi{p}", [128, 2, 2 * I], F32R) for p in range(2)]
        gu_lo = [sb(f"gu_lo{p}", [128, 2, 2 * I], F32R) for p in range(2)]
        dn_hi = [sb(f"dn_hi{p}", [F, EM, D], F32R) for p in range(2)]
        dn_lo = [sb(f"dn_lo{p}", [F, EM, D], F32R) for p in range(2)]
        gate = sb("gate", [F, EM, CAP])
        inter = sb("inter", [F, EM, CAP])
        in_hi = sb("in_hi", [F, EM, CAP], F32R)
        in_lo = sb("in_lo", [F, EM, CAP], F32R)
        y_rows = sb("y_rows", [CH, 2, D])
        gu_ps = psum[0:4]
        xT_ps, dn_ps, set_ps = psum[4], psum[5], psum[6]

        passed = sem("passed_b")
        set_dve = sem("set_dve")
        set_pe = sem("set_pe")
        order_ready = sem("order_ready")
        row_idx_ready = sem("row_idx_ready")
        cr_in = sem("cr_in")
        before_ready = sem("before_ready")
        tok_ready = sem("tok_ready")
        past_ready = sem("past_ready")
        idx_ready = sem("idx_ready")
        get_idx_ready = sem("get_idx_ready")
        x_in = [sem(f"x_in{p}") for p in range(2)]
        wslot_ready = sem("wslot_ready")
        xT_mm = sem("xT_mm")
        x_hi = sem("x_hi_ready")
        x_split = sem("x_split")
        raw_in = [sem(f"raw_in{p}") for p in range(2)]
        gu_hi_ready = sem("gu_hi_ready")
        dn_hi_ready = sem("dn_hi_ready")
        gu_split = sem("gu_split")
        dn_split = sem("dn_split")
        gu_mm = sem("gu_mm")
        gate_ready = sem("gate_ready")
        inter_ready = sem("inter_ready")
        in_hi_ready = sem("in_hi_ready")
        in_lo_ready = sem("in_lo_ready")
        dn_mm = sem("dn_mm")
        y_ready = sem("y_rows_ready")
        put_idx_ready = sem("put_idx_ready")
        added = sem("added")
        zero_rows = sem("zero_rows")

        def load_order(eng, n):
            return eng.value_load(order[0:1, bass.ds(n, 1)], min_val=0, max_val=E - 1)

        def load_active(eng):
            eng.wait_ge(order_ready, 1)
            return eng.value_load(n_active[0:1, 0:1], min_val=K, max_val=E)

        def arrivals(n, p, per):
            return (n - p) * (per // 2) + per

        with nc.Block() as block:
            @block.sync
            def _(sp):
                act_n = load_active(sp)

                def load(n, p, first=False):
                    if not first:
                        wait_apart(sp, passed, (gu_split, 2 * n - 2), (dn_split, n - 1))
                    e = load_order(sp, n)
                    sp.dma_start(raw_gu[p][:, 0, :], wgu[e, 0:DA, :]).then_inc(raw_in[p], 16)
                    sp.dma_start(raw_gu[p][0:DB, 1, :], wgu[e, DA:D, :]).then_inc(raw_in[p], 16)
                    sp.dma_start(raw_gu[p][DB:128, 1, :], wgu[e, DA:D, :]).then_inc(raw_in[p], 16)
                    sp.dma_start(raw_dn[p][:, :, :], wdn[e, :, :].rearrange("(c p) n -> p c n", p=F)).then_inc(raw_in[p], 16)

                load(0, 0, True)
                load(1, 1, True)
                with sp.Fori(0, act_n, 2) as j:
                    for p in range(2):
                        load(j + p + 2, p)
                last = (act_n + 1) // 2
                wait_apart(sp, passed, (raw_in[0], last * 64 + 64), (raw_in[1], last * 64 + 64))

            @block.gpsimd
            def _(pool):
                act_n = load_active(pool)

                def get_counts(n):
                    e = load_order(pool, n)
                    wait_apart(pool, passed, (idx_ready, n))
                    pool.tensor_copy(row_idx[:, :], row_of[:, :, bass.ds(e, 1)].rearrange("p h o -> p (h o)")).then_inc(row_idx_ready, 1)
                    wait_apart(pool, passed, (row_idx_ready, n + 1))
                    for h in range(2):
                        pool.indirect_dma_start(count_rows[:, h, :], None, crow[:, :],
                                                bass.IndirectOffsetOnAxis(ap=row_idx[:, h:h + 1], axis=0)).then_inc(cr_in, 16)

                def get_tokens(n, p, first=False):
                    waits = [(idx_ready, n + 1)]
                    if not first:
                        waits += [(x_in[1 - p], arrivals(n - 1, 1 - p, 32)), (xT_mm, n - 1), (wslot_ready, n - 1)]
                    elif n == 1:
                        waits += [(x_in[0], 32)]
                    wait_apart(pool, passed, *waits)
                    pool.tensor_copy(get_idx[:, :], slot_tok[:, bass.ds(n, 1), :].rearrange("p o h -> p (o h)")).then_inc(get_idx_ready, 1)
                    wait_apart(pool, passed, (get_idx_ready, n + 1))
                    for h in range(2):
                        pool.indirect_dma_start(x_rows[p][:, h, :], None, yw[:, :],
                                                bass.IndirectOffsetOnAxis(ap=get_idx[:, h:h + 1], axis=0)).then_inc(x_in[p], 16)

                def down_lo(n, p):
                    pool.wait_ge(dn_hi_ready, n + 1)
                    pool.tensor_tensor(dn_lo[p][:, :, :], raw_dn[p][:, :, :], dn_hi[p][:, :, :].bitcast(F32),
                                       ALU.subtract).then_inc(dn_split, 1)

                def inter_lo(n):
                    for m in range(EM):
                        pool.wait_ge(in_hi_ready, 4 * n + m + 1)
                        pool.tensor_tensor(in_lo[:, m, :], inter[:, m, :], in_hi[:, m, :].bitcast(F32),
                                           ALU.subtract).then_inc(in_lo_ready, 1)

                def add_rows(n):
                    wait_apart(pool, passed, (added, n * 32 + 16))
                    pool.tensor_copy(put_idx[:, :], slot_tok[:, bass.ds(n, 1), :].rearrange("p o h -> p (o h)")).then_inc(put_idx_ready, 1)
                    wait_apart(pool, passed, (put_idx_ready, n + 1), (y_ready, n + 2))
                    for h in range(2):
                        pool.indirect_dma_start(acc[:, :], bass.IndirectOffsetOnAxis(ap=put_idx[:, h:h + 1], axis=0),
                                                y_rows[:, h, :], None, compute_op=ALU.add).then_inc(added, 16)

                pool.memset(y_rows[:, :, :], 0.0).then_inc(zero_rows, 1)
                pool.wait_ge(zero_rows, 1)
                pool.dma_start(acc[T:T + CAP, :].rearrange("(h p) c -> p h c", p=CH), y_rows[:, :, :]).then_inc(added, 16)
                pool.sem_inc(in_lo_ready, 1)
                get_counts(0)
                down_lo(0, 0)
                get_tokens(0, 0, True)
                get_counts(1)
                get_tokens(1, 1, True)
                get_counts(2)
                with pool.Fori(0, act_n, 2) as j:
                    for p in range(2):
                        n = j + p
                        down_lo(n + 1, 1 - p)
                        inter_lo(n)
                        get_tokens(n + 2, p)
                        get_counts(n + 3)
                        add_rows(n)
                pairs = (act_n + 1) // 2
                wait_apart(pool, passed, (added, pairs * 64 + 16), (cr_in, pairs * 64 + 96),
                           (x_in[0], pairs * 32 + 32), (x_in[1], pairs * 32 + 32))

            @block.scalar
            def _(act):
                act_n = load_active(act)

                def gu_part(n, p, h):
                    if h == 0:
                        act.wait_ge(raw_in[p], arrivals(n, p, 64))
                    act.activation(gu_hi[p][:, h, :], raw_gu[p][:, h, :], ACT.Copy).then_inc(gu_hi_ready, 1)

                def down_hi(n, p):
                    act.activation(dn_hi[p][:, :, :], raw_dn[p][:, :, :], ACT.Copy).then_inc(dn_hi_ready, 1)

                def split_x(n):
                    act.wait_ge(xT_mm, n + 1)
                    act.activation(x_hiA[:, :], xT_ps[:, 0:CAP], ACT.Copy)
                    act.activation(x_st[0:DB, :], xT_ps[0:DB, CAP:2 * CAP], ACT.Copy).then_inc(x_hi, 1)

                def silu(n, m):
                    act.wait_ge(gu_mm, 4 * n + m + 1)
                    act.activation(gate[:, m, :], gu_ps[m][0:F, 0:CAP], ACT.Silu).then_inc(gate_ready, 1)

                def hi(n, m):
                    act.wait_ge(inter_ready, 4 * n + m + 1)
                    act.activation(in_hi[:, m, :], inter[:, m, :], ACT.Copy).then_inc(in_hi_ready, 1)

                gu_part(0, 0, 0)
                gu_part(0, 0, 1)
                down_hi(0, 0)
                split_x(0)
                with act.Fori(0, act_n, 2) as j:
                    for p in range(2):
                        n = j + p
                        gu_part(n + 1, 1 - p, 0)
                        silu(n, 0)
                        silu(n, 1)
                        gu_part(n + 1, 1 - p, 1)
                        hi(n, 0)
                        silu(n, 2)
                        hi(n, 1)
                        silu(n, 3)
                        hi(n, 2)
                        hi(n, 3)
                        down_hi(n + 1, 1 - p)
                        split_x(n + 1)

            @block.tensor
            def _(pe):
                pe.wait_ge(set_dve, 1)
                pe.matmul(set_ps[:, 0:1], up_strict[:, :], active[:, :], start=True, stop=True)
                pe.matmul(set_ps[:, 1:2], ones[:, :], active[:, :], start=True, stop=True).then_inc(set_pe, 1)
                pe.wait_ge(set_dve, 7)
                pe.matmul(xT_ps[0:1, 0:E], ecol[:, :], pick[:, :], start=True, stop=True).then_inc(set_pe, 1)
                act_n = load_active(pe)

                def turn(n, p):
                    pe.wait_ge(x_in[p], arrivals(n, p, 32))
                    for h in range(2):
                        pe.transpose(xT_ps[:, h * CH:(h + 1) * CH], x_rows[p][:, h, 0:DA], ident[0:CH, 0:CH])
                        mm = pe.transpose(xT_ps[0:DB, CAP + h * CH:CAP + (h + 1) * CH], x_rows[p][:, h, DA:D],
                                          ident[0:CH, 0:CH])
                    mm.then_inc(xT_mm, 1)

                def gate_up(n, p):
                    pe.wait_ge(x_split, n + 1)
                    pe.wait_ge(gu_split, 2 * n + 2)
                    for m in range(EM):
                        for half in range(2):
                            cols = slice(half * I + m * F, half * I + (m + 1) * F)
                            ps = gu_ps[m][0:F, half * CAP:(half + 1) * CAP]
                            passes = ((x_hiA, gu_hi[p][:, 0, cols]), (x_hiA, gu_lo[p][:, 0, cols]),
                                      (x_loA, gu_hi[p][:, 0, cols]), (x_st, gu_hi[p][:, 1, cols]),
                                      (x_st, gu_lo[p][:, 1, cols]))
                            for i, (x, w) in enumerate(passes):
                                mm = pe.matmul(ps, w, x[:, :], start=i == 0, stop=i == 4)
                        mm.then_inc(gu_mm, 1)

                def down(n, p):
                    pe.wait_ge(y_ready, n + 1)
                    pe.wait_ge(dn_split, n + 1)
                    for h in range(2):
                        rows = slice(h * CH, (h + 1) * CH)
                        for m in range(EM):
                            if h == 0:
                                pe.wait_ge(in_hi_ready, 4 * n + m + 1)
                                pe.wait_ge(in_lo_ready, 4 * n + m + 2)
                            for i, (x, w) in enumerate(((in_hi, dn_hi), (in_hi, dn_lo), (in_lo, dn_hi))):
                                mm = pe.matmul(dn_ps[0:CH, h * D:(h + 1) * D], x[:, m, rows], w[p][:, m, :],
                                               start=m == 0 and i == 0, stop=m == EM - 1 and i == 2)
                    mm.then_inc(dn_mm, 1)

                turn(0, 0)
                with pe.Fori(0, act_n, 2) as j:
                    for p in range(2):
                        n = j + p
                        gate_up(n, p)
                        turn(n + 1, 1 - p)
                        down(n, p)

            @block.vector
            def _(dve):
                steps = [0]

                def then(ins):
                    steps[0] += 1
                    ins.then_inc(set_dve, 1)
                    dve.wait_ge(set_dve, steps[0])

                then(dve.tensor_scalar(active[:, :], countT[:, S - 1:S], 0.0, None, ALU.is_gt))
                dve.wait_ge(set_pe, 1)
                then(dve.tensor_copy(rank[:, :], set_ps[:, 0:2]))
                then(dve.tensor_tensor(idle_a[:, :], rank[:, 1:2], ecol[:, :], ALU.add))
                then(dve.tensor_tensor(idle[:, :], idle_a[:, :], rank[:, 0:1], ALU.subtract))
                then(dve.tensor_tensor(diff[:, :], rank[:, 0:1], idle[:, :], ALU.subtract))
                then(dve.scalar_tensor_tensor(place[:, :], diff[:, :], active[:, 0:1], idle[:, :], ALU.mult, ALU.add))
                then(dve.tensor_scalar(pick[:, :], iota[:, :], place[:, 0:1], None, ALU.is_equal))
                then(dve.tensor_scalar(full_clip[:, :, :], images_full[:, :, :], float(B - 1), None, ALU.min))
                for h in range(2):
                    dve.scalar_tensor_tensor(row_of[:, h, :], full_clip[:, h, :], float(E), iota[0:CH, :], ALU.mult, ALU.add)
                dve.tensor_scalar(tok_base[:, :, :], full_clip[:, :, :], float(S), None, ALU.mult)
                then(dve.memset(order[:, :], 0))
                dve.tensor_copy(n_active[:, :], rank[0:1, 1:2])
                dve.wait_ge(set_pe, 2)
                dve.tensor_copy(order[:, 0:E], xT_ps[0:1, 0:E]).then_inc(order_ready, 1)
                act_n = load_active(dve)

                def slots(n):
                    e = load_order(dve, n)
                    wait_apart(dve, passed, (cr_in, 32 * n + 32))
                    for h in range(2):
                        ins = dve.tensor_scalar(le[:, h, :], count_rows[:, h, :], slot[:, h:h + 1], 0.0, ALU.is_le, ALU.add,
                                                accum_out=before[:, h:h + 1])
                    ins.then_inc(before_ready, 1)
                    dve.wait_ge(before_ready, n + 1)
                    dve.tensor_tensor(tok[:, :], before[:, :], tok_base[:, :, bass.ds(e, 1)].rearrange("p h o -> p (h o)"),
                                      ALU.add).then_inc(tok_ready, 1)
                    dve.wait_ge(tok_ready, n + 1)
                    dve.scalar_tensor_tensor(past[:, :], tok[:, :], float(T), slot[:, :], ALU.is_ge,
                                             ALU.mult).then_inc(past_ready, 1)
                    dve.wait_ge(past_ready, n + 1)
                    dve.tensor_tensor(slot_tok[:, bass.ds(n, 1), :].rearrange("p o h -> p (o h)"), tok[:, :], past[:, :],
                                      ALU.add).then_inc(idx_ready, 1)

                def slot_weights(n, p):
                    e = load_order(dve, n)
                    wait_apart(dve, passed, (x_in[p], arrivals(n, p, 32)))
                    dve.tensor_copy(w_slot[p][:, :], x_rows[p][:, :, bass.ds(e + D, 1)].rearrange("p h o -> p (h o)")).then_inc(wslot_ready, 1)

                def split_x(n):
                    dve.wait_ge(x_hi, n + 1)
                    dve.tensor_tensor(x_loA[:, :], xT_ps[:, 0:CAP], x_hiA[:, :].bitcast(F32), ALU.subtract)
                    dve.tensor_tensor(x_st[DB:128, :], xT_ps[0:DB, CAP:2 * CAP], x_st[0:DB, :].bitcast(F32),
                                      ALU.subtract).then_inc(x_split, 1)

                def gu_low(n, p, h):
                    dve.wait_ge(gu_hi_ready, 2 * n + h + 1)
                    dve.tensor_tensor(gu_lo[p][:, h, :], raw_gu[p][:, h, :], gu_hi[p][:, h, :].bitcast(F32),
                                      ALU.subtract).then_inc(gu_split, 1)

                def gated(n, m):
                    dve.wait_ge(gate_ready, 4 * n + m + 1)
                    dve.wait_ge(in_lo_ready, 4 * n + 1)
                    dve.tensor_tensor(inter[:, m, :], gate[:, m, :], gu_ps[m][0:F, CAP:2 * CAP],
                                      ALU.mult).then_inc(inter_ready, 1)

                def weigh(n, p):
                    dve.wait_ge(dn_mm, n + 1)
                    dve.wait_ge(added, 32 * n + 16)
                    dve.wait_ge(wslot_ready, n + 1)
                    for h in range(2):
                        ins = dve.tensor_scalar(y_rows[:, h, :], dn_ps[0:CH, h * D:(h + 1) * D], w_slot[p][:, h:h + 1],
                                                None, ALU.mult)
                    ins.then_inc(y_ready, 1)

                dve.sem_inc(y_ready, 1)
                slots(0)
                slots(1)
                gu_low(0, 0, 0)
                gu_low(0, 0, 1)
                split_x(0)
                slot_weights(0, 0)
                with dve.Fori(0, act_n, 2) as j:
                    for p in range(2):
                        n = j + p
                        gated(n, 0)
                        gu_low(n + 1, 1 - p, 0)
                        gated(n, 1)
                        gated(n, 2)
                        gu_low(n + 1, 1 - p, 1)
                        gated(n, 3)
                        slots(n + 2)
                        split_x(n + 1)
                        slot_weights(n + 1, 1 - p)
                        weigh(n, p)


def block_c(nc, psum, all_hiA, all_loA, all_B, acc, wsg, wsu, wsd, out):
    with ExitStack() as ctx:
        def sb(name, shape, dt=F32):
            return ctx.enter_context(nc.sbuf_tensor(name, shape, dt))

        def sem(name):
            return ctx.enter_context(nc.semaphore(name))

        RAW = 2 * IS
        raw = sb("raw_s", [128, RAW])
        raw_d = sb("raw_sd", [F, SM, D])
        s_hi = sb("s_hi", [128, 2, RAW], F32R)
        s_lo = sb("s_lo", [128, 2, RAW], F32R)
        d_hi = sb("d_hi", [F, SM, D], F32R)
        d_lo = sb("d_lo", [F, SM, D], F32R)
        gate = [sb(f"s_gate{i}", [F, CHUNK]) for i in range(2)]
        inter = [sb(f"s_inter{i}", [F, CHUNK]) for i in range(2)]
        in_hi = sb("s_in_hi", [F, SM, CHUNK], F32R)
        in_lo = sb("s_in_lo", [F, SM, CHUNK], F32R)
        rows_in = sb("rows_in", [128, CHUNK // 128, D])
        rows_out = sb("rows_out", [128, CHUNK // 128, D])

        passed = sem("passed_c")
        raw_in = sem("raw_s_in")
        hi_set = sem("s_hi_set")
        lo_set = sem("s_lo_set")
        g_mm = sem("g_mm")
        u_mm = sem("u_mm")
        gate_ready = sem("s_gate_ready")
        inter_ready = sem("s_inter_ready")
        hi_ready = sem("s_in_hi_ready")
        lo_ready = sem("s_in_lo_ready")
        d_mm = sem("d_mm")
        sum_ready = sem("sum_ready")
        acc_in = sem("acc_in")
        out_done = sem("out_done")
        g_ps = [psum[0], psum[1]]
        u_ps = [psum[2], psum[3]]
        d_ps = psum[4:8]
        TILES = CHUNK // 128

        def first_token(c):
            return NCHUNK * CHUNK if isinstance(c, int) and c == 0 else (c - 1) * CHUNK

        def tiles_before(c):
            return 0 if isinstance(c, int) and c == 0 else c * TILES - (TILES - 1)

        def tiles(width):
            return [(t, min(128, width - 128 * t)) for t in range((width + 127) // 128)]

        with nc.Block() as block:
            @block.sync
            def _(sp):
                for h in range(2):
                    if h:
                        sp.wait_ge(hi_set, 1)
                        sp.wait_ge(lo_set, 1)
                    for i, w in enumerate((wsg, wsu)):
                        cols = slice(i * IS, (i + 1) * IS)
                        if h == 0:
                            sp.dma_start(raw[:, cols], w[0:DA, :]).then_inc(raw_in, 16)
                        else:
                            sp.dma_start(raw[0:DB, cols], w[DA:D, :]).then_inc(raw_in, 16)
                            sp.dma_start(raw[DB:128, cols], w[DA:D, :]).then_inc(raw_in, 16)
                sp.dma_start(raw_d[:, :, :], wsd.rearrange("(c p) n -> p c n", p=F)).then_inc(raw_in, 16)

                def load(c, width):
                    wait_apart(sp, passed, (sum_ready, tiles_before(c)))
                    rows = acc[bass.ds(first_token(c), width), :]
                    if width == CHUNK:
                        sp.dma_start(rows_in[:, :, :], rows.rearrange("(t p) n -> p t n", p=128)).then_inc(acc_in, 16)
                    else:
                        sp.dma_start(rows_in[0:width, 0, :], rows).then_inc(acc_in, 16)

                def store(c, width):
                    wait_apart(sp, passed, (sum_ready, tiles_before(c) + len(tiles(width))))
                    rows = out[bass.ds(first_token(c), width), :]
                    if width == CHUNK:
                        sp.dma_start(rows.rearrange("(t p) n -> p t n", p=128), rows_out[:, :, :]).then_inc(out_done, 16)
                    else:
                        sp.dma_start(rows, rows_out[0:width, 0, :]).then_inc(out_done, 16)

                load(0, TAIL)
                store(0, TAIL)
                with sp.Fori(1, NCHUNK + 1) as c:
                    load(c, CHUNK)
                    store(c, CHUNK)
                sp.wait_ge(out_done, 16 * (NCHUNK + 1))

            @block.scalar
            def _(act):
                act.wait_ge(raw_in, 32)
                act.activation(s_hi[:, 0, :], raw[:, :], ACT.Copy).then_inc(hi_set, 1)
                act.wait_ge(raw_in, 112)
                act.activation(s_hi[:, 1, :], raw[:, :], ACT.Copy).then_inc(hi_set, 1)
                act.activation(d_hi[:, :, :], raw_d[:, :, :], ACT.Copy).then_inc(hi_set, 1)

                def silu(c, m, width):
                    act.wait_ge(g_mm, SM * c + m + 1)
                    if m >= 2:
                        act.wait_ge(inter_ready, SM * c + m - 1)
                    else:
                        wait(act, inter_ready, SM * c)
                    act.activation(gate[m % 2][:, 0:width], g_ps[m % 2][0:F, 0:width], ACT.Silu).then_inc(gate_ready, 1)

                def hi(c, m, width):
                    act.wait_ge(inter_ready, SM * c + m + 1)
                    act.activation(in_hi[:, m, 0:width], inter[m % 2][:, 0:width], ACT.Copy).then_inc(hi_ready, 1)

                def chunk(c, width):
                    silu(c, 0, width)
                    for m in range(1, SM):
                        silu(c, m, width)
                        hi(c, m - 1, width)
                    hi(c, SM - 1, width)

                chunk(0, TAIL)
                with act.Fori(1, NCHUNK + 1) as c:
                    chunk(c, CHUNK)

            @block.vector
            def _(dve):
                dve.wait_ge(hi_set, 1)
                dve.tensor_tensor(s_lo[:, 0, :], raw[:, :], s_hi[:, 0, :].bitcast(F32), ALU.subtract).then_inc(lo_set, 1)
                dve.wait_ge(hi_set, 2)
                dve.tensor_tensor(s_lo[:, 1, :], raw[:, :], s_hi[:, 1, :].bitcast(F32), ALU.subtract).then_inc(lo_set, 1)
                dve.wait_ge(hi_set, 3)
                dve.tensor_tensor(d_lo[:, :, :], raw_d[:, :, :], d_hi[:, :, :].bitcast(F32), ALU.subtract).then_inc(lo_set, 1)

                def gated(c, m, width):
                    dve.wait_ge(gate_ready, SM * c + m + 1)
                    dve.wait_ge(u_mm, SM * c + m + 1)
                    if m >= 2:
                        dve.wait_ge(lo_ready, SM * c + m - 1)
                    else:
                        wait(dve, lo_ready, SM * c)
                    dve.tensor_tensor(inter[m % 2][:, 0:width], gate[m % 2][:, 0:width], u_ps[m % 2][0:F, 0:width],
                                      ALU.mult).then_inc(inter_ready, 1)

                def lo(c, m, width):
                    dve.wait_ge(hi_ready, SM * c + m + 1)
                    dve.tensor_tensor(in_lo[:, m, 0:width], inter[m % 2][:, 0:width], in_hi[:, m, 0:width].bitcast(F32),
                                      ALU.subtract).then_inc(lo_ready, 1)

                def chunk(c, width):
                    gated(c, 0, width)
                    for m in range(1, SM):
                        gated(c, m, width)
                        lo(c, m - 1, width)
                    lo(c, SM - 1, width)
                    dve.wait_ge(acc_in, 16 * c + 16)
                    wait(dve, out_done, 16 * c)
                    for t, r in tiles(width):
                        dve.wait_ge(d_mm, tiles_before(c) + t + 1)
                        dve.tensor_tensor(rows_out[0:r, t, :], d_ps[t][0:r, 0:D], rows_in[0:r, t, :],
                                          ALU.add).then_inc(sum_ready, 1)

                chunk(0, TAIL)
                with dve.Fori(1, NCHUNK + 1) as c:
                    chunk(c, CHUNK)

            @block.tensor
            def _(pe):
                pe.wait_ge(lo_set, 3)

                def chunk(c, width):
                    data = [big[:, bass.ds(first_token(c), width)] for big in (all_hiA, all_loA, all_B)]
                    for m in range(SM):
                        for half, ps, done in ((0, g_ps, g_mm), (1, u_ps, u_mm)):
                            if m >= 2:
                                pe.wait_ge(inter_ready, SM * c + m - 1)
                            else:
                                wait(pe, inter_ready, SM * c)
                            cols = slice(half * IS + m * F, half * IS + (m + 1) * F)
                            passes = ((data[0], s_hi[:, 0, cols]), (data[0], s_lo[:, 0, cols]), (data[1], s_hi[:, 0, cols]),
                                      (data[2], s_hi[:, 1, cols]), (data[2], s_lo[:, 1, cols]))
                            for i, (x, w) in enumerate(passes):
                                mm = pe.matmul(ps[m % 2][0:F, 0:width], w, x, start=i == 0, stop=i == 4)
                            mm.then_inc(done, 1)
                    for t, r in tiles(width):
                        wait(pe, sum_ready, tiles_before(c))
                        for m in range(SM):
                            if t == 0:
                                pe.wait_ge(hi_ready, SM * c + m + 1)
                                pe.wait_ge(lo_ready, SM * c + m + 1)
                            rows = slice(t * 128, t * 128 + r)
                            for i, (x, w) in enumerate(((in_hi, d_hi), (in_hi, d_lo), (in_lo, d_hi))):
                                mm = pe.matmul(d_ps[t][0:r, 0:D], x[:, m, rows], w[:, m, :],
                                               start=m == 0 and i == 0, stop=m == SM - 1 and i == 2)
                        mm.then_inc(d_mm, 1)

                chunk(0, TAIL)
                with pe.Fori(1, NCHUNK + 1) as c:
                    chunk(c, CHUNK)


def constants():
    import numpy as np

    i = np.arange(S, dtype=np.float32)
    diff = i[None, :] - i[:, None]
    decay = np.where(diff >= 0, np.float32(0.99) ** np.maximum(diff, 0), 0).astype(np.float32) / np.sqrt(np.float32(D))
    mask = np.zeros((128, SCOLS), np.float32)
    cum = np.zeros((128, 3, S), np.float32)
    for t in range(3):
        o, r = t * 128, TL[t]
        mask[:r, SOFF[t]:SOFF[t] + S - o] = decay[o:o + r, o:]
        cum[:r, t, :] = diff[o:o + r, :] >= 0
    p = np.arange(128, dtype=np.float32)
    return {
        "c_mask": mask,
        "c_cum": cum,
        "c_up": (p[:, None] < p[None, :]).astype(np.float32),
        "c_ident": np.eye(128, dtype=np.float32),
        "c_slot": np.arange(CAP, dtype=np.float32).reshape(2, CH).T,
        "c_iota": np.tile(np.arange(E, dtype=np.float32), (128, 1)),
        "c_ecol": p[:, None].copy(),
    }


def kernel(**inputs):
    import numpy as np
    import concourse.bacc as bacc
    from concourse.bass_utils import run_bass_kernel_spmd

    a = {k: np.asarray(v) for k, v in inputs.items()}
    g, ps = 14, 16
    xp = a["x"].reshape(B, 3, g, ps, g, ps).transpose(0, 1, 3, 5, 2, 4).reshape(B, KC, 128, NPATCH).transpose(0, 2, 1, 3)
    arrays = {
        "xp": xp,
        "txt": a["txt"],
        "wtok": a["L0_tok_W"].T.reshape(KC, 128, D).transpose(1, 0, 2),
        "btok": a["L0_tok_b"].reshape(1, D),
        "cls": a["L0_tok_class_token"],
        "pos": a["L0_tok_pos_embed"],
        "wqkv": a["L0_attn_W_qkv"],
        "bqk": a["L0_attn_b_qkv"][:2 * D].reshape(4, 96).T,
        "bv": a["L0_attn_b_qkv"][2 * D:].reshape(1, D),
        "wg": a["L0_ffn_Wg"].T,
        "ebias": a["L0_ffn_e_bias"].reshape(1, E),
        "wgu": a["L0_ffn_W_gate_up"],
        "wdn": a["L0_ffn_W_down"],
        "wsg": a["L0_ffn_Wsg"],
        "wsu": a["L0_ffn_Wsu"],
        "wsd": a["L0_ffn_Wsd"],
        **constants(),
    }
    arrays = {k: np.ascontiguousarray(v) for k, v in arrays.items()}
    nc = bacc.Bacc("TRN2", target_bir_lowering=False, num_devices=1)
    args = [nc.dram_tensor(k, v.shape, F32, kind="ExternalInput").ap() for k, v in arrays.items()]
    out = nc.dram_tensor("result", (T, D), F32, kind="ExternalOutput").ap()
    build(nc, *args, out)
    r = run_bass_kernel_spmd(nc, [arrays], core_ids=[0])
    return r.results[0]["result"].reshape(B, S, D)
```

```python
from contextlib import ExitStack

import concourse.bass as bass
from concourse import mybir

F32 = mybir.dt.float32
F32R = mybir.dt.float32r
BF16 = mybir.dt.bfloat16
I32 = mybir.dt.int32
ALU = mybir.AluOpType
ACT = mybir.ActivationFunctionType

B = 16
NPATCH = 196
DIN = 768
KC = DIN // 128
D = 192
DA = 128
DB = D - DA
TXT = 128
IMG = NPATCH + 1
S = IMG + TXT
SP = S + 1
T = B * S
TL = [128, 128, S - 256]
E = 128
K = 6
I = 464
IS = 928
CAP = 192
CH = CAP // 2
F = 116
EM = I // F
SM = IS // F
YW = D + E
LIST = E + 8
CHUNK = 512
NCHUNK = T // CHUNK
TAIL = T - NCHUNK * CHUNK
SOFF = [0, S, S + (S - 128)]
SCOLS = S + (S - 128) + (S - 256)
EPS = 1e-5
SCALE = 2.5
ABOVE = 200.0
LOW = -3.0e38
ROUTED = -3.3e38


def wait(eng, sem, value):
    if isinstance(value, int) and value <= 0:
        return
    eng.wait_ge(sem, value)


def wait_apart(eng, passed, *waits):
    for sem, v in waits:
        if not isinstance(v, int) or v > 0:
            eng.wait_ge(sem, v)
            eng.sem_inc(passed, 1)


def by_turns(n):
    return bass.ds((n % 2) * 3, 3)


def build(nc, xp, txt, wtok, btok, cls, pos, wqkv, bqk, bv, wg, ebias, wgu, wdn, wsg, wsu, wsd,
          c_mask, c_cum, c_up, c_ident, c_slot, c_iota, c_ecol, c_rest, c_rest_col, out):
    yw = nc.dram_tensor("yw_rows", (T + CAP, YW), F32, kind="Internal").ap()
    acc = nc.dram_tensor("acc_rows", (T + CAP, D), F32, kind="Internal").ap()
    crow = nc.dram_tensor("count_rows", (E, B, SP), BF16, kind="Internal").ap()

    with ExitStack() as top:
        def keep(name, shape, dt=F32):
            return top.enter_context(nc.sbuf_tensor(name, shape, dt))

        psum = [top.enter_context(nc.psum_tensor(f"bank{i}", [128, 512], F32)) for i in range(8)]

        all_hiA = keep("all_hiA", [128, T], F32R)
        all_loA = keep("all_loA", [128, T], F32R)
        all_B = keep("all_B", [128, T], F32R)
        ident = keep("ident", [128, 128])
        ones = keep("ones", [128, 128])
        slot = keep("slot", [CH, 2])
        rest = keep("rest", [CH, 2])
        iota = keep("iota", [128, E])
        ecol = keep("ecol", [128, 1])
        up_strict = keep("up_strict", [128, 128])
        images_full = keep("images_full", [CH, 2, E])
        countT = keep("countT", [E, SP], BF16)

        block_a(nc, psum, all_hiA, all_loA, all_B, ident, ones, slot, rest, iota, ecol, up_strict, images_full, countT,
                yw, acc, crow, xp, txt, wtok, btok, cls, pos, wqkv, bqk, bv, wg, ebias,
                c_mask, c_cum, c_up, c_ident, c_slot, c_iota, c_ecol, c_rest_col)
        s_hi = keep("s_hi", [128, 2, 2 * IS], F32R)
        s_lo = keep("s_lo", [128, 2, 2 * IS], F32R)
        s_dn = keep("s_dn", [F, SM, 2 * D], F32R)
        block_b(nc, psum, ident, ones, rest, iota, ecol, up_strict, images_full, countT, yw, acc, crow, wgu, wdn,
                wsg, wsu, wsd, s_hi, s_lo, s_dn, c_rest)
        block_c(nc, psum, all_hiA, all_loA, all_B, acc, s_hi, s_lo, s_dn, out)


def block_a(nc, psum, all_hiA, all_loA, all_B, ident, ones, slot, rest, iota, ecol, up_strict, images_full, countT,
            yw, acc, crow, xp, txt, wtok, btok, cls, pos, wqkv, bqk, bv, wg, ebias,
            c_mask, c_cum, c_up, c_ident, c_slot, c_iota, c_ecol, c_rest_col):
    with ExitStack() as ctx:
        def sb(name, shape, dt=F32):
            return ctx.enter_context(nc.sbuf_tensor(name, shape, dt))

        def sem(name):
            return ctx.enter_context(nc.semaphore(name))

        patches = sb("patches", [128, KC, 256])
        w_tok = sb("w_tok", [128, KC, D])
        addend = sb("addend", [128, 2, D])
        pos_sb = sb("pos_sb", [128, 2, D])
        txt2 = sb("txt2", [128, D])
        raw_qkv = sb("raw_qkv", [128, 2, 3 * D])
        qkv_hi = sb("qkv_hi", [128, 2, 3 * D], F32R)
        qkv_lo = sb("qkv_lo", [128, 2, 3 * D], F32R)
        raw_g = sb("raw_g", [128, 2, E])
        g_hi = sb("g_hi", [128, 2, E], F32R)
        g_lo = sb("g_lo", [128, 2, E], F32R)
        b_qk = sb("b_qk", [96, 4])
        b_v = sb("b_v", [128, D])
        e_bias = sb("e_bias", [128, E])
        mask = sb("mask", [128, SCOLS])
        cum32 = sb("cum32", [128, 3, SP])
        cum = sb("cum", [128, 3, SP], BF16)
        ones_b = sb("ones_b", [128, SP], BF16)
        above = sb("above", [128, 1])
        zero = sb("zero", [CH, 2, YW])
        half_neg = sb("half_neg", [128, 3])
        h0 = sb("h0", [128, 6, D])
        h1 = sb("h1", [128, 3, D])
        q_k = sb("q_k", [96, 4, S])
        v_sb = sb("v_sb", [128, 3, D])
        scores = sb("scores", [128, SCOLS])
        sig = sb("sig", [128, 3, E])
        choice = sb("choice", [128, 3, E + 2])
        best = sb("best", [128, 3, 8])
        left = sb("left", [128, 3, E + 2])
        chosen = sb("chosen", [128, 3, E], BF16)
        w_raw = sb("w_raw", [128, 3, E])
        w_sum = sb("w_sum", [128, 3])
        w_sum2 = sb("w_sum2", [128, 3])
        w_inv = sb("w_inv", [128, 3])
        chosen_all = sb("chosen_all", [128, E], BF16)
        y1 = sb("y1", [128, 3, D])
        y2 = sb("y2", [128, 3, YW])
        norm = []
        for i, y in ((1, y1), (2, y2)):
            norm.append(dict(
                y=y, stats=sb(f"stats{i}", [128, 3, 6]), mv=sb(f"mv{i}", [128, 3, 2]), ve=sb(f"ve{i}", [128, 3]),
                rstd=sb(f"rstd{i}", [128, 3]), hiA=sb(f"y{i}_hiA", [128, SP], F32R),
                loA=sb(f"y{i}_loA", [128, SP], F32R), st=sb(f"y{i}_B", [128, SP], F32R),
                s_stats=sem(f"stats{i}_done"), s_mv=sem(f"mv{i}_ready"), s_ve=sem(f"ve{i}_ready"),
                s_rstd=sem(f"rstd{i}_ready"), s_y=sem(f"y{i}_ready"), s_T=sem(f"y{i}T_in_psum"),
                s_hi=sem(f"y{i}T_hi_ready"), s_lo=sem(f"y{i}T_split"), bankA=psum[5 if i == 1 else 3],
                bankB=psum[6 if i == 1 else 4]))
        n1, n2 = norm
        tok_ps, pv_ps, pv2_ps, lg_ps, ct_ps = psum[0], psum[1], psum[2], psum[3], psum[4]
        qk_ps = [psum[7], psum[5], psum[6], psum[0]]
        sc_ps = [psum[7], psum[5], psum[6]]

        passed = sem("passed_a")
        const_in = sem("const_in")
        base_in = sem("base_in")
        base_set = sem("base_set")
        set_up = sem("set_up")
        set_up_act = sem("set_up_act")
        pool_set = sem("pool_set")
        lo_set = sem("lo_set")
        x_in = sem("x_in")
        t1_in = sem("t1_in")
        t2_in = sem("t2_in")
        tok_mm = sem("tok_mm")
        h0_ready = sem("h0_ready")
        h0_txt = sem("h0_txt")
        qk_mm = sem("qk_mm")
        v_mm = sem("v_mm")
        qk_ready = sem("qk_ready")
        v_ready = sem("v_ready")
        sc_mm = sem("sc_mm")
        sc_ready = sem("sc_ready")
        pv_mm = sem("pv_mm")
        h1_ready = sem("h1_ready")
        lg_mm = sem("lg_mm")
        sig_ready = sem("sig_ready")
        choice_ready = sem("choice_ready")
        best_ready = sem("best_ready")
        best6_ready = sem("best6_ready")
        left_ready = sem("left_ready")
        chosen_ready = sem("chosen_ready")
        wraw_ready = sem("wraw_ready")
        wsum_ready = sem("wsum_ready")
        winv_ready = sem("winv_ready")
        w_ready = sem("w_ready")
        all_added = sem("all_added")
        ct_mm = sem("ct_mm")
        ce_mm = sem("ce_mm")
        ct_ready = sem("ct_ready")
        full_ready = sem("full_ready")
        h1_out = sem("h1_out")
        big_out = sem("big_out")
        yw_out = sem("yw_out")
        ct_out = sem("ct_out")
        pad_out = sem("pad_out")
        N_CONST = 18

        with nc.Block() as block:
            @block.sync
            def _(sp):
                sp.dma_start(pos_sb[:, 0, :], pos[0:128, :]).then_inc(base_in, 16)
                sp.dma_start(pos_sb[0:IMG - 128, 1, :], pos[128:IMG, :]).then_inc(base_in, 16)
                sp.dma_start(addend[0:1, 0, :], cls).then_inc(base_in, 16)
                sp.dma_start(addend[1:128, 0, :], btok.to_broadcast([127, D])).then_inc(base_in, 16)
                sp.dma_start(addend[0:IMG - 128, 1, :], btok.to_broadcast([IMG - 128, D])).then_inc(base_in, 16)

                def load(n):
                    wait_apart(sp, passed, (tok_mm, n))
                    sp.dma_start(patches[:, :, 1:IMG], xp[n, :, :, :]).then_inc(x_in, 16)
                    wait_apart(sp, passed, (h0_ready, n))
                    sp.dma_start(addend[IMG - 128:128, 1, :], txt[n, 0:256 - IMG, :]).then_inc(t1_in, 16)
                    wait_apart(sp, passed, (h0_txt, n))
                    sp.dma_start(txt2[0:TL[2], :], txt[n, 256 - IMG:TXT, :]).then_inc(t2_in, 16)

                def store_residual(n):
                    wait_apart(sp, passed, (h1_ready, n + 1))
                    rows = acc[bass.ds(n * S, S), :]
                    sp.dma_start(rows[0:256, :].rearrange("(t p) c -> p t c", p=128), h1[:, 0:2, :]).then_inc(h1_out, 16)
                    sp.dma_start(rows[256:S, :], h1[0:TL[2], 2, :]).then_inc(h1_out, 16)

                def store(n):
                    wait_apart(sp, passed, (n2["s_lo"], n + 1))
                    for big, own in ((all_hiA, n2["hiA"]), (all_loA, n2["loA"]), (all_B, n2["st"])):
                        sp.dma_start(big[:, bass.ds(n * S, S)].bitcast(F32), own[:, 0:S].bitcast(F32)).then_inc(big_out, 16)
                    wait_apart(sp, passed, (w_ready, n + 1))
                    rows = yw[bass.ds(n * S, S), :]
                    sp.dma_start(rows[0:256, :].rearrange("(t p) c -> p t c", p=128), y2[:, 0:2, :]).then_inc(yw_out, 16)
                    sp.dma_start(rows[256:S, :], y2[0:TL[2], 2, :]).then_inc(yw_out, 16)
                    wait_apart(sp, passed, (ct_ready, n + 1))
                    sp.dma_start(crow[:, bass.ds(n, 1), :].rearrange("e o t -> e (o t)"), countT[:, :]).then_inc(ct_out, 16)

                sp.dma_start(w_tok[:, :, :], wtok).then_inc(const_in, 16)
                sp.wait_ge(pool_set, 1)
                load(0)
                for half, src in ((0, wqkv[0:DA, :]), (1, wqkv[DA:D, :])):
                    sp.dma_start(raw_qkv[0:DA if half == 0 else DB, half, :], src).then_inc(const_in, 16)
                sp.dma_start(raw_qkv[DB:128, 1, :], wqkv[DA:D, :]).then_inc(const_in, 16)
                for half, src in ((0, wg[0:DA, :]), (1, wg[DA:D, :])):
                    sp.dma_start(raw_g[0:DA if half == 0 else DB, half, :], src).then_inc(const_in, 16)
                sp.dma_start(raw_g[DB:128, 1, :], wg[DA:D, :]).then_inc(const_in, 16)
                sp.dma_start(ident[:, :], c_ident).then_inc(const_in, 16)
                sp.dma_start(b_qk[:, :], bqk).then_inc(const_in, 16)
                sp.dma_start(b_v[:, :], bv.to_broadcast([128, D])).then_inc(const_in, 16)
                sp.dma_start(mask[:, :], c_mask).then_inc(const_in, 16)
                sp.dma_start(e_bias[:, :], ebias.to_broadcast([128, E])).then_inc(const_in, 16)
                sp.dma_start(cum32[:, :, :], c_cum).then_inc(const_in, 16)
                sp.dma_start(up_strict[:, :], c_up).then_inc(const_in, 16)
                sp.dma_start(slot[:, :], c_slot).then_inc(const_in, 16)
                sp.dma_start(rest[:, :], c_rest_col).then_inc(const_in, 16)
                sp.dma_start(iota[:, :], c_iota).then_inc(const_in, 16)
                sp.dma_start(ecol[:, :], c_ecol).then_inc(const_in, 16)
                load(1)
                sp.dma_start(yw[T:T + CAP, :].rearrange("(h p) c -> p h c", p=CH), zero[:, :, :]).then_inc(pad_out, 16)
                load(2)
                with sp.Fori(0, B - 3) as i:
                    store_residual(i)
                    load(i + 3)
                    store(i)
                for n in range(B - 3, B):
                    store_residual(n)
                    store(n)
                sp.wait_ge(h1_out, 32 * B)
                sp.wait_ge(big_out, 48 * B)
                sp.wait_ge(yw_out, 32 * B)
                sp.wait_ge(ct_out, 16 * B)
                sp.wait_ge(pad_out, 16)

            def rstd_pool(pool, c, n):
                wait_apart(pool, passed, (c["s_mv"], n + 1))
                pool.tensor_scalar(c["ve"][:, :], c["mv"][:, :, 1], EPS, None, ALU.add).then_inc(c["s_ve"], 1)
                pool.wait_ge(c["s_ve"], n + 1)
                wait(pool, c["s_y"], n)
                pool.tensor_tensor(c["rstd"][:, :], c["ve"][:, :], half_neg[:, :], ALU.pow).then_inc(c["s_rstd"], 1)

            @block.gpsimd
            def _(pool):
                pool.memset(patches[:, :, :], 0.0)
                pool.memset(zero[:, :, :], 0.0).then_inc(pool_set, 1)
                pool.memset(half_neg[:, :], -0.5)
                pool.memset(above[:, :], ABOVE)
                pool.memset(images_full[:, :, :], 0.0)
                pool.memset(ones_b[:, :], 1.0)
                pool.memset(ones[:, :], 1.0)
                pool.memset(chosen_all[:, :], 0.0)
                pool.memset(choice[:, :, :], LOW)
                pool.memset(w_sum[:, :], 1.0)
                for c in norm:
                    pool.memset(c["mv"][:, :, :], 1.0)
                    for name in ("hiA", "loA", "st"):
                        pool.memset(c[name][:, :].bitcast(F32), 0.0)
                pool.memset(w_inv[:, :], 0.0).then_inc(pool_set, 1)
                pool.wait_ge(pool_set, 2)

                def text_rows(n):
                    wait_apart(pool, passed, (h1_ready, n - 1), (t2_in, 16 * n + 16))
                    pool.tensor_copy(h0[0:TL[2], bass.ds((n % 2) * 3 + 2, 1), :].rearrange("p o c -> p (o c)"),
                                     txt2[0:TL[2], :]).then_inc(h0_txt, 1)

                def count_chosen(n):
                    pool.wait_ge(chosen_ready, n + 1)
                    pool.wait_ge(ce_mm, n + 1)
                    for t in range(3):
                        wait(pool, all_added, 3 * n + t)
                        pool.tensor_tensor(chosen_all[0:TL[t], :], chosen_all[0:TL[t], :], chosen[0:TL[t], t, :],
                                           ALU.add).then_inc(all_added, 1)

                def step(n):
                    rstd_pool(pool, n2, n)
                    if not isinstance(n, int) or n < B - 2:
                        text_rows(n + 2)
                        rstd_pool(pool, n1, n + 2)
                    count_chosen(n)

                for n in range(2):
                    text_rows(n)
                    rstd_pool(pool, n1, n)
                step(0)
                with pool.Fori(1, B - 2) as i:
                    step(i)
                step(B - 2)
                step(B - 1)

            @block.scalar
            def _(act):
                act.wait_ge(const_in, 16 * N_CONST)
                act.activation(qkv_hi[:, :, :], raw_qkv[:, :, :], ACT.Copy).then_inc(set_up_act, 1)
                act.activation(g_hi[:, :, :], raw_g[:, :, :], ACT.Copy).then_inc(set_up_act, 1)
                act.wait_ge(pool_set, 2)

                def split_hi(c, n, used, per):
                    act.wait_ge(c["s_T"], n + 1)
                    wait(act, used, n * per)
                    if c is n2:
                        wait(act, big_out, 48 * n)
                    act.activation(c["hiA"][:, 0:S], c["bankA"][:, 0:S], ACT.Copy)
                    act.activation(c["st"][0:DB, 0:S], c["bankB"][0:DB, 0:S], ACT.Copy).then_inc(c["s_hi"], 1)

                def qk_evac(n):
                    wait(act, sc_mm, 3 * n)
                    for m in range(4):
                        act.wait_ge(qk_mm, 4 * n + m + 1)
                        act.activation(q_k[:, m, :], qk_ps[m][0:96, 0:S], ACT.Identity,
                                       bias=b_qk[:, m:m + 1]).then_inc(qk_ready, 1)

                def sigmoid(n):
                    act.wait_ge(lg_mm, n + 1)
                    wait(act, wraw_ready, 3 * n)
                    act.activation(sig[:, 0:2, :], lg_ps[:, 0:2 * E].rearrange("p (t e) -> p t e", t=2), ACT.Sigmoid)
                    act.activation(sig[0:TL[2], 2, :], lg_ps[0:TL[2], 2 * E:3 * E], ACT.Sigmoid).then_inc(sig_ready, 1)

                def counts(n):
                    act.wait_ge(ct_mm, n + 1)
                    wait(act, ct_out, 16 * n)
                    act.activation(countT[:, :], ct_ps[:, 0:SP], ACT.Relu, bias=above[:, :], scale=-1.0).then_inc(ct_ready, 1)

                def step(n):
                    more = not isinstance(n, int) or n < B - 1
                    split_hi(n2, n, lg_mm, 1)
                    if more:
                        split_hi(n1, n + 1, v_mm, 1)
                    sigmoid(n)
                    if more:
                        qk_evac(n + 1)
                    counts(n)

                split_hi(n1, 0, v_mm, 1)
                qk_evac(0)
                step(0)
                with act.Fori(1, B - 2) as i:
                    step(i)
                step(B - 2)
                step(B - 1)

            @block.tensor
            def _(pe):
                def split_product(ps, a, w_hi, w_lo, stationary):
                    hiA, loA, st = a
                    passes = ((hiA, w_hi[0]), (hiA, w_lo[0]), (loA, w_hi[0]), (st, w_hi[1]), (st, w_lo[1]))
                    for i, (x, w) in enumerate(passes):
                        mm = pe.matmul(ps, x if stationary else w, w if stationary else x, start=i == 0, stop=i == 4)
                    return mm

                def tokens(n):
                    pe.wait_ge(x_in, 16 * n + 16)
                    wait(pe, qk_ready, 4 * (n - 1))
                    wait(pe, h0_ready, n)
                    for t in range(2):
                        for c in range(KC):
                            mm = pe.matmul(tok_ps[:, t * D:(t + 1) * D], patches[:, c, t * 128:(t + 1) * 128],
                                           w_tok[:, c, :], start=c == 0, stop=c == KC - 1)
                    mm.then_inc(tok_mm, 1)

                def turn(c, n):
                    pe.wait_ge(c["s_y"], n + 1)
                    if c is n1:
                        wait(pe, sc_ready, 3 * n)
                    else:
                        wait(pe, full_ready, n)
                        wait(pe, ct_ready, n)
                    for t in range(3):
                        r, o = TL[t], t * 128
                        pe.transpose(c["bankA"][:, o:o + r], c["y"][0:r, t, 0:DA], ident[0:r, 0:r])
                    for t in range(3):
                        r, o = TL[t], t * 128
                        mm = pe.transpose(c["bankB"][0:DB, o:o + r], c["y"][0:r, t, DA:D], ident[0:r, 0:r])
                    mm.then_inc(c["s_T"], 1)

                def qkv(n):
                    pe.wait_ge(n1["s_lo"], n + 1)
                    wait(pe, sc_ready, 3 * n)
                    pe.wait_ge(h0_ready, n + 2 if not isinstance(n, int) or n < B - 1 else B)
                    data = (n1["hiA"][:, :], n1["loA"][:, :], n1["st"][:, :])
                    for m in range(4):
                        cols = slice(m * 96, (m + 1) * 96)
                        split_product(qk_ps[m][0:96, 0:SP], data, [qkv_hi[:, h, cols] for h in range(2)],
                                      [qkv_lo[:, h, cols] for h in range(2)], False).then_inc(qk_mm, 1)
                    wait(pe, h1_ready, n)
                    for t in range(3):
                        r, o = TL[t], t * 128
                        data = (n1["hiA"][:, o:o + r], n1["loA"][:, o:o + r], n1["st"][:, o:o + r])
                        ps = pv_ps[0:r, t * D:(t + 1) * D] if t < 2 else pv2_ps[0:r, 0:D]
                        mm = split_product(ps, data, [qkv_hi[:, h, 2 * D:] for h in range(2)],
                                           [qkv_lo[:, h, 2 * D:] for h in range(2)], True)
                    mm.then_inc(v_mm, 1)

                def score(n):
                    pe.wait_ge(qk_ready, 4 * n + 4)
                    for t in range(3):
                        r, o = TL[t], t * 128
                        for h in range(2):
                            mm = pe.matmul(sc_ps[t][0:r, 0:S - o], q_k[:, 2 + h, o:o + r], q_k[:, h, o:S],
                                           start=h == 0, stop=h == 1)
                        mm.then_inc(sc_mm, 1)

                def attend(n):
                    pe.wait_ge(sc_ready, 3 * n + 3)
                    pe.wait_ge(v_ready, n + 1)
                    for q in range(3):
                        r = TL[q]
                        ps = pv_ps[0:r, q * D:(q + 1) * D] if q < 2 else pv2_ps[0:r, 0:D]
                        for t in range(q + 1):
                            c = SOFF[t] + (q - t) * 128
                            mm = pe.matmul(ps, scores[0:TL[t], c:c + r], v_sb[0:TL[t], t, :], start=t == 0, stop=t == q)
                    mm.then_inc(pv_mm, 1)

                def logits(n):
                    pe.wait_ge(n2["s_lo"], n + 1)
                    for t in range(3):
                        r, o = TL[t], t * 128
                        data = (n2["hiA"][:, o:o + r], n2["loA"][:, o:o + r], n2["st"][:, o:o + r])
                        mm = split_product(lg_ps[0:r, t * E:(t + 1) * E], data, [g_hi[:, h, :] for h in range(2)],
                                           [g_lo[:, h, :] for h in range(2)], True)
                    mm.then_inc(lg_mm, 1)

                def running_counts(n):
                    pe.wait_ge(chosen_ready, n + 1)
                    wait(pe, all_added, 3 * n)
                    for t in range(3):
                        pe.matmul(ct_ps[:, 0:SP], chosen[0:TL[t], t, :], cum[0:TL[t], t, :], start=t == 0, stop=False)
                    pe.matmul(ct_ps[:, 0:SP], chosen_all[:, :], ones_b[:, :], start=False, stop=True).then_inc(ct_mm, 1)
                    for t in range(3):
                        pe.matmul(lg_ps[:, 0:E], ones_b[0:TL[t], 0:128], chosen[0:TL[t], t, :], start=t == 0, stop=False)
                    pe.matmul(lg_ps[:, 0:E], ones_b[:, 0:128], chosen_all[:, :], start=False, stop=True).then_inc(ce_mm, 1)

                pe.wait_ge(const_in, 16 * N_CONST)
                def step(n):
                    more = not isinstance(n, int) or n < B - 1
                    attend(n)
                    if not isinstance(n, int) or n < B - 2:
                        tokens(n + 2)
                    turn(n2, n)
                    if more:
                        turn(n1, n + 1)
                    logits(n)
                    if more:
                        qkv(n + 1)
                        score(n + 1)
                    running_counts(n)

                tokens(0)
                turn(n1, 0)
                tokens(1)
                pe.wait_ge(lo_set, 3)
                qkv(0)
                score(0)
                step(0)
                with pe.Fori(1, B - 2) as i:
                    step(i)
                step(B - 2)
                step(B - 1)

            @block.vector
            def _(dve):
                dve.wait_ge(base_in, 16 * 5)
                dve.tensor_tensor(addend[:, 0, :], addend[:, 0, :], pos_sb[:, 0, :], ALU.add)
                dve.tensor_tensor(addend[0:IMG - 128, 1, :], addend[0:IMG - 128, 1, :], pos_sb[0:IMG - 128, 1, :],
                                  ALU.add).then_inc(base_set, 1)
                dve.wait_ge(base_set, 1)
                dve.wait_ge(pool_set, 2)

                def stats(c, h, n):
                    for t in range(3):
                        ins = dve.bn_stats(c["stats"][0:TL[t], t, :], h[0:TL[t], t, :])
                    ins.then_inc(c["s_stats"], 1)
                    wait_apart(dve, passed, (c["s_stats"], n + 1))
                    for t in range(3):
                        ins = dve.bn_aggr(c["mv"][0:TL[t], t, :], c["stats"][0:TL[t], t, :])
                    ins.then_inc(c["s_mv"], 1)

                def normed(c, h, n):
                    dve.wait_ge(c["s_rstd"], n + 1)
                    wait(dve, c["s_T"], n)
                    if c is n2:
                        wait(dve, yw_out, 32 * n)
                    for t in range(3):
                        r = TL[t]
                        ins = dve.tensor_scalar(c["y"][0:r, t, 0:D], h[0:r, t, :], c["mv"][0:r, t, 0:1],
                                                c["rstd"][0:r, t:t + 1], ALU.subtract, ALU.mult)
                    ins.then_inc(c["s_y"], 1)

                def split_lo(c, n):
                    dve.wait_ge(c["s_hi"], n + 1)
                    dve.tensor_tensor(c["loA"][:, 0:S], c["bankA"][:, 0:S], c["hiA"][:, 0:S].bitcast(F32), ALU.subtract)
                    dve.tensor_tensor(c["st"][DB:128, 0:S], c["bankB"][0:DB, 0:S], c["st"][0:DB, 0:S].bitcast(F32),
                                      ALU.subtract).then_inc(c["s_lo"], 1)

                def token_rows(n):
                    dve.wait_ge(tok_mm, n + 1)
                    dve.wait_ge(t1_in, 16 * n + 16)
                    dve.tensor_tensor(h0[:, bass.ds((n % 2) * 3, 2), :], tok_ps[:, 0:2 * D].rearrange("p (t c) -> p t c", t=2),
                                      addend[:, :, :], ALU.add).then_inc(h0_ready, 1)
                    wait_apart(dve, passed, (h0_ready, n + 1), (h0_txt, n + 1))
                    stats(n1, h0[:, by_turns(n), :], n)

                def residual(n):
                    dve.wait_ge(pv_mm, n + 1)
                    wait(dve, h1_out, 32 * n)
                    dve.tensor_tensor(h1[:, 0:2, :], pv_ps[:, 0:2 * D].rearrange("p (t c) -> p t c", t=2),
                                      h0[:, bass.ds((n % 2) * 3, 2), :], ALU.add)
                    dve.tensor_tensor(h1[0:TL[2], 2, :], pv2_ps[0:TL[2], 0:D],
                                      h0[0:TL[2], bass.ds((n % 2) * 3 + 2, 1), :].rearrange("p o c -> p (o c)"),
                                      ALU.add).then_inc(h1_ready, 1)
                    dve.wait_ge(h1_ready, n + 1)
                    stats(n2, h1, n)

                def values(n):
                    dve.wait_ge(v_mm, n + 1)
                    for t in range(3):
                        r = TL[t]
                        ps = pv_ps[0:r, t * D:(t + 1) * D] if t < 2 else pv2_ps[0:r, 0:D]
                        ins = dve.tensor_tensor(v_sb[0:r, t, :], ps, b_v[0:r, :], ALU.add)
                    ins.then_inc(v_ready, 1)

                def decay(n):
                    for t in range(3):
                        r, w = TL[t], S - t * 128
                        dve.wait_ge(sc_mm, 3 * n + t + 1)
                        dve.tensor_tensor(scores[0:r, SOFF[t]:SOFF[t] + w], sc_ps[t][0:r, 0:w],
                                          mask[0:r, SOFF[t]:SOFF[t] + w], ALU.mult).then_inc(sc_ready, 1)

                def route(n):
                    dve.wait_ge(sig_ready, n + 1)
                    for t in range(3):
                        r = TL[t]
                        ins = dve.tensor_tensor(choice[0:r, t, 0:E], sig[0:r, t, :], e_bias[0:r, :], ALU.add)
                    ins.then_inc(choice_ready, 1)
                    wait_apart(dve, passed, (choice_ready, n + 1))
                    for t in range(3):
                        r = TL[t]
                        ins = dve.max(best[0:r, t, :], choice[0:r, t, :])
                    ins.then_inc(best_ready, 1)
                    dve.wait_ge(best_ready, n + 1)
                    dve.memset(best[:, :, K:8], LOW).then_inc(best6_ready, 1)
                    wait_apart(dve, passed, (best6_ready, n + 1))
                    for t in range(3):
                        r = TL[t]
                        ins = dve.match_replace(left[0:r, t, :], best[0:r, t, :], choice[0:r, t, :], ROUTED)
                    ins.then_inc(left_ready, 1)
                    dve.wait_ge(left_ready, n + 1)
                    wait(dve, all_added, 3 * n)
                    for t in range(3):
                        r = TL[t]
                        ins = dve.tensor_tensor(chosen[0:r, t, :], left[0:r, t, 0:E], choice[0:r, t, 0:E], ALU.not_equal)
                    ins.then_inc(chosen_ready, 1)
                    dve.wait_ge(chosen_ready, n + 1)
                    for t in range(3):
                        r = TL[t]
                        ins = dve.scalar_tensor_tensor(w_raw[0:r, t, :], sig[0:r, t, :], 1.0, chosen[0:r, t, :],
                                                       ALU.mult, ALU.mult, accum_out=w_sum[0:r, t:t + 1])
                        ins.then_inc(wraw_ready, 1)
                    dve.wait_ge(wraw_ready, 3 * n + 3)
                    dve.tensor_scalar(w_sum2[:, :], w_sum[:, :], 1e-20, None, ALU.add).then_inc(wsum_ready, 1)
                    dve.wait_ge(wsum_ready, n + 1)
                    dve.reciprocal(w_inv[:, :], w_sum2[:, :]).then_inc(winv_ready, 1)
                    dve.wait_ge(winv_ready, n + 1)
                    for t in range(3):
                        r = TL[t]
                        ins = dve.tensor_scalar(y2[0:r, t, D:YW], w_raw[0:r, t, :], w_inv[0:r, t:t + 1], SCALE,
                                                ALU.mult, ALU.mult)
                    ins.then_inc(w_ready, 1)

                def count_full(n):
                    dve.wait_ge(ce_mm, n + 1)
                    for h in range(2):
                        ins = dve.scalar_tensor_tensor(images_full[:, h, :], lg_ps[0:CH, 0:E], slot[:, h:h + 1],
                                                       images_full[:, h, :], ALU.is_le, ALU.add)
                    ins.then_inc(full_ready, 1)

                def step(n):
                    ahead = not isinstance(n, int) or n < B - 2
                    more = not isinstance(n, int) or n < B - 1
                    residual(n)
                    normed(n2, h1, n)
                    if ahead:
                        token_rows(n + 2)
                    split_lo(n2, n)
                    if more:
                        split_lo(n1, n + 1)
                    if ahead:
                        normed(n1, h0[:, by_turns(n + 2), :], n + 2)
                    route(n)
                    if more:
                        values(n + 1)
                        decay(n + 1)
                    count_full(n)

                token_rows(0)
                normed(n1, h0[:, by_turns(0), :], 0)
                dve.wait_ge(const_in, 16 * N_CONST)
                dve.wait_ge(set_up_act, 2)
                dve.tensor_tensor(qkv_lo[:, :, :], raw_qkv[:, :, :], qkv_hi[:, :, :].bitcast(F32),
                                  ALU.subtract).then_inc(lo_set, 1)
                dve.tensor_tensor(g_lo[:, :, :], raw_g[:, :, :], g_hi[:, :, :].bitcast(F32),
                                  ALU.subtract).then_inc(lo_set, 1)
                dve.tensor_copy(cum[:, :, :], cum32[:, :, :]).then_inc(lo_set, 1)
                split_lo(n1, 0)
                token_rows(1)
                normed(n1, h0[:, by_turns(1), :], 1)
                values(0)
                decay(0)
                step(0)
                with dve.Fori(1, B - 2) as i:
                    step(i)
                step(B - 2)
                step(B - 1)


def block_b(nc, psum, ident, ones, rest, iota, ecol, up_strict, images_full, countT, yw, acc, crow, wgu, wdn,
            wsg, wsu, wsd, s_hi, s_lo, s_dn, c_rest):
    with ExitStack() as ctx:
        def sb(name, shape, dt=F32):
            return ctx.enter_context(nc.sbuf_tensor(name, shape, dt))

        def sem(name):
            return ctx.enter_context(nc.semaphore(name))

        active = sb("active", [128, 1])
        rank = sb("rank", [128, 2])
        idle_a = sb("idle_a", [128, 1])
        idle = sb("idle", [128, 1])
        diff = sb("diff", [128, 1])
        place = sb("place", [128, 1])
        pick = sb("pick", [128, E])
        order = sb("order", [1, LIST], I32)
        n_active = sb("n_active", [1, 1], I32)
        tok_base = sb("tok_base", [CH, 2, E])
        rest_row = sb("rest_row", [B, CAP])
        counts = [sb(f"counts{p}", [B, SP], BF16) for p in range(2)]
        reach = sb("reach", [B, CAP])
        image = sb("image", [B, CAP], BF16)
        le = sb("le", [CH, 2, S])
        before = sb("before", [CH, 2])
        tok = sb("tok", [CH, 2])
        past = sb("past", [CH, 2])
        slot_no = sb("slot_no", [CH, 2])
        slot_tok = sb("slot_tok", [CH, LIST, 2], I32)
        get_idx = sb("get_idx", [CH, 2], I32)
        put_idx = sb("put_idx", [CH, 2], I32)
        x_rows = [sb(f"x_rows{p}", [CH, 2, YW]) for p in range(2)]
        w_slot = [sb(f"w_slot{p}", [CH, 2]) for p in range(2)]
        x_hiA = sb("x_hiA", [128, CAP], F32R)
        x_loA = sb("x_loA", [128, CAP], F32R)
        x_st = sb("x_st", [128, CAP], F32R)
        raw_gu = [sb(f"raw_gu{p}", [128, 2, 2 * I]) for p in range(2)]
        down_w = [sb(f"down_w{p}", [F, EM, D]) for p in range(2)]
        gu_hi = [sb(f"gu_hi{p}", [128, 2, 2 * I], F32R) for p in range(2)]
        gu_lo = [sb(f"gu_lo{p}", [128, 2, 2 * I], F32R) for p in range(2)]
        gate = sb("gate", [F, EM, CAP])
        inter = sb("inter", [F, EM, CAP])
        y_rows = sb("y_rows", [CH, 2, D])
        raw_s = sb("raw_s", [128, 2 * IS])
        raw_sd = sb("raw_sd", [F, SM, D])
        gu_ps = psum[0:4]
        xT_ps, dn_ps, cnt_ps = psum[4], psum[5], psum[6:8]

        passed = sem("passed_b")
        set_dve = sem("set_dve")
        set_pe = sem("set_pe")
        order_ready = sem("order_ready")
        rest_in = sem("rest_in")
        cr_in = [sem(f"cr_in{p}") for p in range(2)]
        reach_ready = sem("reach_ready")
        image_ready = sem("image_ready")
        cnt_mm = sem("cnt_mm")
        before_ready = sem("before_ready")
        tok_ready = sem("tok_ready")
        past_ready = sem("past_ready")
        idx_ready = sem("idx_ready")
        get_idx_ready = sem("get_idx_ready")
        x_in = [sem(f"x_in{p}") for p in range(2)]
        wslot_ready = sem("wslot_ready")
        xT_mm = sem("xT_mm")
        x_hi = sem("x_hi_ready")
        x_split = sem("x_split")
        raw_in = [sem(f"raw_in{p}") for p in range(2)]
        down_in = [sem(f"down_in{p}") for p in range(2)]
        gu_hi_ready = sem("gu_hi_ready")
        gu_split = sem("gu_split")
        gu_mm = sem("gu_mm")
        gate_ready = sem("gate_ready")
        inter_ready = sem("inter_ready")
        dn_mm = sem("dn_mm")
        y_ready = sem("y_rows_ready")
        put_idx_ready = sem("put_idx_ready")
        added = sem("added")
        zero_rows = sem("zero_rows")
        s_in = sem("s_in")
        s_hi_set = sem("s_hi_set")
        s_lo_set = sem("s_lo_set")

        def load_order(eng, n):
            return eng.value_load(order[0:1, bass.ds(n, 1)], min_val=0, max_val=E - 1)

        def load_active(eng):
            eng.wait_ge(order_ready, 1)
            return eng.value_load(n_active[0:1, 0:1], min_val=K, max_val=E)

        def arrivals(n, p, per):
            return (n - p) * (per // 2) + per

        with nc.Block() as block:
            @block.sync
            def _(sp):
                sp.dma_start(rest_row[:, :], c_rest).then_inc(rest_in, 16)
                for i, w in enumerate((wsg, wsu)):
                    sp.dma_start(raw_s[:, i * IS:(i + 1) * IS], w[0:DA, :]).then_inc(s_in, 16)
                act_n = load_active(sp)

                def load_counts(n, p, first=False):
                    if not first:
                        wait_apart(sp, passed, (cnt_mm, n - 1))
                    e = load_order(sp, n)
                    sp.dma_start(counts[p][:, :], crow[e, :, :]).then_inc(cr_in[p], 16)

                def load(n, p, first=False):
                    if not first:
                        wait_apart(sp, passed, (gu_split, 2 * n - 2))
                    e = load_order(sp, n)
                    sp.dma_start(raw_gu[p][:, 0, :], wgu[e, 0:DA, :]).then_inc(raw_in[p], 16)
                    sp.dma_start(raw_gu[p][0:DB, 1, :], wgu[e, DA:D, :]).then_inc(raw_in[p], 16)
                    sp.dma_start(raw_gu[p][DB:128, 1, :], wgu[e, DA:D, :]).then_inc(raw_in[p], 16)

                def load_down(n, p, first=False):
                    if not first:
                        wait_apart(sp, passed, (dn_mm, n - 1))
                    e = load_order(sp, n)
                    sp.dma_start(down_w[p][:, :, :], wdn[e, :, :].rearrange("(c p) n -> p c n", p=F)).then_inc(down_in[p], 16)

                load_counts(0, 0, True)
                load_counts(1, 1, True)
                load(0, 0, True)
                load_down(0, 0, True)
                load(1, 1, True)
                load_down(1, 1, True)
                sp.wait_ge(s_hi_set, 1)
                sp.wait_ge(s_lo_set, 1)
                for i, w in enumerate((wsg, wsu)):
                    for r in (0, DB):
                        sp.dma_start(raw_s[r:r + DB, i * IS:(i + 1) * IS], w[DA:D, :]).then_inc(s_in, 16)
                sp.dma_start(raw_sd[:, :, :], wsd.rearrange("(c p) n -> p c n", p=F)).then_inc(s_in, 16)
                load_counts(2, 0)
                with sp.Fori(0, act_n, 2) as j:
                    for p in range(2):
                        load_counts(j + p + 3, 1 - p)
                        load(j + p + 2, p)
                        load_down(j + p + 2, p)
                pairs = (act_n + 1) // 2
                wait_apart(sp, passed, *[(x, pairs * m + a) for x, m, a in (
                    (raw_in[0], 48, 48), (raw_in[1], 48, 48), (down_in[0], 16, 16), (down_in[1], 16, 16),
                    (cr_in[0], 16, 32), (cr_in[1], 16, 16))])

            @block.gpsimd
            def _(pool):
                pool.memset(y_rows[:, :, :], 0.0).then_inc(zero_rows, 1)
                pool.wait_ge(zero_rows, 1)
                pool.dma_start(acc[T:T + CAP, :].rearrange("(h p) c -> p h c", p=CH), y_rows[:, :, :]).then_inc(added, 16)
                act_n = load_active(pool)

                def get_tokens(n, p, first=False):
                    waits = [(idx_ready, n + 1)]
                    if not first:
                        waits += [(x_in[1 - p], arrivals(n - 1, 1 - p, 32)), (xT_mm, n - 1), (wslot_ready, n - 1)]
                    elif n == 1:
                        waits += [(x_in[0], 32)]
                    wait_apart(pool, passed, *waits)
                    pool.tensor_copy(get_idx[:, :], slot_tok[:, bass.ds(n, 1), :].rearrange("p o h -> p (o h)")).then_inc(get_idx_ready, 1)
                    wait_apart(pool, passed, (get_idx_ready, n + 1))
                    for h in range(2):
                        pool.indirect_dma_start(x_rows[p][:, h, :], None, yw[:, :],
                                                bass.IndirectOffsetOnAxis(ap=get_idx[:, h:h + 1], axis=0)).then_inc(x_in[p], 16)

                def add_rows(n):
                    wait_apart(pool, passed, (added, n * 32 + 16))
                    pool.tensor_copy(put_idx[:, :], slot_tok[:, bass.ds(n, 1), :].rearrange("p o h -> p (o h)")).then_inc(put_idx_ready, 1)
                    wait_apart(pool, passed, (put_idx_ready, n + 1), (y_ready, n + 2))
                    for h in range(2):
                        pool.indirect_dma_start(acc[:, :], bass.IndirectOffsetOnAxis(ap=put_idx[:, h:h + 1], axis=0),
                                                y_rows[:, h, :], None, compute_op=ALU.add).then_inc(added, 16)

                get_tokens(0, 0, True)
                get_tokens(1, 1, True)
                with pool.Fori(0, act_n, 2) as j:
                    for p in range(2):
                        get_tokens(j + p + 2, p)
                        add_rows(j + p)
                pairs = (act_n + 1) // 2
                wait_apart(pool, passed, (added, pairs * 64 + 16), (x_in[0], pairs * 32 + 32), (x_in[1], pairs * 32 + 32))

            @block.scalar
            def _(act):
                act.wait_ge(s_in, 32)
                act.activation(s_hi[:, 0, :], raw_s[:, :], ACT.Copy).then_inc(s_hi_set, 1)
                act_n = load_active(act)

                def gu_part(n, p, h):
                    if h == 0:
                        act.wait_ge(raw_in[p], arrivals(n, p, 48))
                    act.activation(gu_hi[p][:, h, :], raw_gu[p][:, h, :], ACT.Copy).then_inc(gu_hi_ready, 1)

                def split_x(n):
                    act.wait_ge(xT_mm, n + 1)
                    act.activation(x_hiA[:, :], xT_ps[:, 0:CAP], ACT.Copy)
                    act.activation(x_st[0:DB, :], xT_ps[0:DB, CAP:2 * CAP], ACT.Copy).then_inc(x_hi, 1)

                def silu(n, m):
                    act.wait_ge(gu_mm, 4 * n + m + 1)
                    act.activation(gate[:, m, :], gu_ps[m][0:F, 0:CAP], ACT.Silu).then_inc(gate_ready, 1)

                gu_part(0, 0, 0)
                gu_part(0, 0, 1)
                split_x(0)
                act.wait_ge(s_in, 112)
                act.activation(s_hi[:, 1, :], raw_s[:, :], ACT.Copy).then_inc(s_hi_set, 1)
                act.activation(s_dn[:, :, 0:D], raw_sd[:, :, :], ACT.Copy).then_inc(s_hi_set, 1)
                with act.Fori(0, act_n, 2) as j:
                    for p in range(2):
                        n = j + p
                        gu_part(n + 1, 1 - p, 0)
                        silu(n, 0)
                        silu(n, 1)
                        gu_part(n + 1, 1 - p, 1)
                        silu(n, 2)
                        silu(n, 3)
                        split_x(n + 1)

            @block.tensor
            def _(pe):
                pe.wait_ge(set_dve, 1)
                pe.matmul(cnt_ps[0][:, 0:1], up_strict[:, :], active[:, :], start=True, stop=True)
                pe.matmul(cnt_ps[0][:, 1:2], ones[:, :], active[:, :], start=True, stop=True).then_inc(set_pe, 1)
                pe.wait_ge(set_dve, 7)
                pe.matmul(xT_ps[0:1, 0:E], ecol[:, :], pick[:, :], start=True, stop=True).then_inc(set_pe, 1)
                act_n = load_active(pe)

                def slot_rows(n, p):
                    pe.wait_ge(image_ready, n + 1)
                    for h in range(2):
                        mm = pe.matmul(cnt_ps[h][0:CH, 0:SP], image[:, h * CH:(h + 1) * CH], counts[p][:, :],
                                       start=True, stop=True)
                    mm.then_inc(cnt_mm, 1)

                def turn(n, p):
                    pe.wait_ge(x_in[p], arrivals(n, p, 32))
                    for h in range(2):
                        pe.transpose(xT_ps[:, h * CH:(h + 1) * CH], x_rows[p][:, h, 0:DA], ident[0:CH, 0:CH])
                        mm = pe.transpose(xT_ps[0:DB, CAP + h * CH:CAP + (h + 1) * CH], x_rows[p][:, h, DA:D],
                                          ident[0:CH, 0:CH])
                    mm.then_inc(xT_mm, 1)

                def gate_up(n, p):
                    pe.wait_ge(x_split, n + 1)
                    pe.wait_ge(gu_split, 2 * n + 2)
                    for m in range(EM):
                        for half in range(2):
                            cols = slice(half * I + m * F, half * I + (m + 1) * F)
                            ps = gu_ps[m][0:F, half * CAP:(half + 1) * CAP]
                            passes = ((x_hiA, gu_hi[p][:, 0, cols]), (x_hiA, gu_lo[p][:, 0, cols]),
                                      (x_loA, gu_hi[p][:, 0, cols]), (x_st, gu_hi[p][:, 1, cols]),
                                      (x_st, gu_lo[p][:, 1, cols]))
                            for i, (x, w) in enumerate(passes):
                                mm = pe.matmul(ps, w, x[:, :], start=i == 0, stop=i == 4)
                        mm.then_inc(gu_mm, 1)

                def down(n, p):
                    pe.wait_ge(y_ready, n + 1)
                    pe.wait_ge(down_in[p], arrivals(n, p, 16))
                    for h in range(2):
                        rows = slice(h * CH, (h + 1) * CH)
                        for m in range(EM):
                            if h == 0:
                                pe.wait_ge(inter_ready, 4 * n + m + 1)
                            mm = pe.matmul(dn_ps[0:CH, h * D:(h + 1) * D], inter[:, m, rows], down_w[p][:, m, :],
                                           start=m == 0, stop=m == EM - 1)
                    mm.then_inc(dn_mm, 1)

                slot_rows(0, 0)
                slot_rows(1, 1)
                turn(0, 0)
                with pe.Fori(0, act_n, 2) as j:
                    for p in range(2):
                        n = j + p
                        gate_up(n, p)
                        slot_rows(n + 2, p)
                        turn(n + 1, 1 - p)
                        down(n, p)

            @block.vector
            def _(dve):
                steps = [0]

                def then(ins):
                    steps[0] += 1
                    ins.then_inc(set_dve, 1)
                    dve.wait_ge(set_dve, steps[0])

                then(dve.tensor_scalar(active[:, :], countT[:, SP - 1:SP], ABOVE, None, ALU.is_lt))
                dve.wait_ge(set_pe, 1)
                then(dve.tensor_copy(rank[:, :], cnt_ps[0][:, 0:2]))
                then(dve.tensor_tensor(idle_a[:, :], rank[:, 1:2], ecol[:, :], ALU.add))
                then(dve.tensor_tensor(idle[:, :], idle_a[:, :], rank[:, 0:1], ALU.subtract))
                then(dve.tensor_tensor(diff[:, :], rank[:, 0:1], idle[:, :], ALU.subtract))
                then(dve.scalar_tensor_tensor(place[:, :], diff[:, :], active[:, 0:1], idle[:, :], ALU.mult, ALU.add))
                then(dve.tensor_scalar(pick[:, :], iota[:, :], place[:, 0:1], None, ALU.is_equal))
                dve.tensor_scalar(tok_base[:, :, :], images_full[:, :, :], float(S), None, ALU.mult)
                dve.tensor_scalar(slot_no[:, :], rest[:, :], -1.0, ABOVE, ALU.mult, ALU.add)
                then(dve.memset(order[:, :], 0))
                dve.tensor_copy(n_active[:, :], rank[0:1, 1:2])
                dve.wait_ge(set_pe, 2)
                dve.tensor_copy(order[:, 0:E], xT_ps[0:1, 0:E]).then_inc(order_ready, 1)
                act_n = load_active(dve)

                def slot_images(n, p):
                    dve.wait_ge(cr_in[p], arrivals(n, p, 16))
                    dve.tensor_scalar(reach[:, :], rest_row[:, :], counts[p][:, 0:1], None, ALU.is_le).then_inc(reach_ready, 1)
                    dve.wait_ge(reach_ready, n + 1)
                    dve.scalar_tensor_tensor(image[:, :], rest_row[:, :], counts[p][:, SP - 1:SP], reach[:, :],
                                             ALU.is_gt, ALU.mult).then_inc(image_ready, 1)

                def slots(n):
                    e = load_order(dve, n)
                    wait_apart(dve, passed, (cnt_mm, n + 1))
                    for h in range(2):
                        ins = dve.tensor_scalar(le[:, h, :], cnt_ps[h][0:CH, 1:SP], rest[:, h:h + 1], 0.0, ALU.is_ge, ALU.add,
                                                accum_out=before[:, h:h + 1])
                    ins.then_inc(before_ready, 1)
                    dve.wait_ge(before_ready, n + 1)
                    dve.tensor_tensor(tok[:, :], before[:, :], tok_base[:, :, bass.ds(e, 1)].rearrange("p h o -> p (h o)"),
                                      ALU.add).then_inc(tok_ready, 1)
                    dve.wait_ge(tok_ready, n + 1)
                    dve.scalar_tensor_tensor(past[:, :], tok[:, :], float(T), slot_no[:, :], ALU.is_ge,
                                             ALU.mult).then_inc(past_ready, 1)
                    dve.wait_ge(past_ready, n + 1)
                    dve.tensor_tensor(slot_tok[:, bass.ds(n, 1), :].rearrange("p o h -> p (o h)"), tok[:, :], past[:, :],
                                      ALU.add).then_inc(idx_ready, 1)

                def slot_weights(n, p):
                    e = load_order(dve, n)
                    wait_apart(dve, passed, (x_in[p], arrivals(n, p, 32)))
                    dve.tensor_copy(w_slot[p][:, :], x_rows[p][:, :, bass.ds(e + D, 1)].rearrange("p h o -> p (h o)")).then_inc(wslot_ready, 1)

                def split_x(n):
                    dve.wait_ge(x_hi, n + 1)
                    dve.tensor_tensor(x_loA[:, :], xT_ps[:, 0:CAP], x_hiA[:, :].bitcast(F32), ALU.subtract)
                    dve.tensor_tensor(x_st[DB:128, :], xT_ps[0:DB, CAP:2 * CAP], x_st[0:DB, :].bitcast(F32),
                                      ALU.subtract).then_inc(x_split, 1)

                def gu_low(n, p, h):
                    dve.wait_ge(gu_hi_ready, 2 * n + h + 1)
                    dve.tensor_tensor(gu_lo[p][:, h, :], raw_gu[p][:, h, :], gu_hi[p][:, h, :].bitcast(F32),
                                      ALU.subtract).then_inc(gu_split, 1)

                def gated(n, m):
                    dve.wait_ge(gate_ready, 4 * n + m + 1)
                    dve.tensor_tensor(inter[:, m, :], gate[:, m, :], gu_ps[m][0:F, CAP:2 * CAP],
                                      ALU.mult).then_inc(inter_ready, 1)

                def weigh(n, p):
                    dve.wait_ge(dn_mm, n + 1)
                    dve.wait_ge(added, 32 * n + 16)
                    dve.wait_ge(wslot_ready, n + 1)
                    for h in range(2):
                        ins = dve.tensor_scalar(y_rows[:, h, :], dn_ps[0:CH, h * D:(h + 1) * D], w_slot[p][:, h:h + 1],
                                                None, ALU.mult)
                    ins.then_inc(y_ready, 1)

                dve.sem_inc(y_ready, 1)
                dve.wait_ge(rest_in, 16)
                slot_images(0, 0)
                dve.wait_ge(s_hi_set, 1)
                dve.tensor_tensor(s_lo[:, 0, :], raw_s[:, :], s_hi[:, 0, :].bitcast(F32), ALU.subtract).then_inc(s_lo_set, 1)
                slots(0)
                slot_images(1, 1)
                slots(1)
                gu_low(0, 0, 0)
                gu_low(0, 0, 1)
                split_x(0)
                slot_weights(0, 0)
                dve.wait_ge(s_hi_set, 2)
                dve.tensor_tensor(s_lo[:, 1, :], raw_s[:, :], s_hi[:, 1, :].bitcast(F32), ALU.subtract).then_inc(s_lo_set, 1)
                dve.wait_ge(s_hi_set, 3)
                dve.tensor_tensor(s_dn[:, :, D:2 * D], raw_sd[:, :, :], s_dn[:, :, 0:D].bitcast(F32), ALU.subtract).then_inc(s_lo_set, 1)
                with dve.Fori(0, act_n, 2) as j:
                    for p in range(2):
                        n = j + p
                        slot_images(n + 2, p)
                        gated(n, 0)
                        gu_low(n + 1, 1 - p, 0)
                        gated(n, 1)
                        gated(n, 2)
                        gu_low(n + 1, 1 - p, 1)
                        gated(n, 3)
                        slots(n + 2)
                        split_x(n + 1)
                        slot_weights(n + 1, 1 - p)
                        weigh(n, p)


def block_c(nc, psum, all_hiA, all_loA, all_B, acc, s_hi, s_lo, s_dn, out):
    with ExitStack() as ctx:
        def sb(name, shape, dt=F32):
            return ctx.enter_context(nc.sbuf_tensor(name, shape, dt))

        def sem(name):
            return ctx.enter_context(nc.semaphore(name))

        gate = [sb(f"s_gate{i}", [F, CHUNK]) for i in range(2)]
        inter = [sb(f"s_inter{i}", [F, CHUNK]) for i in range(2)]
        in_hi = sb("s_in_hi", [F, SM, CHUNK], F32R)
        in_lo = sb("s_in_lo", [F, SM, CHUNK], F32R)
        rows_in = sb("rows_in", [128, CHUNK // 128, D])
        rows_half = sb("rows_half", [128, CHUNK // 128, D])
        rows_out = sb("rows_out", [128, CHUNK // 128, D])

        passed = sem("passed_c")
        g_mm = sem("g_mm")
        u_mm = sem("u_mm")
        gate_ready = sem("s_gate_ready")
        inter_ready = sem("s_inter_ready")
        hi_ready = sem("s_in_hi_ready")
        lo_ready = sem("s_in_lo_ready")
        d_mm = sem("d_mm")
        half_ready = sem("half_ready")
        sum_ready = sem("sum_ready")
        acc_in = sem("acc_in")
        out_done = sem("out_done")
        g_ps = [psum[0], psum[1]]
        u_ps = [psum[2], psum[3]]
        d_ps = psum[4:8]
        TILES = CHUNK // 128

        def first_token(c):
            return NCHUNK * CHUNK if isinstance(c, int) and c == 0 else (c - 1) * CHUNK

        def tiles_before(c):
            return 0 if isinstance(c, int) and c == 0 else c * TILES - (TILES - 1)

        def tiles(width):
            return [(t, min(128, width - 128 * t)) for t in range((width + 127) // 128)]

        with nc.Block() as block:
            @block.sync
            def _(sp):
                def load(c, width):
                    wait_apart(sp, passed, (sum_ready, tiles_before(c)))
                    rows = acc[bass.ds(first_token(c), width), :]
                    if width == CHUNK:
                        sp.dma_start(rows_in[:, :, :], rows.rearrange("(t p) n -> p t n", p=128)).then_inc(acc_in, 16)
                    else:
                        sp.dma_start(rows_in[0:width, 0, :], rows).then_inc(acc_in, 16)

                def store(c, width):
                    wait_apart(sp, passed, (sum_ready, tiles_before(c) + len(tiles(width))))
                    rows = out[bass.ds(first_token(c), width), :]
                    if width == CHUNK:
                        sp.dma_start(rows.rearrange("(t p) n -> p t n", p=128), rows_out[:, :, :]).then_inc(out_done, 16)
                    else:
                        sp.dma_start(rows, rows_out[0:width, 0, :]).then_inc(out_done, 16)

                load(0, TAIL)
                store(0, TAIL)
                with sp.Fori(1, NCHUNK + 1) as c:
                    load(c, CHUNK)
                    store(c, CHUNK)
                sp.wait_ge(out_done, 16 * (NCHUNK + 1))

            @block.scalar
            def _(act):
                def silu(c, m, width):
                    act.wait_ge(g_mm, SM * c + m + 1)
                    if m >= 2:
                        act.wait_ge(inter_ready, SM * c + m - 1)
                    else:
                        wait(act, inter_ready, SM * c)
                    act.activation(gate[m % 2][:, 0:width], g_ps[m % 2][0:F, 0:width], ACT.Silu).then_inc(gate_ready, 1)

                def hi(c, m, width):
                    act.wait_ge(inter_ready, SM * c + m + 1)
                    act.activation(in_hi[:, m, 0:width], inter[m % 2][:, 0:width], ACT.Copy).then_inc(hi_ready, 1)

                def chunk(c, width):
                    silu(c, 0, width)
                    for m in range(1, SM):
                        silu(c, m, width)
                        hi(c, m - 1, width)
                    hi(c, SM - 1, width)

                chunk(0, TAIL)
                with act.Fori(1, NCHUNK + 1) as c:
                    chunk(c, CHUNK)

            @block.vector
            def _(dve):
                def gated(c, m, width):
                    dve.wait_ge(gate_ready, SM * c + m + 1)
                    dve.wait_ge(u_mm, SM * c + m + 1)
                    if m >= 2:
                        dve.wait_ge(lo_ready, SM * c + m - 1)
                    else:
                        wait(dve, lo_ready, SM * c)
                    dve.tensor_tensor(inter[m % 2][:, 0:width], gate[m % 2][:, 0:width], u_ps[m % 2][0:F, 0:width],
                                      ALU.mult).then_inc(inter_ready, 1)

                def lo(c, m, width):
                    dve.wait_ge(hi_ready, SM * c + m + 1)
                    dve.tensor_tensor(in_lo[:, m, 0:width], inter[m % 2][:, 0:width], in_hi[:, m, 0:width].bitcast(F32),
                                      ALU.subtract).then_inc(lo_ready, 1)

                def chunk(c, width):
                    gated(c, 0, width)
                    for m in range(1, SM):
                        gated(c, m, width)
                        lo(c, m - 1, width)
                    lo(c, SM - 1, width)
                    dve.wait_ge(acc_in, 16 * c + 16)
                    wait(dve, out_done, 16 * c)
                    for t, r in tiles(width):
                        dve.wait_ge(d_mm, tiles_before(c) + t + 1)
                        dve.tensor_tensor(rows_half[0:r, t, :], d_ps[t][0:r, 0:D], rows_in[0:r, t, :],
                                          ALU.add).then_inc(half_ready, 1)
                        dve.wait_ge(half_ready, tiles_before(c) + t + 1)
                        dve.tensor_tensor(rows_out[0:r, t, :], d_ps[t][0:r, D:2 * D], rows_half[0:r, t, :],
                                          ALU.add).then_inc(sum_ready, 1)

                chunk(0, TAIL)
                with dve.Fori(1, NCHUNK + 1) as c:
                    chunk(c, CHUNK)

            @block.tensor
            def _(pe):
                def chunk(c, width):
                    data = [big[:, bass.ds(first_token(c), width)] for big in (all_hiA, all_loA, all_B)]
                    for m in range(SM):
                        for half, ps, done in ((0, g_ps, g_mm), (1, u_ps, u_mm)):
                            if m >= 2:
                                pe.wait_ge(inter_ready, SM * c + m - 1)
                            else:
                                wait(pe, inter_ready, SM * c)
                            cols = slice(half * IS + m * F, half * IS + (m + 1) * F)
                            passes = ((data[0], s_hi[:, 0, cols]), (data[0], s_lo[:, 0, cols]), (data[1], s_hi[:, 0, cols]),
                                      (data[2], s_hi[:, 1, cols]), (data[2], s_lo[:, 1, cols]))
                            for i, (x, w) in enumerate(passes):
                                mm = pe.matmul(ps[m % 2][0:F, 0:width], w, x, start=i == 0, stop=i == 4)
                            mm.then_inc(done, 1)
                    for t, r in tiles(width):
                        wait(pe, sum_ready, tiles_before(c))
                        for m in range(SM):
                            if t == 0:
                                pe.wait_ge(hi_ready, SM * c + m + 1)
                                pe.wait_ge(lo_ready, SM * c + m + 1)
                            rows = slice(t * 128, t * 128 + r)
                            pe.matmul(d_ps[t][0:r, 0:2 * D], in_hi[:, m, rows], s_dn[:, m, :], start=m == 0, stop=False)
                            mm = pe.matmul(d_ps[t][0:r, 0:D], in_lo[:, m, rows], s_dn[:, m, 0:D], start=False,
                                           stop=m == SM - 1)
                        mm.then_inc(d_mm, 1)

                chunk(0, TAIL)
                with pe.Fori(1, NCHUNK + 1) as c:
                    chunk(c, CHUNK)


def constants():
    import numpy as np

    i = np.arange(S, dtype=np.float32)
    diff = i[None, :] - i[:, None]
    decay = np.where(diff >= 0, np.float32(0.99) ** np.maximum(diff, 0), 0).astype(np.float32) / np.sqrt(np.float32(D))
    mask = np.zeros((128, SCOLS), np.float32)
    cum = np.zeros((128, 3, SP), np.float32)
    for t in range(3):
        o, r = t * 128, TL[t]
        mask[:r, SOFF[t]:SOFF[t] + S - o] = decay[o:o + r, o:]
        cum[:r, t, 1:] = diff[o:o + r, :] >= 0
    p = np.arange(128, dtype=np.float32)
    return {
        "c_mask": mask,
        "c_cum": cum,
        "c_up": (p[:, None] < p[None, :]).astype(np.float32),
        "c_ident": np.eye(128, dtype=np.float32),
        "c_slot": np.arange(CAP, dtype=np.float32).reshape(2, CH).T,
        "c_iota": np.tile(np.arange(E, dtype=np.float32), (128, 1)),
        "c_ecol": p[:, None].copy(),
        "c_rest": np.tile(ABOVE - np.arange(CAP, dtype=np.float32), (B, 1)),
        "c_rest_col": ABOVE - np.arange(CAP, dtype=np.float32).reshape(2, CH).T,
    }


def kernel(**inputs):
    import numpy as np
    import concourse.bacc as bacc
    from concourse.bass_utils import run_bass_kernel_spmd

    a = {k: np.asarray(v) for k, v in inputs.items()}
    g, ps = 14, 16
    xp = a["x"].reshape(B, 3, g, ps, g, ps).transpose(0, 1, 3, 5, 2, 4).reshape(B, KC, 128, NPATCH).transpose(0, 2, 1, 3)
    arrays = {
        "xp": xp,
        "txt": a["txt"],
        "wtok": a["L0_tok_W"].T.reshape(KC, 128, D).transpose(1, 0, 2),
        "btok": a["L0_tok_b"].reshape(1, D),
        "cls": a["L0_tok_class_token"],
        "pos": a["L0_tok_pos_embed"],
        "wqkv": a["L0_attn_W_qkv"],
        "bqk": a["L0_attn_b_qkv"][:2 * D].reshape(4, 96).T,
        "bv": a["L0_attn_b_qkv"][2 * D:].reshape(1, D),
        "wg": a["L0_ffn_Wg"].T,
        "ebias": a["L0_ffn_e_bias"].reshape(1, E),
        "wgu": a["L0_ffn_W_gate_up"],
        "wdn": a["L0_ffn_W_down"],
        "wsg": a["L0_ffn_Wsg"],
        "wsu": a["L0_ffn_Wsu"],
        "wsd": a["L0_ffn_Wsd"],
        **constants(),
    }
    arrays = {k: np.ascontiguousarray(v) for k, v in arrays.items()}
    nc = bacc.Bacc("TRN2", target_bir_lowering=False, num_devices=1)
    args = [nc.dram_tensor(k, v.shape, F32, kind="ExternalInput").ap() for k, v in arrays.items()]
    out = nc.dram_tensor("result", (T, D), F32, kind="ExternalOutput").ap()
    build(nc, *args, out)
    r = run_bass_kernel_spmd(nc, [arrays], core_ids=[0])
    return r.results[0]["result"].reshape(B, S, D)
```

```python
from contextlib import ExitStack

import concourse.bass as bass
from concourse import mybir

F32 = mybir.dt.float32
F32R = mybir.dt.float32r
BF16 = mybir.dt.bfloat16
I32 = mybir.dt.int32
ALU = mybir.AluOpType
ACT = mybir.ActivationFunctionType

B = 16
NPATCH = 196
DIN = 768
KC = DIN // 128
D = 192
DA = 128
DB = D - DA
TXT = 128
IMG = NPATCH + 1
S = IMG + TXT
SP = S + 1
T = B * S
TL = [128, 128, S - 256]
E = 128
K = 6
I = 464
IS = 928
CAP = 192
CH = CAP // 2
F = 116
EM = I // F
FM = IS // 128
LAST = IS - 128 * FM
SM = FM + 1
UP = IS + LAST
YW = D + E
LIST = E + 8
STEPS = -(-T // 512)
CHUNK = T // STEPS // 8 * 8
FIRST = T - (STEPS - 1) * CHUNK
TILES = 4
SOFF = [0, S, S + (S - 128)]
SCOLS = S + (S - 128) + (S - 256)
EPS = 1e-5
SCALE = 2.5
ABOVE = 200.0
LOW = -3.0e38
ROUTED = -3.3e38


def wait(eng, sem, value):
    if isinstance(value, int) and value <= 0:
        return
    eng.wait_ge(sem, value)


def wait_apart(eng, passed, *waits):
    for sem, v in waits:
        if not isinstance(v, int) or v > 0:
            eng.wait_ge(sem, v)
            eng.sem_inc(passed, 1)


def by_turns(n):
    return bass.ds((n % 2) * 3, 3)


def build(nc, xp, txt, wtok, btok, cls, pos, wqkv, bqk, bv, wg, ebias, wgu, wdn, wsg, wsu, wsd,
          c_mask, c_cum, c_up, c_ident, c_slot, c_iota, c_ecol, c_rest, c_rest_col, out):
    yw = nc.dram_tensor("yw_rows", (T + CAP, YW), F32, kind="Internal").ap()
    acc = nc.dram_tensor("acc_rows", (T + CAP, D), F32, kind="Internal").ap()
    crow = nc.dram_tensor("count_rows", (E, B, SP), BF16, kind="Internal").ap()

    with ExitStack() as top:
        def keep(name, shape, dt=F32):
            return top.enter_context(nc.sbuf_tensor(name, shape, dt))

        psum = [top.enter_context(nc.psum_tensor(f"bank{i}", [128, 512], F32)) for i in range(8)]

        all_hiA = keep("all_hiA", [128, T], F32R)
        all_loA = keep("all_loA", [128, T], F32R)
        all_B = keep("all_B", [128, T], F32R)
        ident = keep("ident", [128, 128])
        ones = keep("ones", [128, 128])
        slot = keep("slot", [CH, 2])
        rest = keep("rest", [CH, 2])
        iota = keep("iota", [128, E])
        ecol = keep("ecol", [128, 1])
        up_strict = keep("up_strict", [128, 128])
        images_full = keep("images_full", [CH, 2, E])
        countT = keep("countT", [E, SP], BF16)

        block_a(nc, psum, all_hiA, all_loA, all_B, ident, ones, slot, rest, iota, ecol, up_strict, images_full, countT,
                yw, acc, crow, xp, txt, wtok, btok, cls, pos, wqkv, bqk, bv, wg, ebias,
                c_mask, c_cum, c_up, c_ident, c_slot, c_iota, c_ecol, c_rest_col)
        s_hi = keep("s_hi", [128, 2, 2 * IS], F32R)
        s_lo = keep("s_lo", [128, 2, 2 * IS], F32R)
        s_dn = keep("s_dn", [128, FM, 2 * D], F32R)
        s_dl = keep("s_dl", [3 * LAST, D], F32R)
        n_active = keep("n_active", [1, 1], I32)
        y_rows = keep("y_rows", [CH, 2, D])
        added = top.enter_context(nc.semaphore("added"))
        block_b(nc, psum, ident, ones, rest, iota, ecol, up_strict, images_full, countT, yw, acc, crow, wgu, wdn,
                wsg, wsu, wsd, s_hi, s_lo, s_dn, s_dl, n_active, y_rows, added, c_rest)
        block_c(nc, psum, all_hiA, all_loA, all_B, acc, s_hi, s_lo, s_dn, s_dl, n_active, added, out)


def block_a(nc, psum, all_hiA, all_loA, all_B, ident, ones, slot, rest, iota, ecol, up_strict, images_full, countT,
            yw, acc, crow, xp, txt, wtok, btok, cls, pos, wqkv, bqk, bv, wg, ebias,
            c_mask, c_cum, c_up, c_ident, c_slot, c_iota, c_ecol, c_rest_col):
    with ExitStack() as ctx:
        def sb(name, shape, dt=F32):
            return ctx.enter_context(nc.sbuf_tensor(name, shape, dt))

        def sem(name):
            return ctx.enter_context(nc.semaphore(name))

        patches = sb("patches", [128, KC, 256])
        w_tok = sb("w_tok", [128, KC, D])
        addend = sb("addend", [128, 2, D])
        pos_sb = sb("pos_sb", [128, 2, D])
        txt2 = sb("txt2", [128, D])
        raw_qkv = sb("raw_qkv", [128, 2, 3 * D])
        qkv_hi = sb("qkv_hi", [128, 2, 3 * D], F32R)
        qkv_lo = sb("qkv_lo", [128, 2, 3 * D], F32R)
        raw_g = sb("raw_g", [128, 2, E])
        g_hi = sb("g_hi", [128, 2, E], F32R)
        g_lo = sb("g_lo", [128, 2, E], F32R)
        b_qk = sb("b_qk", [96, 4])
        b_v = sb("b_v", [128, D])
        e_bias = sb("e_bias", [128, E])
        mask = sb("mask", [128, SCOLS])
        cum32 = sb("cum32", [128, 3, SP])
        cum = sb("cum", [128, 3, SP], BF16)
        ones_b = sb("ones_b", [128, SP], BF16)
        above = sb("above", [128, 1])
        zero = sb("zero", [CH, 2, YW])
        half_neg = sb("half_neg", [128, 3])
        h0 = sb("h0", [128, 6, D])
        h1 = sb("h1", [128, 3, D])
        q_k = sb("q_k", [96, 4, S])
        v_sb = sb("v_sb", [128, 3, D])
        scores = sb("scores", [128, SCOLS])
        sig = sb("sig", [128, 3, E])
        choice = sb("choice", [128, 3, E + 2])
        best = sb("best", [128, 3, 8])
        left = sb("left", [128, 3, E + 2])
        chosen = sb("chosen", [128, 3, E], BF16)
        w_raw = sb("w_raw", [128, 3, E])
        w_sum = sb("w_sum", [128, 3])
        w_sum2 = sb("w_sum2", [128, 3])
        w_inv = sb("w_inv", [128, 3])
        chosen_all = sb("chosen_all", [128, E], BF16)
        y1 = sb("y1", [128, 3, D])
        y2 = sb("y2", [128, 3, D])
        w_rows = sb("w_rows", [128, 3, E])
        norm = []
        for i, y in ((1, y1), (2, y2)):
            norm.append(dict(
                y=y, stats=sb(f"stats{i}", [128, 3, 6]), mv=sb(f"mv{i}", [128, 3, 2]), ve=sb(f"ve{i}", [128, 3]),
                rstd=sb(f"rstd{i}", [128, 3]), hiA=sb(f"y{i}_hiA", [128, SP], F32R),
                loA=sb(f"y{i}_loA", [128, SP], F32R), st=sb(f"y{i}_B", [128, SP], F32R),
                s_stats=sem(f"stats{i}_done"), s_mv=sem(f"mv{i}_ready"), s_ve=sem(f"ve{i}_ready"),
                s_rstd=sem(f"rstd{i}_ready"), s_y=sem(f"y{i}_ready"), s_T=sem(f"y{i}T_in_psum"),
                s_hi=sem(f"y{i}T_hi_ready"), s_lo=sem(f"y{i}T_split"), bankA=psum[5 if i == 1 else 3],
                bankB=psum[6 if i == 1 else 4]))
        n1, n2 = norm
        tok_ps, pv_ps, pv2_ps, lg_ps, ct_ps = psum[0], psum[1], psum[2], psum[3], psum[4]
        qk_ps = [psum[7], psum[5], psum[6], psum[0]]
        sc_ps = [psum[7], psum[5], psum[6]]

        passed = sem("passed_a")
        const_in = sem("const_in")
        w_in = sem("w_in")
        base_in = sem("base_in")
        base_set = sem("base_set")
        set_up = sem("set_up")
        set_up_act = sem("set_up_act")
        pool_set = sem("pool_set")
        lo_set = sem("lo_set")
        x_in = sem("x_in")
        t1_in = sem("t1_in")
        t2_in = sem("t2_in")
        tok_mm = sem("tok_mm")
        h0_ready = sem("h0_ready")
        h0_txt = sem("h0_txt")
        qk_mm = sem("qk_mm")
        v_mm = sem("v_mm")
        qk_ready = sem("qk_ready")
        v_ready = sem("v_ready")
        sc_mm = sem("sc_mm")
        sc_ready = sem("sc_ready")
        pv_mm = sem("pv_mm")
        h1_ready = sem("h1_ready")
        lg_mm = sem("lg_mm")
        sig_ready = sem("sig_ready")
        choice_ready = sem("choice_ready")
        best_ready = sem("best_ready")
        best6_ready = sem("best6_ready")
        left_ready = sem("left_ready")
        chosen_ready = sem("chosen_ready")
        wraw_ready = sem("wraw_ready")
        wsum_ready = sem("wsum_ready")
        winv_ready = sem("winv_ready")
        w_ready = sem("w_ready")
        all_added = sem("all_added")
        ct_mm = sem("ct_mm")
        ce_mm = sem("ce_mm")
        ct_ready = sem("ct_ready")
        full_ready = sem("full_ready")
        h1_out = sem("h1_out")
        big_out = sem("big_out")
        y_out = sem("y_out")
        w_out = sem("w_out")
        ct_out = sem("ct_out")
        pad_out = sem("pad_out")
        N_CONST = 17

        with nc.Block() as block:
            @block.sync
            def _(sp):
                def load(n):
                    wait_apart(sp, passed, (tok_mm, n))
                    sp.dma_start(patches[:, :, 1:IMG], xp[n, :, :, :]).then_inc(x_in, 16)
                    wait_apart(sp, passed, (h0_ready, n))
                    sp.dma_start(addend[IMG - 128:128, 1, :], txt[n, 0:256 - IMG, :]).then_inc(t1_in, 16)
                    wait_apart(sp, passed, (h0_txt, n))
                    sp.dma_start(txt2[0:TL[2], :], txt[n, 256 - IMG:TXT, :]).then_inc(t2_in, 16)

                def store_residual(n):
                    wait_apart(sp, passed, (h1_ready, n + 1))
                    rows = acc[bass.ds(n * S, S), :]
                    sp.dma_start(rows[0:256, :].rearrange("(t p) c -> p t c", p=128), h1[:, 0:2, :]).then_inc(h1_out, 16)
                    sp.dma_start(rows[256:S, :], h1[0:TL[2], 2, :]).then_inc(h1_out, 16)

                def store_rows(buf, n, cols, out_sem):
                    rows = yw[bass.ds(n * S, S), cols]
                    sp.dma_start(rows[0:256, :].rearrange("(t p) c -> p t c", p=128), buf[:, 0:2, :]).then_inc(out_sem, 16)
                    sp.dma_start(rows[256:S, :], buf[0:TL[2], 2, :]).then_inc(out_sem, 16)

                def store_routing(n):
                    wait_apart(sp, passed, (w_ready, n + 1))
                    store_rows(w_rows, n, slice(D, YW), w_out)
                    wait_apart(sp, passed, (ct_ready, n + 1))
                    sp.dma_start(crow[:, bass.ds(n, 1), :].rearrange("e o t -> e (o t)"), countT[:, :]).then_inc(ct_out, 16)

                def store_normed(n):
                    wait_apart(sp, passed, (n2["s_y"], n + 1))
                    store_rows(y2, n, slice(0, D), y_out)
                    wait_apart(sp, passed, (n2["s_lo"], n + 1))
                    for big, own in ((all_hiA, n2["hiA"]), (all_loA, n2["loA"]), (all_B, n2["st"])):
                        sp.dma_start(big[:, bass.ds(n * S, S)].bitcast(F32), own[:, 0:S].bitcast(F32)).then_inc(big_out, 16)

                sp.dma_start(w_tok[:, :, :], wtok).then_inc(w_in, 16)
                sp.wait_ge(pool_set, 1)
                load(0)
                sp.dma_start(pos_sb[:, 0, :], pos[0:128, :]).then_inc(base_in, 16)
                sp.dma_start(pos_sb[0:IMG - 128, 1, :], pos[128:IMG, :]).then_inc(base_in, 16)
                sp.dma_start(addend[0:1, 0, :], cls).then_inc(base_in, 16)
                sp.dma_start(addend[1:128, 0, :], btok.to_broadcast([127, D])).then_inc(base_in, 16)
                sp.dma_start(addend[0:IMG - 128, 1, :], btok.to_broadcast([IMG - 128, D])).then_inc(base_in, 16)
                for half, src in ((0, wqkv[0:DA, :]), (1, wqkv[DA:D, :])):
                    sp.dma_start(raw_qkv[0:DA if half == 0 else DB, half, :], src).then_inc(const_in, 16)
                sp.dma_start(raw_qkv[DB:128, 1, :], wqkv[DA:D, :]).then_inc(const_in, 16)
                for half, src in ((0, wg[0:DA, :]), (1, wg[DA:D, :])):
                    sp.dma_start(raw_g[0:DA if half == 0 else DB, half, :], src).then_inc(const_in, 16)
                sp.dma_start(raw_g[DB:128, 1, :], wg[DA:D, :]).then_inc(const_in, 16)
                sp.dma_start(ident[:, :], c_ident).then_inc(const_in, 16)
                sp.dma_start(b_qk[:, :], bqk).then_inc(const_in, 16)
                sp.dma_start(b_v[:, :], bv.to_broadcast([128, D])).then_inc(const_in, 16)
                sp.dma_start(mask[:, :], c_mask).then_inc(const_in, 16)
                sp.dma_start(e_bias[:, :], ebias.to_broadcast([128, E])).then_inc(const_in, 16)
                sp.dma_start(cum32[:, :, :], c_cum).then_inc(const_in, 16)
                sp.dma_start(up_strict[:, :], c_up).then_inc(const_in, 16)
                sp.dma_start(slot[:, :], c_slot).then_inc(const_in, 16)
                sp.dma_start(rest[:, :], c_rest_col).then_inc(const_in, 16)
                sp.dma_start(iota[:, :], c_iota).then_inc(const_in, 16)
                sp.dma_start(ecol[:, :], c_ecol).then_inc(const_in, 16)
                load(1)
                sp.wait_ge(pool_set, 2)
                sp.dma_start(yw[T:T + CAP, :].rearrange("(h p) c -> p h c", p=CH), zero[:, :, :]).then_inc(pad_out, 16)
                load(2)
                def step(n):
                    store_residual(n)
                    if not isinstance(n, int) or n < B - 3:
                        load(n + 3)
                    if not isinstance(n, int) or n > 0:
                        store_routing(n - 1)
                    store_normed(n)

                step(0)
                with sp.Fori(1, B - 3) as i:
                    step(i)
                for n in range(B - 3, B):
                    step(n)
                store_routing(B - 1)
                sp.wait_ge(h1_out, 32 * B)
                sp.wait_ge(big_out, 48 * B)
                sp.wait_ge(y_out, 32 * B)
                sp.wait_ge(w_out, 32 * B)
                sp.wait_ge(ct_out, 16 * B)
                sp.wait_ge(pad_out, 16)

            def rstd_pool(pool, c, n):
                wait_apart(pool, passed, (c["s_mv"], n + 1))
                pool.tensor_scalar(c["ve"][:, :], c["mv"][:, :, 1], EPS, None, ALU.add).then_inc(c["s_ve"], 1)
                pool.wait_ge(c["s_ve"], n + 1)
                wait(pool, c["s_y"], n)
                pool.tensor_tensor(c["rstd"][:, :], c["ve"][:, :], half_neg[:, :], ALU.pow).then_inc(c["s_rstd"], 1)

            @block.gpsimd
            def _(pool):
                pool.memset(patches[:, :, 0:1], 0.0)
                pool.memset(patches[:, :, IMG:], 0.0).then_inc(pool_set, 1)
                pool.memset(zero[:, :, :], 0.0)
                pool.memset(half_neg[:, :], -0.5)
                pool.memset(above[:, :], ABOVE)
                pool.memset(images_full[:, :, :], 0.0)
                pool.memset(ones_b[:, :], 1.0)
                pool.memset(ones[:, :], 1.0)
                pool.memset(chosen_all[:, :], 0.0)
                pool.memset(choice[:, :, :], LOW)
                pool.memset(w_sum[:, :], 1.0)
                for c in norm:
                    pool.memset(c["mv"][:, :, :], 1.0)
                    for name in ("hiA", "loA", "st"):
                        pool.memset(c[name][:, :].bitcast(F32), 0.0)
                pool.memset(w_inv[:, :], 0.0).then_inc(pool_set, 1)
                pool.wait_ge(pool_set, 2)

                def text_rows(n):
                    wait_apart(pool, passed, (h1_ready, n - 1), (t2_in, 16 * n + 16))
                    pool.tensor_copy(h0[0:TL[2], bass.ds((n % 2) * 3 + 2, 1), :].rearrange("p o c -> p (o c)"),
                                     txt2[0:TL[2], :]).then_inc(h0_txt, 1)

                def count_chosen(n):
                    pool.wait_ge(chosen_ready, n + 1)
                    pool.wait_ge(ce_mm, n + 1)
                    for t in range(3):
                        wait(pool, all_added, 3 * n + t)
                        pool.tensor_tensor(chosen_all[0:TL[t], :], chosen_all[0:TL[t], :], chosen[0:TL[t], t, :],
                                           ALU.add).then_inc(all_added, 1)

                def step(n):
                    rstd_pool(pool, n2, n)
                    if not isinstance(n, int) or n < B - 2:
                        text_rows(n + 2)
                        rstd_pool(pool, n1, n + 2)
                    if not isinstance(n, int) or n > 0:
                        count_chosen(n - 1)

                for n in range(2):
                    text_rows(n)
                    rstd_pool(pool, n1, n)
                step(0)
                step(1)
                with pool.Fori(2, B - 2) as i:
                    step(i)
                step(B - 2)
                step(B - 1)
                count_chosen(B - 1)

            @block.scalar
            def _(act):
                act.wait_ge(const_in, 16 * N_CONST)
                act.activation(qkv_hi[:, :, :], raw_qkv[:, :, :], ACT.Copy).then_inc(set_up_act, 1)
                act.activation(g_hi[:, :, :], raw_g[:, :, :], ACT.Copy).then_inc(set_up_act, 1)
                act.wait_ge(pool_set, 2)

                def split_hi(c, n, used, per):
                    act.wait_ge(c["s_T"], n + 1)
                    wait(act, used, n * per)
                    if c is n2:
                        wait(act, big_out, 48 * n)
                    act.activation(c["hiA"][:, 0:S], c["bankA"][:, 0:S], ACT.Copy)
                    act.activation(c["st"][0:DB, 0:S], c["bankB"][0:DB, 0:S], ACT.Copy).then_inc(c["s_hi"], 1)

                def qk_evac(n):
                    wait(act, sc_mm, 3 * n)
                    for m in range(4):
                        act.wait_ge(qk_mm, 4 * n + m + 1)
                        act.activation(q_k[:, m, :], qk_ps[m][0:96, 0:S], ACT.Identity,
                                       bias=b_qk[:, m:m + 1]).then_inc(qk_ready, 1)

                def sigmoid(n):
                    act.wait_ge(lg_mm, n + 1)
                    wait(act, wraw_ready, 3 * n)
                    act.activation(sig[:, 0:2, :], lg_ps[:, 0:2 * E].rearrange("p (t e) -> p t e", t=2), ACT.Sigmoid)
                    act.activation(sig[0:TL[2], 2, :], lg_ps[0:TL[2], 2 * E:3 * E], ACT.Sigmoid).then_inc(sig_ready, 1)

                def counts(n):
                    act.wait_ge(ct_mm, n + 1)
                    wait(act, ct_out, 16 * n)
                    act.activation(countT[:, :], ct_ps[:, 0:SP], ACT.Relu, bias=above[:, :], scale=-1.0).then_inc(ct_ready, 1)

                def step(n):
                    more = not isinstance(n, int) or n < B - 1
                    behind = not isinstance(n, int) or n > 0
                    if behind:
                        sigmoid(n - 1)
                    if more:
                        split_hi(n1, n + 1, v_mm, 1)
                        qk_evac(n + 1)
                    if behind:
                        counts(n - 1)
                    split_hi(n2, n, lg_mm, 1)

                split_hi(n1, 0, v_mm, 1)
                qk_evac(0)
                step(0)
                step(1)
                with act.Fori(2, B - 2) as i:
                    step(i)
                step(B - 2)
                step(B - 1)
                sigmoid(B - 1)
                counts(B - 1)

            @block.tensor
            def _(pe):
                def split_product(ps, a, w_hi, w_lo, stationary):
                    hiA, loA, st = a
                    passes = ((hiA, w_hi[0]), (hiA, w_lo[0]), (loA, w_hi[0]), (st, w_hi[1]), (st, w_lo[1]))
                    for i, (x, w) in enumerate(passes):
                        mm = pe.matmul(ps, x if stationary else w, w if stationary else x, start=i == 0, stop=i == 4)
                    return mm

                def tokens(n):
                    pe.wait_ge(x_in, 16 * n + 16)
                    wait(pe, qk_ready, 4 * (n - 1))
                    wait(pe, h0_ready, n)
                    for t in range(2):
                        for c in range(KC):
                            mm = pe.matmul(tok_ps[:, t * D:(t + 1) * D], patches[:, c, t * 128:(t + 1) * 128],
                                           w_tok[:, c, :], start=c == 0, stop=c == KC - 1)
                    mm.then_inc(tok_mm, 1)

                def turn(c, n):
                    pe.wait_ge(c["s_y"], n + 1)
                    if c is n1:
                        wait(pe, sc_ready, 3 * n)
                    else:
                        wait(pe, full_ready, n)
                        wait(pe, ct_ready, n)
                    for t in range(3):
                        r, o = TL[t], t * 128
                        pe.transpose(c["bankA"][:, o:o + r], c["y"][0:r, t, 0:DA], ident[0:r, 0:r])
                    for t in range(3):
                        r, o = TL[t], t * 128
                        mm = pe.transpose(c["bankB"][0:DB, o:o + r], c["y"][0:r, t, DA:D], ident[0:r, 0:r])
                    mm.then_inc(c["s_T"], 1)

                def qkv(n):
                    pe.wait_ge(n1["s_lo"], n + 1)
                    wait(pe, sc_ready, 3 * n)
                    data = (n1["hiA"][:, :], n1["loA"][:, :], n1["st"][:, :])
                    for m in range(4):
                        if m == 3:
                            pe.wait_ge(h0_ready, n + 2 if not isinstance(n, int) or n < B - 1 else B)
                        cols = slice(m * 96, (m + 1) * 96)
                        split_product(qk_ps[m][0:96, 0:SP], data, [qkv_hi[:, h, cols] for h in range(2)],
                                      [qkv_lo[:, h, cols] for h in range(2)], False).then_inc(qk_mm, 1)
                    wait(pe, h1_ready, n)
                    for t in range(3):
                        r, o = TL[t], t * 128
                        data = (n1["hiA"][:, o:o + r], n1["loA"][:, o:o + r], n1["st"][:, o:o + r])
                        ps = pv_ps[0:r, t * D:(t + 1) * D] if t < 2 else pv2_ps[0:r, 0:D]
                        mm = split_product(ps, data, [qkv_hi[:, h, 2 * D:] for h in range(2)],
                                           [qkv_lo[:, h, 2 * D:] for h in range(2)], True)
                    mm.then_inc(v_mm, 1)

                def score(n):
                    pe.wait_ge(qk_ready, 4 * n + 4)
                    for t in range(3):
                        r, o = TL[t], t * 128
                        for h in range(2):
                            mm = pe.matmul(sc_ps[t][0:r, 0:S - o], q_k[:, 2 + h, o:o + r], q_k[:, h, o:S],
                                           start=h == 0, stop=h == 1)
                        mm.then_inc(sc_mm, 1)

                def attend(n):
                    pe.wait_ge(sc_ready, 3 * n + 3)
                    pe.wait_ge(v_ready, n + 1)
                    for q in range(3):
                        r = TL[q]
                        ps = pv_ps[0:r, q * D:(q + 1) * D] if q < 2 else pv2_ps[0:r, 0:D]
                        for t in range(q + 1):
                            c = SOFF[t] + (q - t) * 128
                            mm = pe.matmul(ps, scores[0:TL[t], c:c + r], v_sb[0:TL[t], t, :], start=t == 0, stop=t == q)
                    mm.then_inc(pv_mm, 1)

                def logits(n):
                    pe.wait_ge(n2["s_lo"], n + 1)
                    for t in range(3):
                        r, o = TL[t], t * 128
                        data = (n2["hiA"][:, o:o + r], n2["loA"][:, o:o + r], n2["st"][:, o:o + r])
                        mm = split_product(lg_ps[0:r, t * E:(t + 1) * E], data, [g_hi[:, h, :] for h in range(2)],
                                           [g_lo[:, h, :] for h in range(2)], True)
                    mm.then_inc(lg_mm, 1)

                def running_counts(n):
                    pe.wait_ge(chosen_ready, n + 1)
                    wait(pe, all_added, 3 * n)
                    for t in range(3):
                        pe.matmul(ct_ps[:, 0:SP], chosen[0:TL[t], t, :], cum[0:TL[t], t, :], start=t == 0, stop=False)
                    pe.matmul(ct_ps[:, 0:SP], chosen_all[:, :], ones_b[:, :], start=False, stop=True).then_inc(ct_mm, 1)
                    for t in range(3):
                        pe.matmul(lg_ps[:, 0:E], ones_b[0:TL[t], 0:128], chosen[0:TL[t], t, :], start=t == 0, stop=False)
                    pe.matmul(lg_ps[:, 0:E], ones_b[:, 0:128], chosen_all[:, :], start=False, stop=True).then_inc(ce_mm, 1)

                def step(n):
                    more = not isinstance(n, int) or n < B - 1
                    behind = not isinstance(n, int) or n > 0
                    attend(n)
                    if behind:
                        logits(n - 1)
                    if more:
                        turn(n1, n + 1)
                    if not isinstance(n, int) or n < B - 2:
                        tokens(n + 2)
                    if more:
                        qkv(n + 1)
                    if behind:
                        running_counts(n - 1)
                    if more:
                        score(n + 1)
                    turn(n2, n)

                pe.wait_ge(w_in, 16)
                tokens(0)
                pe.wait_ge(const_in, 16 * N_CONST)
                turn(n1, 0)
                tokens(1)
                pe.wait_ge(lo_set, 3)
                qkv(0)
                score(0)
                step(0)
                step(1)
                with pe.Fori(2, B - 2) as i:
                    step(i)
                step(B - 2)
                step(B - 1)
                logits(B - 1)
                running_counts(B - 1)

            @block.vector
            def _(dve):
                dve.wait_ge(base_in, 16 * 5)
                dve.tensor_tensor(addend[:, 0, :], addend[:, 0, :], pos_sb[:, 0, :], ALU.add)
                dve.tensor_tensor(addend[0:IMG - 128, 1, :], addend[0:IMG - 128, 1, :], pos_sb[0:IMG - 128, 1, :],
                                  ALU.add).then_inc(base_set, 1)
                dve.wait_ge(base_set, 1)
                dve.wait_ge(pool_set, 2)

                def stats(c, h, n):
                    for t in range(3):
                        ins = dve.bn_stats(c["stats"][0:TL[t], t, :], h[0:TL[t], t, :])
                    ins.then_inc(c["s_stats"], 1)
                    wait_apart(dve, passed, (c["s_stats"], n + 1))
                    for t in range(3):
                        ins = dve.bn_aggr(c["mv"][0:TL[t], t, :], c["stats"][0:TL[t], t, :])
                    ins.then_inc(c["s_mv"], 1)

                def normed(c, h, n):
                    dve.wait_ge(c["s_rstd"], n + 1)
                    wait(dve, c["s_T"], n)
                    if c is n2:
                        wait(dve, y_out, 32 * n)
                    for t in range(3):
                        r = TL[t]
                        ins = dve.tensor_scalar(c["y"][0:r, t, 0:D], h[0:r, t, :], c["mv"][0:r, t, 0:1],
                                                c["rstd"][0:r, t:t + 1], ALU.subtract, ALU.mult)
                    ins.then_inc(c["s_y"], 1)

                def split_lo(c, n):
                    dve.wait_ge(c["s_hi"], n + 1)
                    dve.tensor_tensor(c["loA"][:, 0:S], c["bankA"][:, 0:S], c["hiA"][:, 0:S].bitcast(F32), ALU.subtract)
                    dve.tensor_tensor(c["st"][DB:128, 0:S], c["bankB"][0:DB, 0:S], c["st"][0:DB, 0:S].bitcast(F32),
                                      ALU.subtract).then_inc(c["s_lo"], 1)

                def token_rows(n):
                    dve.wait_ge(tok_mm, n + 1)
                    dve.wait_ge(t1_in, 16 * n + 16)
                    dve.tensor_tensor(h0[:, bass.ds((n % 2) * 3, 2), :], tok_ps[:, 0:2 * D].rearrange("p (t c) -> p t c", t=2),
                                      addend[:, :, :], ALU.add).then_inc(h0_ready, 1)
                    wait_apart(dve, passed, (h0_ready, n + 1), (h0_txt, n + 1))
                    stats(n1, h0[:, by_turns(n), :], n)

                def residual(n):
                    dve.wait_ge(pv_mm, n + 1)
                    wait(dve, h1_out, 32 * n)
                    dve.tensor_tensor(h1[:, 0:2, :], pv_ps[:, 0:2 * D].rearrange("p (t c) -> p t c", t=2),
                                      h0[:, bass.ds((n % 2) * 3, 2), :], ALU.add)
                    dve.tensor_tensor(h1[0:TL[2], 2, :], pv2_ps[0:TL[2], 0:D],
                                      h0[0:TL[2], bass.ds((n % 2) * 3 + 2, 1), :].rearrange("p o c -> p (o c)"),
                                      ALU.add).then_inc(h1_ready, 1)
                    dve.wait_ge(h1_ready, n + 1)
                    stats(n2, h1, n)

                def values(n):
                    dve.wait_ge(v_mm, n + 1)
                    for t in range(3):
                        r = TL[t]
                        ps = pv_ps[0:r, t * D:(t + 1) * D] if t < 2 else pv2_ps[0:r, 0:D]
                        ins = dve.tensor_tensor(v_sb[0:r, t, :], ps, b_v[0:r, :], ALU.add)
                    ins.then_inc(v_ready, 1)

                def decay(n):
                    for t in range(3):
                        r, w = TL[t], S - t * 128
                        dve.wait_ge(sc_mm, 3 * n + t + 1)
                        dve.tensor_tensor(scores[0:r, SOFF[t]:SOFF[t] + w], sc_ps[t][0:r, 0:w],
                                          mask[0:r, SOFF[t]:SOFF[t] + w], ALU.mult).then_inc(sc_ready, 1)

                def choose(n):
                    dve.wait_ge(sig_ready, n + 1)
                    for t in range(3):
                        r = TL[t]
                        ins = dve.tensor_tensor(choice[0:r, t, 0:E], sig[0:r, t, :], e_bias[0:r, :], ALU.add)
                    ins.then_inc(choice_ready, 1)
                    wait_apart(dve, passed, (choice_ready, n + 1))
                    for t in range(3):
                        r = TL[t]
                        ins = dve.max(best[0:r, t, :], choice[0:r, t, :])
                    ins.then_inc(best_ready, 1)
                    dve.wait_ge(best_ready, n + 1)
                    dve.memset(best[:, :, K:8], LOW).then_inc(best6_ready, 1)
                    wait_apart(dve, passed, (best6_ready, n + 1))
                    for t in range(3):
                        r = TL[t]
                        ins = dve.match_replace(left[0:r, t, :], best[0:r, t, :], choice[0:r, t, :], ROUTED)
                    ins.then_inc(left_ready, 1)
                    dve.wait_ge(left_ready, n + 1)
                    wait(dve, all_added, 3 * n)
                    for t in range(3):
                        r = TL[t]
                        ins = dve.tensor_tensor(chosen[0:r, t, :], left[0:r, t, 0:E], choice[0:r, t, 0:E], ALU.not_equal)
                    ins.then_inc(chosen_ready, 1)

                def weights(n):
                    dve.wait_ge(chosen_ready, n + 1)
                    for t in range(3):
                        r = TL[t]
                        ins = dve.scalar_tensor_tensor(w_raw[0:r, t, :], sig[0:r, t, :], 1.0, chosen[0:r, t, :],
                                                       ALU.mult, ALU.mult, accum_out=w_sum[0:r, t:t + 1])
                        ins.then_inc(wraw_ready, 1)
                    dve.wait_ge(wraw_ready, 3 * n + 3)
                    dve.tensor_scalar(w_sum2[:, :], w_sum[:, :], 1e-20, None, ALU.add).then_inc(wsum_ready, 1)
                    dve.wait_ge(wsum_ready, n + 1)
                    dve.reciprocal(w_inv[:, :], w_sum2[:, :]).then_inc(winv_ready, 1)
                    dve.wait_ge(winv_ready, n + 1)
                    wait(dve, w_out, 32 * n)
                    for t in range(3):
                        r = TL[t]
                        ins = dve.tensor_scalar(w_rows[0:r, t, :], w_raw[0:r, t, :], w_inv[0:r, t:t + 1], SCALE,
                                                ALU.mult, ALU.mult)
                    ins.then_inc(w_ready, 1)

                def count_full(n):
                    dve.wait_ge(ce_mm, n + 1)
                    for h in range(2):
                        ins = dve.scalar_tensor_tensor(images_full[:, h, :], lg_ps[0:CH, 0:E], slot[:, h:h + 1],
                                                       images_full[:, h, :], ALU.is_le, ALU.add)
                    ins.then_inc(full_ready, 1)

                def step(n):
                    ahead = not isinstance(n, int) or n < B - 2
                    more = not isinstance(n, int) or n < B - 1
                    behind = not isinstance(n, int) or n > 0
                    residual(n)
                    if more:
                        split_lo(n1, n + 1)
                    if behind:
                        choose(n - 1)
                    if ahead:
                        token_rows(n + 2)
                    if behind and more:
                        weights(n - 1)
                    normed(n2, h1, n)
                    if behind:
                        count_full(n - 1)
                    if behind and not more:
                        weights(n - 1)
                    if more:
                        values(n + 1)
                        decay(n + 1)
                    if ahead:
                        normed(n1, h0[:, by_turns(n + 2), :], n + 2)
                    split_lo(n2, n)

                token_rows(0)
                normed(n1, h0[:, by_turns(0), :], 0)
                dve.wait_ge(const_in, 16 * N_CONST)
                dve.wait_ge(set_up_act, 2)
                dve.tensor_tensor(qkv_lo[:, :, :], raw_qkv[:, :, :], qkv_hi[:, :, :].bitcast(F32),
                                  ALU.subtract).then_inc(lo_set, 1)
                dve.tensor_tensor(g_lo[:, :, :], raw_g[:, :, :], g_hi[:, :, :].bitcast(F32),
                                  ALU.subtract).then_inc(lo_set, 1)
                dve.tensor_copy(cum[:, :, :], cum32[:, :, :]).then_inc(lo_set, 1)
                split_lo(n1, 0)
                token_rows(1)
                normed(n1, h0[:, by_turns(1), :], 1)
                values(0)
                decay(0)
                step(0)
                step(1)
                with dve.Fori(2, B - 2) as i:
                    step(i)
                step(B - 2)
                step(B - 1)
                choose(B - 1)
                weights(B - 1)
                count_full(B - 1)


def block_b(nc, psum, ident, ones, rest, iota, ecol, up_strict, images_full, countT, yw, acc, crow, wgu, wdn,
            wsg, wsu, wsd, s_hi, s_lo, s_dn, s_dl, n_active, y_rows, added, c_rest):
    with ExitStack() as ctx:
        def sb(name, shape, dt=F32):
            return ctx.enter_context(nc.sbuf_tensor(name, shape, dt))

        def sem(name):
            return ctx.enter_context(nc.semaphore(name))

        active = sb("active", [128, 1])
        rank = sb("rank", [128, 2])
        idle_a = sb("idle_a", [128, 1])
        idle = sb("idle", [128, 1])
        diff = sb("diff", [128, 1])
        place = sb("place", [128, 1])
        pick = sb("pick", [128, E])
        order = sb("order", [1, LIST], I32)
        tok_base = sb("tok_base", [CH, 2, E])
        rest_row = sb("rest_row", [B, CAP])
        counts = [sb(f"counts{p}", [B, SP], BF16) for p in range(2)]
        reach = sb("reach", [B, CAP])
        image = sb("image", [B, CAP], BF16)
        le = sb("le", [CH, 2, S])
        before = sb("before", [CH, 2])
        tok = sb("tok", [CH, 2])
        past = sb("past", [CH, 2])
        slot_no = sb("slot_no", [CH, 2])
        slot_tok = sb("slot_tok", [CH, LIST, 2], I32)
        get_idx = sb("get_idx", [CH, 2], I32)
        put_idx = sb("put_idx", [CH, 2], I32)
        x_rows = [sb(f"x_rows{p}", [CH, 2, YW]) for p in range(2)]
        w_slot = [sb(f"w_slot{p}", [CH, 2]) for p in range(2)]
        x_hiA = sb("x_hiA", [128, CAP], F32R)
        x_loA = sb("x_loA", [128, CAP], F32R)
        x_st = sb("x_st", [128, CAP], F32R)
        raw_gu = [sb(f"raw_gu{p}", [128, 2, 2 * I]) for p in range(2)]
        down_w = [sb(f"down_w{p}", [F, EM, D]) for p in range(2)]
        gu_hi = [sb(f"gu_hi{p}", [128, 2, 2 * I], F32R) for p in range(2)]
        gu_lo = [sb(f"gu_lo{p}", [128, 2, 2 * I], F32R) for p in range(2)]
        gate = sb("gate", [F, EM, CAP])
        inter = sb("inter", [F, EM, CAP])
        raw_s = sb("raw_s", [128, 2 * IS])
        raw_sd = sb("raw_sd", [128, FM, D])
        raw_sl = sb("raw_sl", [3 * LAST, D])
        gu_ps = psum[0:4]
        xT_ps, dn_ps, cnt_ps = psum[4], psum[5], psum[6:8]

        passed = sem("passed_b")
        set_dve = sem("set_dve")
        set_pe = sem("set_pe")
        order_ready = sem("order_ready")
        rest_in = sem("rest_in")
        cr_in = [sem(f"cr_in{p}") for p in range(2)]
        reach_ready = sem("reach_ready")
        image_ready = sem("image_ready")
        cnt_mm = sem("cnt_mm")
        before_ready = sem("before_ready")
        tok_ready = sem("tok_ready")
        past_ready = sem("past_ready")
        idx_ready = sem("idx_ready")
        get_idx_ready = sem("get_idx_ready")
        x_in = [sem(f"x_in{p}") for p in range(2)]
        wslot_ready = sem("wslot_ready")
        xT_mm = sem("xT_mm")
        x_hi = sem("x_hi_ready")
        x_split = sem("x_split")
        raw_in = [sem(f"raw_in{p}") for p in range(2)]
        down_in = [sem(f"down_in{p}") for p in range(2)]
        gu_hi_ready = sem("gu_hi_ready")
        gu_split = sem("gu_split")
        gu_mm = sem("gu_mm")
        gate_ready = sem("gate_ready")
        inter_ready = sem("inter_ready")
        dn_mm = sem("dn_mm")
        y_ready = sem("y_rows_ready")
        put_idx_ready = sem("put_idx_ready")
        zero_rows = sem("zero_rows")
        s_in = sem("s_in")
        s_hi_set = sem("s_hi_set")
        s_lo_set = sem("s_lo_set")

        def load_order(eng, n):
            return eng.value_load(order[0:1, bass.ds(n, 1)], min_val=0, max_val=E - 1)

        def load_active(eng):
            eng.wait_ge(order_ready, 1)
            return eng.value_load(n_active[0:1, 0:1], min_val=K, max_val=E)

        def arrivals(n, p, per):
            return (n - p) * (per // 2) + per

        with nc.Block() as block:
            @block.sync
            def _(sp):
                sp.dma_start(rest_row[:, :], c_rest).then_inc(rest_in, 16)
                columns = ((wsg, slice(0, IS), 0), (wsu, slice(IS - LAST, IS), IS), (wsu, slice(0, IS - LAST), UP))
                for w, part, col in columns:
                    sp.dma_start(raw_s[:, col:col + part.stop - part.start], w[0:DA, part]).then_inc(s_in, 16)
                act_n = load_active(sp)

                def load_counts(n, p, first=False):
                    if not first:
                        wait_apart(sp, passed, (cnt_mm, n - 1))
                    e = load_order(sp, n)
                    sp.dma_start(counts[p][:, :], crow[e, :, :]).then_inc(cr_in[p], 16)

                def load(n, p, first=False):
                    if not first:
                        wait_apart(sp, passed, (gu_split, 2 * n - 2))
                    e = load_order(sp, n)
                    sp.dma_start(raw_gu[p][:, 0, :], wgu[e, 0:DA, :]).then_inc(raw_in[p], 16)
                    sp.dma_start(raw_gu[p][0:DB, 1, :], wgu[e, DA:D, :]).then_inc(raw_in[p], 16)
                    sp.dma_start(raw_gu[p][DB:128, 1, :], wgu[e, DA:D, :]).then_inc(raw_in[p], 16)

                def load_down(n, p, first=False):
                    if not first:
                        wait_apart(sp, passed, (dn_mm, n - 1))
                    e = load_order(sp, n)
                    sp.dma_start(down_w[p][:, :, :], wdn[e, :, :].rearrange("(c p) n -> p c n", p=F)).then_inc(down_in[p], 16)

                load_counts(0, 0, True)
                load_counts(1, 1, True)
                load(0, 0, True)
                load_down(0, 0, True)
                load(1, 1, True)
                load_down(1, 1, True)
                sp.wait_ge(s_hi_set, 1)
                sp.wait_ge(s_lo_set, 1)
                for w, part, col in columns:
                    for r in (0, DB):
                        sp.dma_start(raw_s[r:r + DB, col:col + part.stop - part.start], w[DA:D, part]).then_inc(s_in, 16)
                sp.dma_start(raw_sd[:, :, :], wsd[0:128 * FM, :].rearrange("(c p) n -> p c n", p=128)).then_inc(s_in, 16)
                for i in range(3):
                    sp.dma_start(raw_sl[i * LAST:(i + 1) * LAST, :], wsd[128 * FM:IS, :]).then_inc(s_in, 16)
                load_counts(2, 0)
                with sp.Fori(0, act_n, 2) as j:
                    for p in range(2):
                        load_counts(j + p + 3, 1 - p)
                        load(j + p + 2, p)
                        load_down(j + p + 2, p)
                pairs = (act_n + 1) // 2
                wait_apart(sp, passed, *[(x, pairs * m + a) for x, m, a in (
                    (raw_in[0], 48, 48), (raw_in[1], 48, 48), (down_in[0], 16, 16), (down_in[1], 16, 16),
                    (cr_in[0], 16, 32), (cr_in[1], 16, 16))])

            @block.gpsimd
            def _(pool):
                pool.memset(y_rows[:, :, :], 0.0).then_inc(zero_rows, 1)
                pool.wait_ge(zero_rows, 1)
                pool.dma_start(acc[T:T + CAP, :].rearrange("(h p) c -> p h c", p=CH), y_rows[:, :, :]).then_inc(added, 16)
                act_n = load_active(pool)

                def get_tokens(n, p, first=False):
                    waits = [(idx_ready, n + 1)]
                    if not first:
                        waits += [(x_in[1 - p], arrivals(n - 1, 1 - p, 32)), (xT_mm, n - 1), (wslot_ready, n - 1)]
                    elif n == 1:
                        waits += [(x_in[0], 32)]
                    wait_apart(pool, passed, *waits)
                    pool.tensor_copy(get_idx[:, :], slot_tok[:, bass.ds(n, 1), :].rearrange("p o h -> p (o h)")).then_inc(get_idx_ready, 1)
                    wait_apart(pool, passed, (get_idx_ready, n + 1))
                    for h in range(2):
                        pool.indirect_dma_start(x_rows[p][:, h, :], None, yw[:, :],
                                                bass.IndirectOffsetOnAxis(ap=get_idx[:, h:h + 1], axis=0)).then_inc(x_in[p], 16)

                def add_rows(n):
                    wait_apart(pool, passed, (added, n * 32 + 16))
                    pool.tensor_copy(put_idx[:, :], slot_tok[:, bass.ds(n, 1), :].rearrange("p o h -> p (o h)")).then_inc(put_idx_ready, 1)
                    wait_apart(pool, passed, (put_idx_ready, n + 1), (y_ready, n + 2))
                    for h in range(2):
                        pool.indirect_dma_start(acc[:, :], bass.IndirectOffsetOnAxis(ap=put_idx[:, h:h + 1], axis=0),
                                                y_rows[:, h, :], None, compute_op=ALU.add).then_inc(added, 16)

                get_tokens(0, 0, True)
                get_tokens(1, 1, True)
                with pool.Fori(0, act_n, 2) as j:
                    for p in range(2):
                        get_tokens(j + p + 2, p)
                        add_rows(j + p)
                pairs = (act_n + 1) // 2
                wait_apart(pool, passed, (x_in[0], pairs * 32 + 32), (x_in[1], pairs * 32 + 32))

            @block.scalar
            def _(act):
                act.wait_ge(s_in, 16 * 3)
                act.activation(s_hi[:, 0, :], raw_s[:, :], ACT.Copy).then_inc(s_hi_set, 1)
                act_n = load_active(act)

                def gu_part(n, p, h):
                    if h == 0:
                        act.wait_ge(raw_in[p], arrivals(n, p, 48))
                    act.activation(gu_hi[p][:, h, :], raw_gu[p][:, h, :], ACT.Copy).then_inc(gu_hi_ready, 1)

                def split_x(n):
                    act.wait_ge(xT_mm, n + 1)
                    act.activation(x_hiA[:, :], xT_ps[:, 0:CAP], ACT.Copy)
                    act.activation(x_st[0:DB, :], xT_ps[0:DB, CAP:2 * CAP], ACT.Copy).then_inc(x_hi, 1)

                def silu(n, m):
                    act.wait_ge(gu_mm, 4 * n + m + 1)
                    act.activation(gate[:, m, :], gu_ps[m][0:F, 0:CAP], ACT.Silu).then_inc(gate_ready, 1)

                gu_part(0, 0, 0)
                gu_part(0, 0, 1)
                split_x(0)
                with act.Fori(0, act_n, 2) as j:
                    for p in range(2):
                        n = j + p
                        gu_part(n + 1, 1 - p, 0)
                        silu(n, 0)
                        silu(n, 1)
                        gu_part(n + 1, 1 - p, 1)
                        silu(n, 2)
                        silu(n, 3)
                        split_x(n + 1)
                act.wait_ge(s_in, 16 * 13)
                act.activation(s_hi[:, 1, :], raw_s[:, :], ACT.Copy).then_inc(s_hi_set, 1)
                act.activation(s_dn[:, :, 0:D], raw_sd[:, :, :], ACT.Copy)
                act.activation(s_dl[:, :], raw_sl[:, :], ACT.Copy).then_inc(s_hi_set, 1)

            @block.tensor
            def _(pe):
                pe.wait_ge(set_dve, 1)
                pe.matmul(cnt_ps[0][:, 0:1], up_strict[:, :], active[:, :], start=True, stop=True)
                pe.matmul(cnt_ps[0][:, 1:2], ones[:, :], active[:, :], start=True, stop=True).then_inc(set_pe, 1)
                pe.wait_ge(set_dve, 7)
                pe.matmul(xT_ps[0:1, 0:E], ecol[:, :], pick[:, :], start=True, stop=True).then_inc(set_pe, 1)
                act_n = load_active(pe)

                def slot_rows(n, p):
                    pe.wait_ge(image_ready, n + 1)
                    for h in range(2):
                        mm = pe.matmul(cnt_ps[h][0:CH, 0:SP], image[:, h * CH:(h + 1) * CH], counts[p][:, :],
                                       start=True, stop=True)
                    mm.then_inc(cnt_mm, 1)

                def turn(n, p):
                    pe.wait_ge(x_in[p], arrivals(n, p, 32))
                    for h in range(2):
                        pe.transpose(xT_ps[:, h * CH:(h + 1) * CH], x_rows[p][:, h, 0:DA], ident[0:CH, 0:CH])
                        mm = pe.transpose(xT_ps[0:DB, CAP + h * CH:CAP + (h + 1) * CH], x_rows[p][:, h, DA:D],
                                          ident[0:CH, 0:CH])
                    mm.then_inc(xT_mm, 1)

                def gate_up(n, p):
                    pe.wait_ge(x_split, n + 1)
                    pe.wait_ge(gu_split, 2 * n + 2)
                    for m in range(EM):
                        for half in range(2):
                            cols = slice(half * I + m * F, half * I + (m + 1) * F)
                            ps = gu_ps[m][0:F, half * CAP:(half + 1) * CAP]
                            passes = ((x_hiA, gu_hi[p][:, 0, cols]), (x_hiA, gu_lo[p][:, 0, cols]),
                                      (x_loA, gu_hi[p][:, 0, cols]), (x_st, gu_hi[p][:, 1, cols]),
                                      (x_st, gu_lo[p][:, 1, cols]))
                            for i, (x, w) in enumerate(passes):
                                mm = pe.matmul(ps, w, x[:, :], start=i == 0, stop=i == 4)
                        mm.then_inc(gu_mm, 1)

                def down(n, p):
                    pe.wait_ge(y_ready, n + 1)
                    pe.wait_ge(down_in[p], arrivals(n, p, 16))
                    for h in range(2):
                        rows = slice(h * CH, (h + 1) * CH)
                        for m in range(EM):
                            if h == 0:
                                pe.wait_ge(inter_ready, 4 * n + m + 1)
                            mm = pe.matmul(dn_ps[0:CH, h * D:(h + 1) * D], inter[:, m, rows], down_w[p][:, m, :],
                                           start=m == 0, stop=m == EM - 1)
                    mm.then_inc(dn_mm, 1)

                slot_rows(0, 0)
                slot_rows(1, 1)
                turn(0, 0)
                with pe.Fori(0, act_n, 2) as j:
                    for p in range(2):
                        n = j + p
                        gate_up(n, p)
                        slot_rows(n + 2, p)
                        turn(n + 1, 1 - p)
                        down(n, p)

            @block.vector
            def _(dve):
                steps = [0]

                def then(ins):
                    steps[0] += 1
                    ins.then_inc(set_dve, 1)
                    dve.wait_ge(set_dve, steps[0])

                then(dve.tensor_scalar(active[:, :], countT[:, SP - 1:SP], ABOVE, None, ALU.is_lt))
                dve.wait_ge(set_pe, 1)
                then(dve.tensor_copy(rank[:, :], cnt_ps[0][:, 0:2]))
                then(dve.tensor_tensor(idle_a[:, :], rank[:, 1:2], ecol[:, :], ALU.add))
                then(dve.tensor_tensor(idle[:, :], idle_a[:, :], rank[:, 0:1], ALU.subtract))
                then(dve.tensor_tensor(diff[:, :], rank[:, 0:1], idle[:, :], ALU.subtract))
                then(dve.scalar_tensor_tensor(place[:, :], diff[:, :], active[:, 0:1], idle[:, :], ALU.mult, ALU.add))
                then(dve.tensor_scalar(pick[:, :], iota[:, :], place[:, 0:1], None, ALU.is_equal))
                dve.tensor_scalar(tok_base[:, :, :], images_full[:, :, :], float(S), None, ALU.mult)
                dve.tensor_scalar(slot_no[:, :], rest[:, :], -1.0, ABOVE, ALU.mult, ALU.add)
                then(dve.memset(order[:, :], 0))
                dve.tensor_copy(n_active[:, :], rank[0:1, 1:2])
                dve.wait_ge(set_pe, 2)
                dve.tensor_copy(order[:, 0:E], xT_ps[0:1, 0:E]).then_inc(order_ready, 1)
                act_n = load_active(dve)

                def slot_images(n, p):
                    dve.wait_ge(cr_in[p], arrivals(n, p, 16))
                    dve.tensor_scalar(reach[:, :], rest_row[:, :], counts[p][:, 0:1], None, ALU.is_le).then_inc(reach_ready, 1)
                    dve.wait_ge(reach_ready, n + 1)
                    dve.scalar_tensor_tensor(image[:, :], rest_row[:, :], counts[p][:, SP - 1:SP], reach[:, :],
                                             ALU.is_gt, ALU.mult).then_inc(image_ready, 1)

                def slots(n):
                    e = load_order(dve, n)
                    wait_apart(dve, passed, (cnt_mm, n + 1))
                    for h in range(2):
                        ins = dve.tensor_scalar(le[:, h, :], cnt_ps[h][0:CH, 1:SP], rest[:, h:h + 1], 0.0, ALU.is_ge, ALU.add,
                                                accum_out=before[:, h:h + 1])
                    ins.then_inc(before_ready, 1)
                    dve.wait_ge(before_ready, n + 1)
                    dve.tensor_tensor(tok[:, :], before[:, :], tok_base[:, :, bass.ds(e, 1)].rearrange("p h o -> p (h o)"),
                                      ALU.add).then_inc(tok_ready, 1)
                    dve.wait_ge(tok_ready, n + 1)
                    dve.scalar_tensor_tensor(past[:, :], tok[:, :], float(T), slot_no[:, :], ALU.is_ge,
                                             ALU.mult).then_inc(past_ready, 1)
                    dve.wait_ge(past_ready, n + 1)
                    dve.tensor_tensor(slot_tok[:, bass.ds(n, 1), :].rearrange("p o h -> p (o h)"), tok[:, :], past[:, :],
                                      ALU.add).then_inc(idx_ready, 1)

                def slot_weights(n, p):
                    e = load_order(dve, n)
                    wait_apart(dve, passed, (x_in[p], arrivals(n, p, 32)))
                    dve.tensor_copy(w_slot[p][:, :], x_rows[p][:, :, bass.ds(e + D, 1)].rearrange("p h o -> p (h o)")).then_inc(wslot_ready, 1)

                def split_x(n):
                    dve.wait_ge(x_hi, n + 1)
                    dve.tensor_tensor(x_loA[:, :], xT_ps[:, 0:CAP], x_hiA[:, :].bitcast(F32), ALU.subtract)
                    dve.tensor_tensor(x_st[DB:128, :], xT_ps[0:DB, CAP:2 * CAP], x_st[0:DB, :].bitcast(F32),
                                      ALU.subtract).then_inc(x_split, 1)

                def gu_low(n, p, h):
                    dve.wait_ge(gu_hi_ready, 2 * n + h + 1)
                    dve.tensor_tensor(gu_lo[p][:, h, :], raw_gu[p][:, h, :], gu_hi[p][:, h, :].bitcast(F32),
                                      ALU.subtract).then_inc(gu_split, 1)

                def gated(n, m):
                    dve.wait_ge(gate_ready, 4 * n + m + 1)
                    dve.tensor_tensor(inter[:, m, :], gate[:, m, :], gu_ps[m][0:F, CAP:2 * CAP],
                                      ALU.mult).then_inc(inter_ready, 1)

                def weigh(n, p):
                    dve.wait_ge(dn_mm, n + 1)
                    dve.wait_ge(added, 32 * n + 16)
                    dve.wait_ge(wslot_ready, n + 1)
                    for h in range(2):
                        ins = dve.tensor_scalar(y_rows[:, h, :], dn_ps[0:CH, h * D:(h + 1) * D], w_slot[p][:, h:h + 1],
                                                None, ALU.mult)
                    ins.then_inc(y_ready, 1)

                dve.sem_inc(y_ready, 1)
                dve.wait_ge(rest_in, 16)
                slot_images(0, 0)
                slots(0)
                slot_images(1, 1)
                slots(1)
                gu_low(0, 0, 0)
                gu_low(0, 0, 1)
                split_x(0)
                slot_weights(0, 0)
                dve.wait_ge(s_hi_set, 1)
                dve.tensor_tensor(s_lo[:, 0, :], raw_s[:, :], s_hi[:, 0, :].bitcast(F32), ALU.subtract).then_inc(s_lo_set, 1)
                with dve.Fori(0, act_n, 2) as j:
                    for p in range(2):
                        n = j + p
                        slot_images(n + 2, p)
                        gated(n, 0)
                        gu_low(n + 1, 1 - p, 0)
                        gated(n, 1)
                        gated(n, 2)
                        gu_low(n + 1, 1 - p, 1)
                        gated(n, 3)
                        slots(n + 2)
                        split_x(n + 1)
                        slot_weights(n + 1, 1 - p)
                        weigh(n, p)
                dve.wait_ge(s_hi_set, 2)
                dve.tensor_tensor(s_lo[:, 1, :], raw_s[:, :], s_hi[:, 1, :].bitcast(F32), ALU.subtract).then_inc(s_lo_set, 1)
                dve.wait_ge(s_hi_set, 3)
                dve.tensor_tensor(s_dn[:, :, D:2 * D], raw_sd[:, :, :], s_dn[:, :, 0:D].bitcast(F32), ALU.subtract)
                dve.tensor_tensor(s_dl[2 * LAST:, :], raw_sl[2 * LAST:, :], s_dl[2 * LAST:, :].bitcast(F32),
                                  ALU.subtract).then_inc(s_lo_set, 1)


def block_c(nc, psum, all_hiA, all_loA, all_B, acc, s_hi, s_lo, s_dn, s_dl, n_active, added, out):
    with ExitStack() as ctx:
        def sb(name, shape, dt=F32):
            return ctx.enter_context(nc.sbuf_tensor(name, shape, dt))

        def sem(name):
            return ctx.enter_context(nc.semaphore(name))

        gate = [sb(f"s_gate{i}", [128, FIRST]) for i in range(2)]
        inter = [sb(f"s_inter{i}", [128, FIRST]) for i in range(2)]
        in_hi = sb("s_in_hi", [128, FM, FIRST], F32R)
        in_lo = sb("s_in_lo", [128, FM, FIRST], F32R)
        in_last = sb("s_in_last", [3 * LAST, FIRST], F32R)
        rows_in = sb("rows_in", [FIRST // TILES, TILES, D])
        rows_half = sb("rows_half", [FIRST // TILES, TILES, D])
        rows_out = sb("rows_out", [FIRST // TILES, TILES, D])

        passed = sem("passed_c")
        g_mm = sem("g_mm")
        u_mm = sem("u_mm")
        gate_ready = sem("s_gate_ready")
        inter_ready = sem("s_inter_ready")
        hi_ready = sem("s_in_hi_ready")
        lo_ready = sem("s_in_lo_ready")
        d_mm = sem("d_mm")
        half_ready = sem("half_ready")
        sum_ready = sem("sum_ready")
        acc_in = sem("acc_in")
        out_done = sem("out_done")
        g_ps = [psum[0], psum[1]]
        u_ps = [psum[2], psum[3]]
        d_ps = psum[4:8]
        def first_token(c):
            return 0 if isinstance(c, int) and c == 0 else FIRST + (c - 1) * CHUNK

        with nc.Block() as block:
            @block.sync
            def _(sp):
                def load(c, width):
                    wait_apart(sp, passed, (sum_ready, TILES * c))
                    r = width // TILES
                    rows = acc[bass.ds(first_token(c), width), :]
                    sp.dma_start(rows_in[0:r, :, :], rows.rearrange("(t p) n -> p t n", p=r)).then_inc(acc_in, 16)

                def store(c, width):
                    wait_apart(sp, passed, (sum_ready, TILES * c + TILES))
                    r = width // TILES
                    rows = out[bass.ds(first_token(c), width), :]
                    sp.dma_start(rows.rearrange("(t p) n -> p t n", p=r), rows_out[0:r, :, :]).then_inc(out_done, 16)

                pairs = (sp.value_load(n_active[0:1, 0:1], min_val=K, max_val=E) + 1) // 2
                wait_apart(sp, passed, (added, pairs * 64 + 16))
                load(0, FIRST)
                store(0, FIRST)
                with sp.Fori(1, STEPS) as c:
                    load(c, CHUNK)
                    store(c, CHUNK)
                sp.wait_ge(out_done, 16 * STEPS)

            @block.scalar
            def _(act):
                def silu(c, m, width):
                    act.wait_ge(g_mm, SM * c + m + 1)
                    if m >= 2:
                        act.wait_ge(inter_ready, SM * c + m - 1)
                    else:
                        wait(act, inter_ready, SM * c)
                    r = 128 if m < FM else LAST
                    act.activation(gate[m % 2][0:r, 0:width], g_ps[m % 2][0:r, 0:width], ACT.Silu).then_inc(gate_ready, 1)

                def hi(c, m, width):
                    act.wait_ge(inter_ready, SM * c + m + 1)
                    if m < FM:
                        act.activation(in_hi[:, m, 0:width], inter[m % 2][:, 0:width], ACT.Copy).then_inc(hi_ready, 1)
                    else:
                        act.activation(in_last[0:LAST, 0:width], inter[m % 2][0:LAST, 0:width], ACT.Copy)
                        act.activation(in_last[2 * LAST:, 0:width], inter[m % 2][0:LAST, 0:width],
                                       ACT.Copy).then_inc(hi_ready, 1)

                def chunk(c, width):
                    silu(c, 0, width)
                    for m in range(1, SM):
                        silu(c, m, width)
                        hi(c, m - 1, width)
                    hi(c, SM - 1, width)

                chunk(0, FIRST)
                with act.Fori(1, STEPS) as c:
                    chunk(c, CHUNK)

            @block.vector
            def _(dve):
                def gated(c, m, width):
                    dve.wait_ge(gate_ready, SM * c + m + 1)
                    if m < FM:
                        dve.wait_ge(u_mm, FM * c + m + 1)
                    if m >= 2:
                        dve.wait_ge(lo_ready, SM * c + m - 1)
                    else:
                        wait(dve, lo_ready, SM * c)
                    r = 128 if m < FM else LAST
                    up = u_ps[m % 2][:, 0:width] if m < FM else g_ps[m % 2][LAST:2 * LAST, 0:width]
                    dve.tensor_tensor(inter[m % 2][0:r, 0:width], gate[m % 2][0:r, 0:width], up,
                                      ALU.mult).then_inc(inter_ready, 1)

                def lo(c, m, width):
                    dve.wait_ge(hi_ready, SM * c + m + 1)
                    r = 128 if m < FM else LAST
                    hi_part = in_hi[:, m, 0:width] if m < FM else in_last[0:LAST, 0:width]
                    lo_part = in_lo[:, m, 0:width] if m < FM else in_last[LAST:2 * LAST, 0:width]
                    dve.tensor_tensor(lo_part, inter[m % 2][0:r, 0:width], hi_part.bitcast(F32),
                                      ALU.subtract).then_inc(lo_ready, 1)

                def chunk(c, width):
                    gated(c, 0, width)
                    for m in range(1, SM):
                        gated(c, m, width)
                        lo(c, m - 1, width)
                    lo(c, SM - 1, width)
                    dve.wait_ge(acc_in, 16 * c + 16)
                    wait(dve, out_done, 16 * c)
                    r = width // TILES
                    for t in range(TILES):
                        dve.wait_ge(d_mm, TILES * c + t + 1)
                        dve.tensor_tensor(rows_half[0:r, t, :], d_ps[t][0:r, 0:D], rows_in[0:r, t, :],
                                          ALU.add).then_inc(half_ready, 1)
                        dve.wait_ge(half_ready, TILES * c + t + 1)
                        dve.tensor_tensor(rows_out[0:r, t, :], d_ps[t][0:r, D:2 * D], rows_half[0:r, t, :],
                                          ALU.add).then_inc(sum_ready, 1)

                chunk(0, FIRST)
                with dve.Fori(1, STEPS) as c:
                    chunk(c, CHUNK)

            @block.tensor
            def _(pe):
                def chunk(c, width):
                    data = [big[:, bass.ds(first_token(c), width)] for big in (all_hiA, all_loA, all_B)]
                    for m in range(SM):
                        if m == FM:
                            wait_apart(pe, passed, (inter_ready, SM * c + m - 1))
                        elif m >= 2:
                            pe.wait_ge(inter_ready, SM * c + m - 1)
                        else:
                            wait(pe, inter_ready, SM * c)
                        if m < FM:
                            products = ((m * 128, 128, g_ps, g_mm), (UP + m * 128, 128, u_ps, u_mm))
                        else:
                            products = ((m * 128, 2 * LAST, g_ps, g_mm),)
                        for col, r, ps, done in products:
                            cols = slice(col, col + r)
                            passes = ((data[0], s_hi[:, 0, cols]), (data[0], s_lo[:, 0, cols]), (data[1], s_hi[:, 0, cols]),
                                      (data[2], s_hi[:, 1, cols]), (data[2], s_lo[:, 1, cols]))
                            for i, (x, w) in enumerate(passes):
                                mm = pe.matmul(ps[m % 2][0:r, 0:width], w, x, start=i == 0, stop=i == 4)
                            mm.then_inc(done, 1)
                    r = width // TILES
                    for t in range(TILES):
                        wait(pe, sum_ready, TILES * c)
                        rows = slice(t * r, (t + 1) * r)
                        for m in range(FM):
                            if t == 0:
                                pe.wait_ge(hi_ready, SM * c + m + 1)
                                pe.wait_ge(lo_ready, SM * c + m + 1)
                            pe.matmul(d_ps[t][0:r, 0:2 * D], in_hi[:, m, rows], s_dn[:, m, :], start=m == 0, stop=False)
                            pe.matmul(d_ps[t][0:r, 0:D], in_lo[:, m, rows], s_dn[:, m, 0:D], start=False, stop=False)
                        if t == 0:
                            pe.wait_ge(hi_ready, SM * c + SM)
                            pe.wait_ge(lo_ready, SM * c + SM)
                        pe.matmul(d_ps[t][0:r, 0:D], in_last[:, rows], s_dl[:, :], start=False, stop=True).then_inc(d_mm, 1)

                chunk(0, FIRST)
                with pe.Fori(1, STEPS) as c:
                    chunk(c, CHUNK)


def constants():
    import numpy as np

    i = np.arange(S, dtype=np.float32)
    diff = i[None, :] - i[:, None]
    decay = np.where(diff >= 0, np.float32(0.99) ** np.maximum(diff, 0), 0).astype(np.float32) / np.sqrt(np.float32(D))
    mask = np.zeros((128, SCOLS), np.float32)
    cum = np.zeros((128, 3, SP), np.float32)
    for t in range(3):
        o, r = t * 128, TL[t]
        mask[:r, SOFF[t]:SOFF[t] + S - o] = decay[o:o + r, o:]
        cum[:r, t, 1:] = diff[o:o + r, :] >= 0
    p = np.arange(128, dtype=np.float32)
    return {
        "c_mask": mask,
        "c_cum": cum,
        "c_up": (p[:, None] < p[None, :]).astype(np.float32),
        "c_ident": np.eye(128, dtype=np.float32),
        "c_slot": np.arange(CAP, dtype=np.float32).reshape(2, CH).T,
        "c_iota": np.tile(np.arange(E, dtype=np.float32), (128, 1)),
        "c_ecol": p[:, None].copy(),
        "c_rest": np.tile(ABOVE - np.arange(CAP, dtype=np.float32), (B, 1)),
        "c_rest_col": ABOVE - np.arange(CAP, dtype=np.float32).reshape(2, CH).T,
    }


def kernel(**inputs):
    import numpy as np
    import concourse.bacc as bacc
    from concourse.bass_utils import run_bass_kernel_spmd

    a = {k: np.asarray(v) for k, v in inputs.items()}
    g, ps = 14, 16
    xp = a["x"].reshape(B, 3, g, ps, g, ps).transpose(0, 1, 3, 5, 2, 4).reshape(B, KC, 128, NPATCH).transpose(0, 2, 1, 3)
    arrays = {
        "xp": xp,
        "txt": a["txt"],
        "wtok": a["L0_tok_W"].T.reshape(KC, 128, D).transpose(1, 0, 2),
        "btok": a["L0_tok_b"].reshape(1, D),
        "cls": a["L0_tok_class_token"],
        "pos": a["L0_tok_pos_embed"],
        "wqkv": a["L0_attn_W_qkv"],
        "bqk": a["L0_attn_b_qkv"][:2 * D].reshape(4, 96).T,
        "bv": a["L0_attn_b_qkv"][2 * D:].reshape(1, D),
        "wg": a["L0_ffn_Wg"].T,
        "ebias": a["L0_ffn_e_bias"].reshape(1, E),
        "wgu": a["L0_ffn_W_gate_up"],
        "wdn": a["L0_ffn_W_down"],
        "wsg": a["L0_ffn_Wsg"],
        "wsu": a["L0_ffn_Wsu"],
        "wsd": a["L0_ffn_Wsd"],
        **constants(),
    }
    arrays = {k: np.ascontiguousarray(v) for k, v in arrays.items()}
    nc = bacc.Bacc("TRN2", target_bir_lowering=False, num_devices=1)
    args = [nc.dram_tensor(k, v.shape, F32, kind="ExternalInput").ap() for k, v in arrays.items()]
    out = nc.dram_tensor("result", (T, D), F32, kind="ExternalOutput").ap()
    build(nc, *args, out)
    r = run_bass_kernel_spmd(nc, [arrays], core_ids=[0])
    return r.results[0]["result"].reshape(B, S, D)
```
